# Optimizing a Trainium2 kernel written in Bass

```python
import numpy as np
import jax
import jax.numpy as jnp

def _softmax(x, axis=-1):
    return jax.nn.softmax(x, axis=axis)

def _gelu(x):
    return jax.nn.gelu(x, approximate=True)

def _silu(x):
    return jax.nn.silu(x)

def _sigmoid(x):
    return jax.nn.sigmoid(x)

def _layernorm(x, axis=-1, eps=1e-05):
    m = jnp.mean(x, axis=axis, keepdims=True)
    v = jnp.var(x, axis=axis, keepdims=True)
    return (x - m) / jnp.sqrt(v + eps)

def _scatter_add(tgt, idx, src, axis=0):
    return tgt.at[idx].add(src)

def _segment_sum(src, seg, n):
    return jax.ops.segment_sum(src, seg, n)
kernel_name = 'mk_vit_tower_d2_tok_img256_r4_e4b103'

def setup_inputs(seed: int=0):
    np.random.seed(seed)
    _w = jnp.asarray

    def _rec_inputs():
        import jax
        import jax.numpy as jnp
        _rk = jax.random.key(seed)
        x = -0.00040386 + 0.999972 * jax.random.normal(jax.random.fold_in(_rk, 1), (4, 3, 224, 224), jnp.float32)
        return x
    x = _rec_inputs()

    def _L0_tok_setup():
        import jax, jax.numpy as jnp
        import numpy as np
        EPS = 1e-05
        P = 8
        DIM = 64
        NUM_TOKENS = 64
        PATCH_DIM = 3 * P * P

        def layernorm(x, g, b):
            mu = jnp.mean(x, axis=-1, keepdims=True)
            var = jnp.mean(jnp.square(x - mu), axis=-1, keepdims=True)
            return (x - mu) * jax.lax.rsqrt(var + EPS) * g + b
        key = jax.random.key(seed)
        ks = jax.random.split(key, 8)
        b, c, h, w = (16, 3, 128, 128)
        x = jax.random.normal(ks[0], (b, c, h, w), dtype=jnp.float32)
        ln1_g = jnp.ones((PATCH_DIM,), jnp.float32)
        ln1_b = jnp.zeros((PATCH_DIM,), jnp.float32)
        W1 = jax.random.normal(ks[1], (PATCH_DIM, DIM), jnp.float32) * 0.02
        b1 = jnp.zeros((DIM,), jnp.float32)
        ln2_g = jnp.ones((DIM,), jnp.float32)
        ln2_b = jnp.zeros((DIM,), jnp.float32)
        Wp1 = jax.random.normal(ks[2], (DIM, DIM), jnp.float32) * 0.02
        bp1 = jnp.zeros((DIM,), jnp.float32)
        lnp_g = jnp.ones((DIM,), jnp.float32)
        lnp_b = jnp.zeros((DIM,), jnp.float32)
        Wp2 = jax.random.normal(ks[3], (DIM, NUM_TOKENS), jnp.float32) * 0.02
        bp2 = jnp.zeros((NUM_TOKENS,), jnp.float32)
        return {'x': x, 'ln1_g': ln1_g, 'ln1_b': ln1_b, 'W1': W1, 'b1': b1, 'ln2_g': ln2_g, 'ln2_b': ln2_b, 'Wp1': Wp1, 'bp1': bp1, 'lnp_g': lnp_g, 'lnp_b': lnp_b, 'Wp2': Wp2, 'bp2': bp2}
    _L0_tok_all = _L0_tok_setup()
    _L0_tok_in = {k: v for k, v in _L0_tok_all.items() if k in ('ln1_g', 'ln1_b', 'W1', 'b1', 'ln2_g', 'ln2_b', 'Wp1', 'bp1', 'lnp_g', 'lnp_b', 'Wp2', 'bp2')}
    del _L0_tok_all

    def _L0_attn_setup():
        import jax, jax.numpy as jnp
        import numpy as np
        GROUPS = 64
        EPS = 1e-05
        DIM = 64
        SEQ = 256
        BATCH = 1

        def _group_norm(y, weight, bias):
            g = y.reshape(y.shape[:-1] + (GROUPS, -1))
            mean = g.mean(axis=-1, keepdims=True)
            var = g.var(axis=-1, keepdims=True)
            g = (g - mean) * jax.lax.rsqrt(var + EPS)
            return g.reshape(y.shape) * weight + bias

        def gate_loop_operator(k, v, q, a):
            kv = (k[..., :, None] * v[..., None, :]).astype(a.dtype)
            aa = a[..., :, None]

            def binop(e_i, e_j):
                a_i, kv_i = e_i
                a_j, kv_j = e_j
                return (a_j * a_i, a_j * kv_i + kv_j)
            _, y = jax.lax.associative_scan(binop, (aa, kv), axis=1)
            y = jnp.real(y).astype(k.dtype)
            return jnp.einsum('bld,blde->ble', q, y)
        key = jax.random.key(seed)
        ks = jax.random.split(key, 7)
        ortho = jax.nn.initializers.orthogonal()
        return {'x': jax.random.normal(ks[0], (BATCH, SEQ, DIM), jnp.float32), 'wq': ortho(ks[1], (DIM, DIM), jnp.float32), 'wk': ortho(ks[2], (DIM, DIM), jnp.float32), 'wv': ortho(ks[3], (DIM, DIM), jnp.float32), 'wa': ortho(ks[4], (DIM, 2 * DIM), jnp.float32), 'wg': ortho(ks[5], (DIM, DIM), jnp.float32), 'wo': ortho(ks[6], (DIM, DIM), jnp.float32), 'gn_weight': jnp.ones((DIM,), jnp.float32), 'gn_bias': jnp.zeros((DIM,), jnp.float32), 'bias': jnp.zeros((DIM,), jnp.float32)}
    _L0_attn_all = _L0_attn_setup()
    _L0_attn_in = {k: v for k, v in _L0_attn_all.items() if k in ('wq', 'wk', 'wv', 'wa', 'wg', 'wo', 'gn_weight', 'gn_bias', 'bias')}
    del _L0_attn_all

    def _L0_ffn_setup():
        import jax, jax.numpy as jnp
        import numpy as np
        B, A = (1024, 8)
        IN, OUT = (64, 64)
        SH1, SH2 = (64, 128)
        EH1, EH2 = (128, 64)
        E, TOPK = (4, 2)

        def _shared_mlp(x, W1, b1, W2, b2, W3, b3):
            h = jax.nn.relu(x @ W1 + b1)
            h = jax.nn.relu(h @ W2 + b2)
            return h @ W3 + b3

        def _experts_mlp(x, eW1, eb1, eW2, eb2, eW3, eb3):
            h = jax.nn.relu(jnp.einsum('baf,efh->ebah', x, eW1) + eb1[:, None, None, :])
            h = jax.nn.relu(jnp.einsum('ebah,ehg->ebag', h, eW2) + eb2[:, None, None, :])
            o = jnp.einsum('ebag,ego->ebao', h, eW3) + eb3[:, None, None, :]
            return jnp.moveaxis(o, 0, -1)
        key = jax.random.key(seed)
        ks = jax.random.split(key, 16)
        s = 0.05
        return {'x': jax.random.normal(ks[0], (B, A, IN), jnp.float32), 'sW1': jax.random.normal(ks[1], (IN, SH1), jnp.float32) * s, 'sb1': jnp.zeros((SH1,), jnp.float32), 'sW2': jax.random.normal(ks[2], (SH1, SH2), jnp.float32) * s, 'sb2': jnp.zeros((SH2,), jnp.float32), 'sW3': jax.random.normal(ks[3], (SH2, OUT), jnp.float32) * s, 'sb3': jnp.zeros((OUT,), jnp.float32), 'eW1': jax.random.normal(ks[4], (E, IN, EH1), jnp.float32) * s, 'eb1': jnp.zeros((E, EH1), jnp.float32), 'eW2': jax.random.normal(ks[5], (E, EH1, EH2), jnp.float32) * s, 'eb2': jnp.zeros((E, EH2), jnp.float32), 'eW3': jax.random.normal(ks[6], (E, EH2, OUT), jnp.float32) * s, 'eb3': jnp.zeros((E, OUT), jnp.float32), 'gW': jax.random.normal(ks[7], (IN, E), jnp.float32) * s, 'gb': jnp.zeros((E,), jnp.float32)}
    _L0_ffn_all = _L0_ffn_setup()
    _L0_ffn_in = {k: v for k, v in _L0_ffn_all.items() if k in ('sW1', 'sb1', 'sW2', 'sb2', 'sW3', 'sb3', 'eW1', 'eb1', 'eW2', 'eb2', 'eW3', 'eb3', 'gW', 'gb')}
    del _L0_ffn_all

    def _L1_attn_setup():
        import jax, jax.numpy as jnp
        import numpy as np
        from math import sqrt
        DIM = 64
        key = jax.random.key(seed)
        k1, k2, k3, k4 = jax.random.split(key, 4)
        B, T, D, H, R = (2, 1024, DIM, 8, 32)

        def xavier(k, shape, fan_in, fan_out):
            a = sqrt(6.0 / (fan_in + fan_out))
            return jax.random.uniform(k, shape, jnp.float32, -a, a)
        x = jax.random.normal(k1, (B, T, D), jnp.float32)
        Q = xavier(k2, (H, R, D), D, R)
        K = xavier(k3, (H, R, D), D, R)
        VO = xavier(k4, (H, D, D), D, D)
        return {'x': x, 'Q': Q, 'K': K, 'VO': VO}
    _L1_attn_all = _L1_attn_setup()
    _L1_attn_in = {k: v for k, v in _L1_attn_all.items() if k in ('Q', 'K', 'VO')}
    del _L1_attn_all

    def _L1_ffn_setup():
        import jax, jax.numpy as jnp
        import numpy as np
        NUM_EXPERTS = 8
        TOP_K = 2
        B, S, D = (8, 2048, 64)

        def _moe(tokens, router_w, w1, b1, w2, b2):
            N = tokens.shape[0]
            E = router_w.shape[0]
            logits = tokens.astype(jnp.float32) @ router_w.astype(jnp.float32).T
            probs = jax.nn.softmax(logits, axis=-1)
            rw, re = jax.lax.top_k(probs, TOP_K)
            if TOP_K > 1:
                rw = rw / jnp.maximum(rw.sum(-1, keepdims=True), 1e-12)
            rw = rw.astype(tokens.dtype)
            combine = jnp.zeros((N, E), tokens.dtype).at[jnp.arange(N)[:, None], re].set(rw)
            out = tokens
            for e in range(E):
                h = jax.nn.gelu(tokens @ w1[e] + b1[e], approximate=False)
                y = h @ w2[e] + b2[e]
                out = out + combine[:, e:e + 1] * y
            return out
        key = jax.random.key(seed)
        ks = jax.random.split(key, 4)
        scale = 1.0 / np.sqrt(D).astype(np.float32)
        return {'input_embeddings': jax.random.normal(ks[0], (B, S, D), jnp.float32), 'router_w': jax.random.normal(ks[1], (NUM_EXPERTS, D), jnp.float32) * scale, 'w1': jax.random.normal(ks[2], (NUM_EXPERTS, D, D), jnp.float32) * scale, 'b1': jnp.zeros((NUM_EXPERTS, D), jnp.float32), 'w2': jax.random.normal(ks[3], (NUM_EXPERTS, D, D), jnp.float32) * scale, 'b2': jnp.zeros((NUM_EXPERTS, D), jnp.float32)}
    _L1_ffn_all = _L1_ffn_setup()
    _L1_ffn_in = {k: v for k, v in _L1_ffn_all.items() if k in ('router_w', 'w1', 'b1', 'w2', 'b2')}
    del _L1_ffn_all
    return {'x': x, 'L0_tok_ln1_g': _L0_tok_in['ln1_g'], 'L0_tok_ln1_b': _L0_tok_in['ln1_b'], 'L0_tok_W1': _L0_tok_in['W1'], 'L0_tok_b1': _L0_tok_in['b1'], 'L0_tok_ln2_g': _L0_tok_in['ln2_g'], 'L0_tok_ln2_b': _L0_tok_in['ln2_b'], 'L0_tok_Wp1': _L0_tok_in['Wp1'], 'L0_tok_bp1': _L0_tok_in['bp1'], 'L0_tok_lnp_g': _L0_tok_in['lnp_g'], 'L0_tok_lnp_b': _L0_tok_in['lnp_b'], 'L0_tok_Wp2': _L0_tok_in['Wp2'], 'L0_tok_bp2': _L0_tok_in['bp2'], 'L0_attn_wq': _L0_attn_in['wq'], 'L0_attn_wk': _L0_attn_in['wk'], 'L0_attn_wv': _L0_attn_in['wv'], 'L0_attn_wa': _L0_attn_in['wa'], 'L0_attn_wg': _L0_attn_in['wg'], 'L0_attn_wo': _L0_attn_in['wo'], 'L0_attn_gn_weight': _L0_attn_in['gn_weight'], 'L0_attn_gn_bias': _L0_attn_in['gn_bias'], 'L0_attn_bias': _L0_attn_in['bias'], 'L0_ffn_sW1': _L0_ffn_in['sW1'], 'L0_ffn_sb1': _L0_ffn_in['sb1'], 'L0_ffn_sW2': _L0_ffn_in['sW2'], 'L0_ffn_sb2': _L0_ffn_in['sb2'], 'L0_ffn_sW3': _L0_ffn_in['sW3'], 'L0_ffn_sb3': _L0_ffn_in['sb3'], 'L0_ffn_eW1': _L0_ffn_in['eW1'], 'L0_ffn_eb1': _L0_ffn_in['eb1'], 'L0_ffn_eW2': _L0_ffn_in['eW2'], 'L0_ffn_eb2': _L0_ffn_in['eb2'], 'L0_ffn_eW3': _L0_ffn_in['eW3'], 'L0_ffn_eb3': _L0_ffn_in['eb3'], 'L0_ffn_gW': _L0_ffn_in['gW'], 'L0_ffn_gb': _L0_ffn_in['gb'], 'L1_attn_Q': _L1_attn_in['Q'], 'L1_attn_K': _L1_attn_in['K'], 'L1_attn_VO': _L1_attn_in['VO'], 'L1_ffn_router_w': _L1_ffn_in['router_w'], 'L1_ffn_w1': _L1_ffn_in['w1'], 'L1_ffn_b1': _L1_ffn_in['b1'], 'L1_ffn_w2': _L1_ffn_in['w2'], 'L1_ffn_b2': _L1_ffn_in['b2']}

def reference(x, L0_tok_ln1_g, L0_tok_ln1_b, L0_tok_W1, L0_tok_b1, L0_tok_ln2_g, L0_tok_ln2_b, L0_tok_Wp1, L0_tok_bp1, L0_tok_lnp_g, L0_tok_lnp_b, L0_tok_Wp2, L0_tok_bp2, L0_attn_wq, L0_attn_wk, L0_attn_wv, L0_attn_wa, L0_attn_wg, L0_attn_wo, L0_attn_gn_weight, L0_attn_gn_bias, L0_attn_bias, L0_ffn_sW1, L0_ffn_sb1, L0_ffn_sW2, L0_ffn_sb2, L0_ffn_sW3, L0_ffn_sb3, L0_ffn_eW1, L0_ffn_eb1, L0_ffn_eW2, L0_ffn_eb2, L0_ffn_eW3, L0_ffn_eb3, L0_ffn_gW, L0_ffn_gb, L1_attn_Q, L1_attn_K, L1_attn_VO, L1_ffn_router_w, L1_ffn_w1, L1_ffn_b1, L1_ffn_w2, L1_ffn_b2):
    import jax
    import jax.numpy as jnp

    def _L0_tok_ref(x, ln1_g, ln1_b, W1, b1, ln2_g, ln2_b, Wp1, bp1, lnp_g, lnp_b, Wp2, bp2):
        import jax, jax.numpy as jnp
        import numpy as np
        EPS = 1e-05
        P = 8
        DIM = 64
        NUM_TOKENS = 64
        PATCH_DIM = 3 * P * P

        def layernorm(x, g, b):
            mu = jnp.mean(x, axis=-1, keepdims=True)
            var = jnp.mean(jnp.square(x - mu), axis=-1, keepdims=True)
            return (x - mu) * jax.lax.rsqrt(var + EPS) * g + b
        b, c, H, W = x.shape
        hp, wp = (H // P, W // P)
        patches = x.reshape(b, c, hp, P, wp, P)
        patches = jnp.transpose(patches, (0, 2, 4, 3, 5, 1))
        patches = patches.reshape(b, hp * wp, P * P * c)
        tokens = layernorm(patches, ln1_g, ln1_b)
        tokens = tokens @ W1 + b1
        tokens = layernorm(tokens, ln2_g, ln2_b)
        q = tokens
        k = tokens
        tokens = jnp.concatenate([q, k, tokens], axis=1)
        h1 = layernorm(tokens @ Wp1 + bp1, lnp_g, lnp_b)
        h1 = jax.nn.silu(h1)
        return h1 @ Wp2 + bp2

    def _L0_attn_ref(x, wq, wk, wv, wa, wg, wo, gn_weight, gn_bias, bias):
        import jax, jax.numpy as jnp
        import numpy as np
        GROUPS = 64
        EPS = 1e-05
        DIM = 64
        SEQ = 256
        BATCH = 1

        def _group_norm(y, weight, bias):
            g = y.reshape(y.shape[:-1] + (GROUPS, -1))
            mean = g.mean(axis=-1, keepdims=True)
            var = g.var(axis=-1, keepdims=True)
            g = (g - mean) * jax.lax.rsqrt(var + EPS)
            return g.reshape(y.shape) * weight + bias

        def gate_loop_operator(k, v, q, a):
            kv = (k[..., :, None] * v[..., None, :]).astype(a.dtype)
            aa = a[..., :, None]

            def binop(e_i, e_j):
                a_i, kv_i = e_i
                a_j, kv_j = e_j
                return (a_j * a_i, a_j * kv_i + kv_j)
            _, y = jax.lax.associative_scan(binop, (aa, kv), axis=1)
            y = jnp.real(y).astype(k.dtype)
            return jnp.einsum('bld,blde->ble', q, y)
        q = x @ wq
        k = x @ wk
        v = x @ wv
        g = x @ wg
        a = (x @ wa).astype(jnp.float32)
        a_real, a_imag = jnp.split(a, 2, axis=-1)
        a_complex = jax.nn.sigmoid(a_real) * jnp.exp(1j * a_imag)
        y = gate_loop_operator(k, v, q, a_complex)
        y = _group_norm(y, gn_weight, gn_bias)
        y = y * jax.nn.silu(g)
        return y @ wo + bias

    def _L0_ffn_ref(x, sW1, sb1, sW2, sb2, sW3, sb3, eW1, eb1, eW2, eb2, eW3, eb3, gW, gb):
        import jax, jax.numpy as jnp
        import numpy as np
        B, A = (1024, 8)
        IN, OUT = (64, 64)
        SH1, SH2 = (64, 128)
        EH1, EH2 = (128, 64)
        E, TOPK = (4, 2)

        def _shared_mlp(x, W1, b1, W2, b2, W3, b3):
            h = jax.nn.relu(x @ W1 + b1)
            h = jax.nn.relu(h @ W2 + b2)
            return h @ W3 + b3

        def _experts_mlp(x, eW1, eb1, eW2, eb2, eW3, eb3):
            h = jax.nn.relu(jnp.einsum('baf,efh->ebah', x, eW1) + eb1[:, None, None, :])
            h = jax.nn.relu(jnp.einsum('ebah,ehg->ebag', h, eW2) + eb2[:, None, None, :])
            o = jnp.einsum('ebag,ego->ebao', h, eW3) + eb3[:, None, None, :]
            return jnp.moveaxis(o, 0, -1)
        all_out = _experts_mlp(x, eW1, eb1, eW2, eb2, eW3, eb3)
        shared = _shared_mlp(x, sW1, sb1, sW2, sb2, sW3, sb3)
        gates = jax.nn.softmax(x @ gW + gb, axis=-1)
        topv, topi = jax.lax.top_k(gates, TOPK)
        topw = jax.nn.softmax(topv, axis=-1)
        sel = jnp.take_along_axis(all_out, topi[:, :, None, :], axis=-1)
        gated = jnp.sum(sel * topw[:, :, None, :], axis=-1)
        return shared + gated

    def _L1_attn_ref(x, Q, K, VO):
        import jax, jax.numpy as jnp
        import numpy as np
        from math import sqrt
        DIM = 64
        d = x.shape[-1]
        q = jnp.einsum('btd,hrd->bhtr', x, Q)
        k = jnp.einsum('bud,hrd->bhur', x, K)
        scores = jnp.einsum('bhtr,bhur->bhtu', q, k) / sqrt(d)
        attn = jax.nn.softmax(scores, axis=-1)
        ctx = jnp.einsum('bhtu,bud->bhtd', attn, x)
        out = jnp.einsum('bhtd,hde->bte', ctx, VO)
        return out

    def _L1_ffn_ref(input_embeddings, router_w, w1, b1, w2, b2):
        import jax, jax.numpy as jnp
        import numpy as np
        NUM_EXPERTS = 8
        TOP_K = 2
        B, S, D = (8, 2048, 64)

        def _moe(tokens, router_w, w1, b1, w2, b2):
            N = tokens.shape[0]
            E = router_w.shape[0]
            logits = tokens.astype(jnp.float32) @ router_w.astype(jnp.float32).T
            probs = jax.nn.softmax(logits, axis=-1)
            rw, re = jax.lax.top_k(probs, TOP_K)
            if TOP_K > 1:
                rw = rw / jnp.maximum(rw.sum(-1, keepdims=True), 1e-12)
            rw = rw.astype(tokens.dtype)
            combine = jnp.zeros((N, E), tokens.dtype).at[jnp.arange(N)[:, None], re].set(rw)
            out = tokens
            for e in range(E):
                h = jax.nn.gelu(tokens @ w1[e] + b1[e], approximate=False)
                y = h @ w2[e] + b2[e]
                out = out + combine[:, e:e + 1] * y
            return out
        b, s, d = input_embeddings.shape
        tokens = input_embeddings.reshape(b * s, d)
        return _moe(tokens, router_w, w1, b1, w2, b2).reshape(b, s, d)
    h = _L0_tok_ref(x, L0_tok_ln1_g, L0_tok_ln1_b, L0_tok_W1, L0_tok_b1, L0_tok_ln2_g, L0_tok_ln2_b, L0_tok_Wp1, L0_tok_bp1, L0_tok_lnp_g, L0_tok_lnp_b, L0_tok_Wp2, L0_tok_bp2)
    h = h + _L0_attn_ref(_layernorm(h, axis=-1), L0_attn_wq, L0_attn_wk, L0_attn_wv, L0_attn_wa, L0_attn_wg, L0_attn_wo, L0_attn_gn_weight, L0_attn_gn_bias, L0_attn_bias)
    h = h + _L0_ffn_ref(_layernorm(h, axis=-1), L0_ffn_sW1, L0_ffn_sb1, L0_ffn_sW2, L0_ffn_sb2, L0_ffn_sW3, L0_ffn_sb3, L0_ffn_eW1, L0_ffn_eb1, L0_ffn_eW2, L0_ffn_eb2, L0_ffn_eW3, L0_ffn_eb3, L0_ffn_gW, L0_ffn_gb)
    h = h + _L1_attn_ref(_layernorm(h, axis=-1), L1_attn_Q, L1_attn_K, L1_attn_VO)
    h = h + _L1_ffn_ref(_layernorm(h, axis=-1), L1_ffn_router_w, L1_ffn_w1, L1_ffn_b1, L1_ffn_w2, L1_ffn_b2)
    return h

_drawn_inputs = setup_inputs


def setup_inputs(seed=0):
    import zlib

    import numpy as np

    out = dict(_drawn_inputs(seed))
    spreads = {'L0_tok_ln1_g': (1.0, 0.574),
     'L0_tok_ln1_b': (0.0, 0.1),
     'L0_tok_b1': (0.0, 0.1),
     'L0_tok_ln2_g': (1.0, 0.2),
     'L0_tok_ln2_b': (0.0, 0.1),
     'L0_tok_bp1': (0.0, 0.1),
     'L0_tok_lnp_g': (1.0, 0.2),
     'L0_tok_lnp_b': (0.0, 0.1),
     'L0_tok_bp2': (0.0, 0.1),
     'L0_attn_gn_weight': (1.0, 0.2),
     'L0_attn_gn_bias': (0.0, 0.1),
     'L0_attn_bias': (0.0, 0.1),
     'L0_ffn_sb1': (0.0, 0.1),
     'L0_ffn_sb2': (0.0, 0.1),
     'L0_ffn_sb3': (0.0, 0.1),
     'L0_ffn_eb1': (0.0, 0.1),
     'L0_ffn_eb2': (0.0, 0.1),
     'L0_ffn_eb3': (0.0, 0.1),
     'L0_ffn_gb': (0.0, 0.1),
     'L1_ffn_b1': (0.0, 0.476),
     'L1_ffn_b2': (0.0, 0.337)}
    factors = {}
    for name, (base, spread) in spreads.items():
        noise = np.random.default_rng([zlib.crc32(name.encode()), seed]).standard_normal(out[name].shape)
        drawn = base * np.exp(spread * noise) if base else spread * noise
        out[name] = jnp.asarray(drawn.astype(out[name].dtype))
    for name, factor in factors.items():
        out[name] = (out[name] * factor).astype(out[name].dtype)
    return out
```

```python
from contextlib import ExitStack

import numpy as np

import concourse.bass as bass
from concourse import mybir
from concourse.alu_op_type import AluOpType as ALU

F32 = mybir.dt.float32
F32R = mybir.dt.float32r
ACT = mybir.ActivationFunctionType
AX = mybir.AxisListType

B, C, IMG, PS = 4, 3, 224, 8
NP = IMG // PS
TOK = NP * NP
HALF = TOK // 2
HCOL = NP // 2
D = 64
FEAT = C * PS * PS
KF = FEAT // 2
REP = 3
EPS = 1e-5
T = 112
NT = TOK // T
HEADS, R = 8, 32
HG = 4
NH = B * HEADS
LEAD = 12
E0, E1 = 4, 8
GT = 98
NGT = HALF // GT
HROWS = 98
GROUPS = 7


class Tally:

    def __init__(self, start=0):
        self.n, self.reg = start, 0

    def one(self):
        self.n += 1
        return 1

    def now(self):
        return self.reg + self.n

    def next(self):
        return self.reg + self.n + 1


def repeat(engine, start, stop, per, body):
    before = {t: t.n for t in per}
    with engine.Fori(start, stop) as i:
        for t, k in per.items():
            t.reg = (i - start) * k if start else i * k
        body(i)
        for t, k in per.items():
            assert t.n - before[t] == k, (t.n - before[t], k)
    for t, k in per.items():
        t.n, t.reg = before[t] + k * (stop - start), 0


TABLE_A = [("ident", 128), ("center", 128), ("mean", 128), ("w1", 2 * D), ("wp1", 128), ("wp2", 128),
           ("wg", 128), ("wo", 128), ("sw1", 128), ("ew1", E0 * 2 * 128), ("ew2", E0 * D),
           ("ew3", E0 * 128), ("sw2", 2 * 128), ("sw3", D), ("gw", 2 * E0), ("eb3", 128),
           ("sel0", E0 * 128), ("gb", 2 * E0), ("idx0", E0),
           ("qk", 2 * 2 * 2 * 128), ("vo", HEADS * D), ("fold", D), ("e63", 1),
           ("ln1_g", 2), ("ln1_b", 2), ("b1", 1), ("ln2_g", 1), ("ln2_b", 1), ("bp1", 1),
           ("lnp_g", 1), ("lnp_b", 1), ("bp2", 1), ("gn_w", 1), ("gn_b", 1), ("abias", 1),
           ("sb1", 1), ("eb1", E0), ("sb2", 1), ("eb2", E0), ("sb3", 1)]
TABLE_B = [("ident", 128), ("center", 128), ("mean", 128), ("router", 2 * E1), ("mw1", E1 * 128),
           ("mw2", E1 * 128), ("mb2", 128), ("sel1", E1 * 128), ("idx1", E1), ("mb1", E1)]


def columns(table):
    at, out = 0, {}
    for name, n in table:
        out[name] = (at, at + n)
        at += n
    return out, at


COLS_A, WIDTH_A = columns(TABLE_A)
COLS_B, WIDTH_B = columns(TABLE_B)


def build(nc, x, table_a, table_b, out):
    ctx = ExitStack()
    with ctx:
        def sem(name):
            return ctx.enter_context(nc.semaphore(name))

        def sb(stack, name, shape, dt=F32):
            return stack.enter_context(nc.sbuf_tensor(name, shape, dt))

        wb = sb(ctx, "wb", [128, WIDTH_B])
        H = sb(ctx, "H", [128, B, HALF])
        xhat = sb(ctx, "xhat", [128, B, HALF])
        eps = sb(ctx, "eps", [128, 1])
        VB = sb(ctx, "VB", [128, HEADS, 2 * D + 2])
        XV = sb(ctx, "XV", [T, B, NT, D])

        reg1 = ExitStack()
        X = sb(reg1, "X", [T, C, PS, IMG])
        xn = sb(reg1, "xn", [T, 2, 4, FEAT])
        xT = sb(reg1, "xT", [KF, 2, 2, 4 * T])
        bst = sb(reg1, "bst", [T, 2, 4, 6])
        mv = sb(reg1, "mv", [T, 2, 4, 2])
        sd = sb(reg1, "sd", [T, 2, 4])
        ri = sb(reg1, "ri", [T, 2, 4])
        state = sb(reg1, "state", [128, B, HALF])
        act = sb(reg1, "act", [128, B, HALF])
        h1 = sb(reg1, "h1", [128, E0, 2, HALF])
        h2 = sb(reg1, "h2", [128, E0, HALF])
        s1 = sb(reg1, "s1", [128, HALF])
        s2 = sb(reg1, "s2", [128, 2, HALF])
        sel0r = sb(reg1, "sel0r", [96, E0, 128], F32R)
        woy = sb(reg1, "woy", [128, 128])
        ycol = sb(reg1, "ycol", [128, 1])
        gate0 = Gate(lambda n, shape, dt=F32: sb(reg1, n, shape, dt), E0)
        wT0 = sb(reg1, "wT0", [96, HALF], F32R)
        reg1.close()
        reg1 = ExitStack()
        QKH = sb(reg1, "QKH", [128, 2, B * 2, TOK], F32R)
        QKL = sb(reg1, "QKL", [128, 2, B * 2, TOK], F32R)

        reg2 = ExitStack()
        wa = sb(reg2, "wa", [128, WIDTH_A])
        sq = sb(reg2, "sq", [128, B, HALF])
        rs = sb(reg2, "rs", [128, B, HALF])
        XF = sb(reg2, "XF", [D, B, TOK])
        reg2.close()
        reg2 = ExitStack()
        Qs = sb(reg2, "Qs", [HROWS, 4, TOK], F32R)
        Ks = sb(reg2, "Ks", [HROWS, 4, TOK], F32R)
        XVs = sb(reg2, "XVs", [T, 4, NT * D])
        VBs = sb(reg2, "VBs", [128, 4, 2 * D + 2])
        PT = sb(reg2, "PT", [T, 2, TOK])
        CT = sb(reg2, "CT", [128, 4 * T])
        mx = sb(reg2, "mx", [T, NT])
        mhl = sb(reg2, "mhl", [T, 2 * NT], F32R)
        mT = sb(reg2, "mT", [2 * NT, T], F32R)
        zi = sb(reg2, "zi", [T, NT])
        part = sb(reg2, "part", [T, NT * D])
        OUT = sb(reg2, "OUT", [T, 2 * B, NT * D])
        reg2.close()
        reg1.close()

        reg1 = ExitStack()
        g1 = sb(reg1, "g1", [128, 2, E1, HALF])
        wT1 = sb(reg1, "wT1", [96, 2, HALF], F32R)
        sel1r = sb(reg1, "sel1r", [96, E1, 128], F32R)
        gate1 = Gate(lambda n, shape, dt=F32: sb(reg1, n, shape, dt), E1)
        sqm = sb(reg1, "sqm", [128, B, HALF])
        rsm = sb(reg1, "rsm", [128, B, HALF])
        OT = sb(reg1, "OT", [T, 2, 4, 128])
        reg1.close()

        row_store = [nc.dram_tensor(f"row_store{n}", (2, TOK), F32, kind="Internal").ap() for n in range(4)]
        P = ctx.enter_context(nc.psum_tensor("P", [128, 8, 512], F32))

        def bank(n, w=HALF):
            return P[:, n, 0:w]

        def A(name, rows=128):
            lo, hi = COLS_A[name]
            return wa[0:rows, lo:hi]

        def Bt(name, rows=128):
            lo, hi = COLS_B[name]
            return wb[0:rows, lo:hi]

        def col(name, n=0, rows=128):
            lo = COLS_A[name][0] + n
            return wa[0:rows, lo:lo + 1]

        def square_buf(S):
            return sqm if S == 5 else sq

        def rstd_buf(S):
            return rsm if S == 5 else rs

        TOK2, POOL3, GATE, MOE0, ATT, MOE1 = range(6)

        pixels_in, wa_in, wb_in = sem("pixels_in"), sem("wa_in"), sem("wb_in")
        xf_in = [sem(f"xf_in{b}") for b in range(B)]
        vec_step, act_step = sem("vec_step"), sem("act_step")
        eps_set, woy_ready, sel0_ready, sel1_ready = sem("eps_set"), sem("woy_ready"), sem("sel0_ready"), sem("sel1_ready")
        stats_ready, sd_ready, xn_ready = sem("stats_ready"), sem("sd_ready"), sem("xn_ready")
        turned, xT_ready, patch_full, t0_done = sem("turned"), sem("xT_ready"), sem("patch_full"), sem("t0_done")
        vo_full, vb_ready = sem("vo_full"), sem("vb_ready")
        centred, squared, var_full, rstd_ready, normed = (sem("centred"), sem("squared"), sem("var_full"),
                                                          sem("rstd_ready"), sem("normed"))
        main_full, t1_ready, silu_ready, h0_ready = sem("main_full"), sem("t1_ready"), sem("silu_ready"), sem("h0_ready")
        h_ready = sem("h_ready")
        logits_full, expo_in, expo_out, gates_ready = (sem("logits_full"), sem("expo_in"), sem("expo_out"),
                                                       sem("gates_ready"))
        hid_full, hid_done = sem("hid_full"), sem("hid_done")
        wbc_full, wbc_done, moe_full = sem("wbc_full"), sem("wbc_done"), sem("moe_full")
        qk_full, qk_hi, qk_lo = sem("qk_full"), sem("qk_hi"), sem("qk_lo")
        xv_full, xv_done, slots_set = sem("xv_full"), sem("xv_done"), sem("slots_set")
        slot_in = [sem(f"slot_in{s}") for s in range(4)]
        mrow_in = [sem(f"mrow_in{s}") for s in range(4)]
        rows_out = sem("rows_out")
        max_full, max_done, mhl_ready = sem("max_full"), sem("max_done"), sem("mhl_ready")
        st_full, exp_done, av_done, ctx_done = sem("st_full"), sem("exp_done"), sem("av_done"), sem("ctx_done")
        proj_full, proj_done = sem("proj_full"), sem("proj_done")
        sums, join_full = sem("sums"), sem("join_full")
        out_full, out_copied, stored = sem("out_full"), sem("out_copied"), [sem(f"stored{b}") for b in range(B)]

        block = ctx.enter_context(nc.Block())

        H_AFTER = {GATE: 0, MOE0: B, ATT: 2 * B, MOE1: 3 * B}

        def hid_index():
            index, n = {}, 0
            for b in range(B + 1):
                if b >= 1:
                    for e in range(E0):
                        index["l2", b - 1, e] = n
                        n += 1
                    for h in range(2):
                        index["s2", b - 1, h] = n
                        n += 1
                    index["wT", b - 1] = n
                    n += 1
                if b < B:
                    for e in range(E0):
                        for h in range(2):
                            index["l1", b, e, h] = n
                            n += 1
                    index["s1", b] = n
                    n += 1
            base = n
            for b in range(B + 1):
                if b >= 1:
                    index["wT1", b - 1] = n
                    n += 1
                if b < B:
                    for e in range(E1):
                        index["g1", b, e] = n
                        n += 1
            return index, base

        HID, HID1 = hid_index()

        @block.sync
        def _(sync):
            for b in range(B):
                sync.dma_start(X[NP * b:NP * (b + 1), :, :, :].rearrange("i c p w -> i c (p w)"),
                               x[b].rearrange("c (i p) w -> i c (p w)", p=PS)).then_inc(pixels_in, 16)
            sync.dma_start(wb[:, :], table_b).then_inc(wb_in, 16)
            for b in range(B):
                sync.wait_ge(normed, 4 * ATT + b + 1)
                for h in range(2):
                    sync.dma_start(XF[:, b, h * HALF:(h + 1) * HALF],
                                   xhat[h * D:(h + 1) * D, b, :]).then_inc(xf_in[b], 16)
            sync.wait_ge(slots_set, 1)

            def fill(i, b, group, s):
                rows = slice(s * R, (s + 1) * R)
                for dst, src in ((Qs[0:R, s, :], QKH[rows, 0, i, :]), (Qs[R:2 * R, s, :], QKH[rows, 0, i, :]),
                                 (Qs[2 * R:3 * R, s, :], QKL[rows, 0, i, :]),
                                 (Ks[0:R, s, :], QKH[rows, 1, i, :]), (Ks[R:2 * R, s, :], QKL[rows, 1, i, :]),
                                 (Ks[2 * R:3 * R, s, :], QKH[rows, 1, i, :])):
                    sync.dma_start(dst.bitcast(F32), src.bitcast(F32)).then_inc(slot_in[s], 16)
                sync.dma_start(XVs[:, s, :], XV[:, b, :, :].rearrange("p t d -> p (t d)")).then_inc(slot_in[s], 16)
                sync.dma_start(VBs[:, s, :], VB[:, group * 4 + s, :]).then_inc(slot_in[s], 16)

            def max_rows(i, s):
                sync.wait_ge(max_done, 8 * (4 * i + s) + 8)
                n = 4 * i + s
                sync.dma_start(row_store[s].rearrange("r (t c) -> (r t) c", c=T), mT[:, :].bitcast(F32)).then_inc(rows_out, 16)
                sync.wait_ge(rows_out, 16 * n + 16)
                sync.dma_start(Qs[96:98, s, :].bitcast(F32), row_store[s]).then_inc(mrow_in[s], 16)

            for s in range(4):
                fill(0, 0, 0, s)
            max_rows(0, 0)

            def heads(i, b, group):
                for s in range(4):
                    max_rows(i + (s == 3), (s + 1) % 4)
                    sync.wait_ge(proj_full, 4 * i + s + 1)
                    fill(i + 1, b, group, s)

            def image(b):
                heads(2 * b, b, 1)
                heads(2 * b + 1, b + 1, 0)
            repeat(sync, 0, B - 1, {}, image)
            heads(2 * B - 2, B - 1, 1)
            for s in range(1, 4):
                max_rows(2 * B - 1, s)
            rows = out.rearrange("b (k i j) d -> b k i j d", k=REP, i=NP)
            for b in range(B):
                sync.wait_ge(out_copied, 2 * (b + 1))
                for k in range(REP):
                    for h in range(2):
                        for jj in range(4):
                            nct = 4 if jj < 2 else 3
                            dst = rows[b, k, :, :, :][:, h * HCOL + jj:h * HCOL + min(jj + 4 * (nct - 1) + 1, HCOL):4, :]
                            sync.dma_start(dst, OT[jj * NP:(jj + 1) * NP, b % 2, 0:nct, h * D:(h + 1) * D]).then_inc(stored[b], 16)
            for b in range(B):
                sync.wait_ge(stored[b], 16 * REP * 8)

        @block.scalar
        def _(scalar):
            scalar.dma_start(wa[:, :], table_a).then_inc(wa_in, 16)
            steps = Tally()

            def deviations(g, p):
                scalar.wait_ge(stats_ready, g + 1)
                nc.scalar.activation(sd[:, p, :], mv[:, p, :, 1], ACT.Sqrt, bias=eps[0:T, :]).then_inc(sd_ready, 1)

            def turned_patches(g, p):
                scalar.wait_ge(turned, g + 1)
                for k in range(2):
                    nc.scalar.activation(xT[:, p, k, :], P[0:KF, 2 * p + k, 0:4 * T], ACT.Identity,
                                         bias=col("ln1_b", k, KF), scale=col("ln1_g", k, KF)).then_inc(xT_ready, 1)

            def tokens_out(g, p):
                scalar.wait_ge(patch_full, g + 1)
                nc.scalar.activation(
                    state.rearrange("p b (j i) -> p b j i", i=NP)[:, :, bass.ds(2 * g, 2), :].rearrange("p b j i -> p j b i"),
                    P[:, 4 + p, 0:2 * T].rearrange("p (j b i) -> p j b i", j=2, b=B), ACT.Identity,
                    bias=col("b1")).then_inc(t0_done, 1)

            scalar.wait_ge(eps_set, 1)
            scalar.wait_ge(wa_in, 16)
            deviations(0, 0)
            deviations(1, 1)
            turned_patches(0, 0)

            def cycle(g, p):
                deviations(g + 1, 1 - p)
                turned_patches(g, p)
                tokens_out(g - 1, 1 - p)

            def two(i):
                cycle(2 * i + 1, 1)
                cycle(2 * i + 2, 0)
            repeat(scalar, 0, 2, {}, two)
            cycle(5, 1)
            turned_patches(6, 0)
            tokens_out(5, 1)
            tokens_out(6, 0)

            def norm(S):
                for b in range(B):
                    scalar.wait_ge(centred, 4 * S + b + 1)
                    nc.scalar.activation(square_buf(S)[:, b, :], bank(b), ACT.Square).then_inc(squared, 1)
                for b in range(B):
                    scalar.wait_ge(var_full, 4 * S + b + 1)
                    nc.scalar.activation(rstd_buf(S)[:, b, :], bank(4 + b), ACT.Ln, bias=eps[:, :]).then_inc(act_step, steps.one())
                for b in range(B):
                    scalar.wait_ge(act_step, steps.now() - (B - 1 - b))
                    nc.scalar.activation(rstd_buf(S)[:, b, :], rstd_buf(S)[:, b, :], ACT.Exp, scale=-0.5).then_inc(rstd_ready, 1)

            norm(TOK2)
            for b in range(B):
                scalar.wait_ge(main_full, b + 1)
                nc.scalar.activation(state[:, b, :], bank(b), ACT.Identity, bias=col("bp1")).then_inc(t1_ready, 1)
            norm(POOL3)
            for b in range(B):
                scalar.wait_ge(normed, 4 * POOL3 + b + 1)
                nc.scalar.activation(act[:, b, :], xhat[:, b, :], ACT.Silu, bias=col("lnp_b"), scale=col("lnp_g"))\
                  .then_inc(silu_ready, 1)
            for b in range(B):
                scalar.wait_ge(main_full, B + b + 1)
                nc.scalar.activation(H[:, b, :], bank(b), ACT.Identity, bias=col("bp2")).then_inc(h0_ready, 1)
            norm(GATE)
            for b in range(B):
                scalar.wait_ge(main_full, 2 * B + b + 1)
                nc.scalar.activation(act[:, b, :], bank(b), ACT.Silu).then_inc(silu_ready, 1)
            norm(MOE0)

            def exponents(gate, n):
                src, dst = (gate.dif, gate.ex) if n == 0 else (gate.d21, gate.e21)
                nc.scalar.activation(dst, src, ACT.Exp).then_inc(expo_out, 1)

            def hidden(key, dst, func, bias=None, rows=128, width=HALF):
                k = HID[key]
                scalar.wait_ge(hid_full, k + 1)
                nc.scalar.activation(dst, P[0:rows, k % 4, 0:width], func, **({} if bias is None else dict(bias=bias)))\
                  .then_inc(hid_done, 1)

            for b in range(B + 1):
                if b >= 1:
                    c = b - 1
                    if c >= 1:
                        scalar.wait_ge(moe_full, c)
                    for e in range(E0):
                        hidden(("l2", c, e), h2[:, e, :], ACT.Relu, col("eb2", e))
                    for h in range(2):
                        hidden(("s2", c, h), s2[:, h, :], ACT.Relu, col("sb2"))
                    if c == 0:
                        scalar.wait_ge(expo_in, 2)
                        exponents(gate0, 1)
                    hidden(("wT", c), wT0[:, :], ACT.Copy, rows=96)
                if b < B:
                    for e in range(E0):
                        for h in range(2):
                            hidden(("l1", b, e, h), h1[:, e, h, :], ACT.Relu, col("eb1", e))
                            if b == 0 and e == 0 and h == 0:
                                scalar.wait_ge(expo_in, 1)
                                exponents(gate0, 0)
                    hidden(("s1", b), s1[:, :], ACT.Relu, col("sb1"))

            norm(ATT)
            for b in range(B):
                for k in range(8):
                    qk, group, h = k // 4, k // 2 % 2, k % 2
                    scalar.wait_ge(qk_full, 8 * b + k + 1)
                    nc.scalar.activation(QKH[:, qk, 2 * b + group, h * HALF:(h + 1) * HALF], bank(k % 4), ACT.Copy)\
                      .then_inc(qk_hi, 1)
                scalar.wait_ge(xv_full, b + 1)
                nc.scalar.activation(XV[:, b, :, 0:D - 1], P[0:T, 4 + b, 0:NT * D].rearrange("p (t d) -> p t d", d=D)[:, :, 0:D - 1],
                                     ACT.Copy).then_inc(xv_done, 1)

            scalar.wait_ge(slots_set, 1)

            def exp_tile(k, p, first):
                scalar.wait_ge(st_full, k + 1)
                if not first:
                    scalar.wait_ge(av_done, k - 1)
                nc.scalar.activation(PT[:, p, :].rearrange("p (c n) -> p c n", c=2), P[0:T, 2 + 2 * p:4 + 2 * p, 0:HALF],
                                     ACT.Exp, scale=float(D) ** -0.5).then_inc(exp_done, 1)

            def context_out(n, first):
                scalar.wait_ge(av_done, 7 * n + 7)
                if not first:
                    scalar.wait_ge(proj_full, n)
                nc.scalar.activation(CT[:, 0:3 * T], P[:, 6, 0:3 * T], ACT.Copy).then_inc(ctx_done, 1)
                nc.scalar.activation(CT[0:D, 3 * T:4 * T], P[0:D, 6, 3 * T:4 * T], ACT.Copy).then_inc(ctx_done, 1)

            def four_heads(i, first=False):
                for s in range(4):
                    for u in range(NT):
                        n, step = 4 * i + s, 7 * s + u
                        exp_tile(7 * n + u, step % 2, first and step < 2)
                        if u == 0 and not (first and s == 0):
                            context_out(n - 1, first and s == 1)
            four_heads(0, True)
            repeat(scalar, 1, 8, {}, four_heads)
            context_out(NH - 1, False)

            norm(MOE1)
            scalar.wait_ge(expo_in, 3)
            exponents(gate1, 0)
            for b in range(B + 1):
                if b >= 1:
                    hidden(("wT1", b - 1), wT1[:, (b - 1) % 2, :], ACT.Copy, rows=96)
                if b < B:
                    if b >= 2:
                        scalar.wait_ge(moe_full, B + b - 1)
                    for e in range(E1):
                        hidden(("g1", b, e), g1[:, b % 2, e, :], ACT.Gelu, Bt("mb1")[:, e:e + 1])
            for b in range(B):
                scalar.wait_ge(out_full, b + 1)
                if b >= 2:
                    scalar.wait_ge(stored[b - 2], 16 * REP * 8)
                nc.scalar.activation(OT[:, b % 2, 0:3, :], P[0:T, 4 + b % 2, 0:3 * 128].rearrange("p (c n) -> p c n", c=3),
                                     ACT.Copy).then_inc(out_copied, 1)
                nc.scalar.activation(OT[0:56, b % 2, 3, :], P[0:56, 4 + b % 2, 3 * 128:4 * 128], ACT.Copy).then_inc(out_copied, 1)

        @block.tensor
        def _(pe):
            def mm(dst, lhsT, rhs, start=True, stop=True, **more):
                return nc.tensor.matmul(dst, lhsT, rhs, start=start, stop=stop, **more)

            pe.wait_ge(wa_in, 16)
            for h in range(2):
                last = mm(P[h * D:(h + 1) * D, 7, 0:HEADS * D], A("fold", D), A("vo", D))
            last.then_inc(vo_full, 1)

            def turn(g, p):
                pe.wait_ge(xn_ready, g + 1)
                for q in range(4):
                    for k in range(2):
                        last = nc.tensor.transpose(P[0:KF, 2 * p + k, q * T:(q + 1) * T], xn[:, p, q, k * KF:(k + 1) * KF],
                                                   A("ident", T)[:, 0:T])
                last.then_inc(turned, 1)

            def project(g, p):
                pe.wait_ge(xT_ready, 2 * g + 2)
                w1 = A("w1", KF).rearrange("p (k d) -> p k d", k=2)
                for k in range(2):
                    for h in range(2):
                        last = mm(P[h * D:(h + 1) * D, 4 + p, 0:2 * T], w1[:, k, :], xT[:, p, k, 2 * T * h:2 * T * (h + 1)],
                                  k == 0, k == 1)
                last.then_inc(patch_full, 1)

            turn(0, 0)

            def two(i):
                turn(2 * i + 1, 1)
                project(2 * i, 0)
                turn(2 * i + 2, 0)
                project(2 * i + 1, 1)
            repeat(pe, 0, 3, {}, two)
            project(6, 0)

            def norm(S, src, source, count):
                for b in range(B):
                    pe.wait_ge(source, count(b))
                    mm(bank(b), Bt("center"), src[:, b, :]).then_inc(centred, 1)
                for b in range(B):
                    pe.wait_ge(squared, 4 * S + b + 1)
                    mm(bank(4 + b), Bt("mean"), square_buf(S)[:, b, :]).then_inc(var_full, 1)

            pe.wait_ge(wb_in, 16)
            pe.wait_ge(vb_ready, 1)
            norm(TOK2, state, t0_done, lambda b: GROUPS)
            for b in range(B):
                pe.wait_ge(normed, 4 * TOK2 + b + 1)
                mm(bank(b), A("wp1"), xhat[:, b, :]).then_inc(main_full, 1)
            norm(POOL3, state, t1_ready, lambda b: b + 1)
            for b in range(B):
                pe.wait_ge(silu_ready, b + 1)
                mm(bank(b), A("wp2"), act[:, b, :]).then_inc(main_full, 1)
            norm(GATE, H, h0_ready, lambda b: b + 1)
            for b in range(B):
                pe.wait_ge(normed, 4 * GATE + b + 1)
                mm(bank(b), A("wg"), xhat[:, b, :]).then_inc(main_full, 1)
            pe.wait_ge(woy_ready, 1)
            for b in range(B):
                pe.wait_ge(silu_ready, B + b + 1)
                mm(bank(4 + b), woy[:, :], act[:, b, :]).then_inc(main_full, 1)
            norm(MOE0, H, h_ready, lambda b: b + 1)

            def logits(weights, E, S):
                pe.wait_ge(normed, 4 * S + B)
                for b in range(B):
                    for ct in range(NGT):
                        at = (b * NGT + ct) * 2 * E
                        last = mm(P[0:GT, 4, at:at + 2 * E], xhat[:, b, ct * GT:(ct + 1) * GT], weights)
                last.then_inc(logits_full, 1)

            def bank_of(key, first):
                k = HID[key]
                if k - 4 >= first:
                    pe.wait_ge(hid_done, k - 3)
                return k % 4

            def gate_rows(key, wsp, b, first):
                n = bank_of(key, first)
                for ct in range(NGT):
                    last = nc.tensor.transpose(P[0:96, n, ct * GT:(ct + 1) * GT], wsp[:, b * NGT + ct, :].bitcast(F32),
                                               Bt("ident", GT)[:, 0:GT])
                last.then_inc(hid_full, 1)

            ew1 = A("ew1").rearrange("p (e h n) -> p e h n", e=E0, h=2)
            ew2 = A("ew2").rearrange("p (e n) -> p e n", e=E0)
            ew3 = A("ew3").rearrange("p (e n) -> p e n", e=E0)
            sw2 = A("sw2").rearrange("p (h n) -> p h n", h=2)

            def first_layer(b):
                for e in range(E0):
                    for h in range(2):
                        mm(bank(bank_of(("l1", b, e, h), 0)), ew1[:, e, h, :], xhat[:, b, :]).then_inc(hid_full, 1)
                mm(bank(bank_of(("s1", b), 0)), A("sw1"), xhat[:, b, :]).then_inc(hid_full, 1)

            def broadcast_gate(sel, rows, n):
                if n >= 2:
                    pe.wait_ge(wbc_done, n - 1)
                mm(bank(5 + n % 2), sel, rows).then_inc(wbc_full, 1)

            logits(A("gw"), E0, MOE0)
            first_layer(0)
            for b in range(B):
                for e in range(E0):
                    pe.wait_ge(hid_done, HID["l1", b, e, 1] + 1)
                    n = bank_of(("l2", b, e), 0)
                    for h in range(2):
                        last = mm(P[h * D:(h + 1) * D, n, 0:HALF], ew2[:, e, :], h1[:, e, h, :])
                    last.then_inc(hid_full, 1)
                pe.wait_ge(hid_done, HID["s1", b] + 1)
                for h in range(2):
                    mm(bank(bank_of(("s2", b, h), 0)), sw2[:, h, :], s1[:, :]).then_inc(hid_full, 1)
                if b == 0:
                    pe.wait_ge(gates_ready, 1)
                gate_rows(("wT", b), gate0.wsp, b, 0)
                if b + 1 < B:
                    first_layer(b + 1)
                pe.wait_ge(hid_done, HID["wT", b] + 1)
                if b == 0:
                    pe.wait_ge(sel0_ready, 1)
                for e in range(2):
                    broadcast_gate(sel0r[:, e, :], wT0[:, :], E0 * b + e)
                if b >= 1:
                    pe.wait_ge(h_ready, B + b)
                mm(bank(7), A("eb3", 96), wT0[:, :].bitcast(F32), True, False, skip_group_check=True)
                for h in range(2):
                    mm(P[h * D:(h + 1) * D, 7, 0:HALF], A("sw3"), s2[:, h, :], False, False, skip_group_check=True)
                for e in range(E0):
                    if e + 2 < E0:
                        broadcast_gate(sel0r[:, e + 2, :], wT0[:, :], E0 * b + e + 2)
                    pe.wait_ge(wbc_done, E0 * b + e + 1)
                    last = mm(bank(7), ew3[:, e, :], h2[:, e, :], False, e == E0 - 1, skip_group_check=True)
                last.then_inc(moe_full, 1)

            norm(ATT, H, h_ready, lambda b: B + b + 1)
            qk = A("qk").rearrange("p (q g h n) -> p q g h n", q=2, g=2, h=2)
            for b in range(B):
                pe.wait_ge(normed, 4 * ATT + b + 1)
                for k in range(8):
                    if 8 * b + k >= 4:
                        pe.wait_ge(qk_lo, 8 * b + k - 3)
                    elif b == 0:
                        pe.wait_ge(normed, 4 * ATT + B)
                    mm(bank(k % 4), qk[:, k // 4, k // 2 % 2, k % 2, :], xhat[:, b, :]).then_inc(qk_full, 1)
                pe.wait_ge(xf_in[b], 32)
                for t in range(NT):
                    last = nc.tensor.transpose(P[0:T, 4 + b, t * D:(t + 1) * D], XF[:, b, t * T:(t + 1) * T],
                                               A("ident", D)[:, 0:D])
                last.then_inc(xv_full, 1)

            pe.wait_ge(xv_done, B)
            pe.wait_ge(qk_lo, 8 * B)

            def max_tile(i, s, t, first):
                if t == 0:
                    pe.wait_ge(slot_in[s], 128 * (i + 1))
                if not first:
                    pe.wait_ge(max_done, 8 * (4 * i + s) + t)
                for c in range(2):
                    last = mm(P[0:T, c, 0:HALF], Qs[0:96, s, t * T:(t + 1) * T], Ks[0:96, s, c * HALF:(c + 1) * HALF])
                last.then_inc(max_full, 1)

            def max_turn(i, s):
                pe.wait_ge(mhl_ready, 4 * i + s + 1)
                pe.wait_ge(max_done, 8 * (4 * i + s) + 7)
                nc.tensor.transpose(P[0:2 * NT, 0, 0:T], mhl[:, :].bitcast(F32), Bt("ident", T)[:, 0:T]).then_inc(max_full, 1)

            def score_tile(i, s, u, p, first):
                k = 7 * (4 * i + s) + u
                if u == 0:
                    pe.wait_ge(mrow_in[s], 16 * (i + 1))
                if not first:
                    pe.wait_ge(exp_done, k - 1)
                for c in range(2):
                    last = mm(P[0:T, 2 + 2 * p + c, 0:HALF], Ks[:, s, u * T:(u + 1) * T], Qs[:, s, c * HALF:(c + 1) * HALF])
                last.then_inc(st_full, 1)

            def context_tile(i, s, u, p, first):
                n = 4 * i + s
                if u == 0:
                    if not first:
                        pe.wait_ge(ctx_done, 2 * n)
                pe.wait_ge(exp_done, 7 * n + u + 1)
                tiles = PT[:, p, :].rearrange("p (t c) -> p t c", c=T)
                xv = XVs[:, s, u * D:(u + 1) * D]
                mm(P[0:D, 6, 0:4 * T], xv, tiles[:, 0:7:2, :], u == 0, u == NT - 1)
                mm(P[D:128, 6, 0:3 * T], xv, tiles[:, 1:6:2, :], u == 0, u == NT - 1).then_inc(av_done, 1)

            def head_out(i, s, first):
                n = 4 * i + s
                pe.wait_ge(ctx_done, 2 * n + 2)
                if not first:
                    pe.wait_ge(proj_done, n)
                for k in range(4):
                    w = 2 * D + 2 if k < 3 else D + 1
                    last = mm(P[0:T, 7, k * 130:k * 130 + w], CT[:, k * T:(k + 1) * T], VBs[:, s, 0:w])
                last.then_inc(proj_full, 1)

            def four_heads(i, first=False, final=False):
                for s in range(4):
                    for u in range(NT):
                        step = 7 * s + u
                        score_tile(i, s, u, step % 2, first and step < 2)
                        if not (first and step == 0):
                            before = step - 1
                            context_tile(i if before >= 0 else i - 1, before // 7 % 4, before % 7, before % 2,
                                         first and before < 7)
                        if u == 2:
                            if not (first and s == 0):
                                head_out(i if s else i - 1, (s - 1) % 4, first and s == 1)
                            if not (final and s == 3):
                                max_turn(i + (s == 3), (s + 1) % 4)
                        ahead = step + LEAD
                        if not (final and ahead >= 28):
                            max_tile(i + ahead // 28, ahead // 7 % 4, ahead % 7, False)

            for j in range(LEAD):
                if j == 7:
                    max_turn(0, 0)
                max_tile(0, j // 7, j % 7, j == 0)
            four_heads(0, first=True)
            repeat(pe, 1, 7, {}, four_heads)
            four_heads(7, final=True)
            context_tile(7, 3, 6, 1, False)
            head_out(7, 3, False)

            pe.wait_ge(sums, 3 * 2 * B)
            ident = Bt("ident", T)
            for b in range(B):
                for t in range(NT):
                    lo, hi = t * T, (t + 1) * T
                    pieces = []
                    if lo < HALF:
                        pieces.append((0, lo, min(hi, HALF), 0))
                    if hi > HALF:
                        pieces.append((1, max(lo, HALF) - HALF, hi - HALF, max(lo, HALF) - lo))
                    for h, c0, c1, skip in pieces:
                        for group in range(2):
                            last = mm(P[h * D:(h + 1) * D, b, c0:c1], OUT[:, 2 * b + group, t * D:(t + 1) * D],
                                      ident[:, skip:skip + c1 - c0], group == 0, group == 1)
                last.then_inc(join_full, 1)

            norm(MOE1, H, h_ready, lambda b: 2 * B + b + 1)
            logits(Bt("router"), E1, MOE1)
            mw1 = Bt("mw1").rearrange("p (e n) -> p e n", e=E1)
            mw2 = Bt("mw2").rearrange("p (e n) -> p e n", e=E1)

            def hidden_layer(b):
                for e in range(E1):
                    mm(bank(bank_of(("g1", b, e), HID1)), mw1[:, e, :], xhat[:, b, :]).then_inc(hid_full, 1)

            hidden_layer(0)
            for b in range(B):
                if b == 0:
                    pe.wait_ge(gates_ready, 2)
                    pe.wait_ge(sel1_ready, 1)
                gate_rows(("wT1", b), gate1.wsp, b, HID1)
                if b + 1 < B:
                    hidden_layer(b + 1)
                pe.wait_ge(hid_done, HID["wT1", b] + 1)
                rows = wT1[:, b % 2, :]
                at = B * E0 + E1 * b
                for e in range(2):
                    broadcast_gate(sel1r[:, e, :], rows, at + e)
                if b >= 1:
                    pe.wait_ge(h_ready, 3 * B + b)
                mm(bank(7), Bt("mb2", 96), rows.bitcast(F32), True, False)
                for e in range(E1):
                    if e + 2 < E1:
                        broadcast_gate(sel1r[:, e + 2, :], rows, at + e + 2)
                    pe.wait_ge(wbc_done, at + e + 1)
                    last = mm(bank(7), mw2[:, e, :], g1[:, b % 2, e, :], False, e == E1 - 1)
                last.then_inc(moe_full, 1)
            for b in range(B):
                pe.wait_ge(h_ready, 3 * B + b + 1)
                if b >= 2:
                    pe.wait_ge(out_copied, 2 * (b - 1))
                if b == 0:
                    pe.wait_ge(gates_ready, 2)
                for ct in range(4):
                    w = T if ct < 3 else HALF - 3 * T
                    last = nc.tensor.transpose(P[0:w, 4 + b % 2, ct * 128:(ct + 1) * 128], H[:, b, ct * T:ct * T + w],
                                               Bt("ident"))
                last.then_inc(out_full, 1)

        @block.vector
        def _(vector):
            steps = Tally()

            def own():
                vector.wait_ge(vec_step, steps.now())

            nc.vector.memset(eps[:, :], EPS).then_inc(eps_set, 1)
            nc.vector.memset(VB[:, :, :], 0.0).then_inc(vec_step, steps.one())
            nc.vector.memset(XV[:, :, :, :], 1.0)

            def pixels(g, q):
                return X.rearrange("p c r w -> p (c r) w")[:, :, bass.ds((q // 2 * HCOL + 2 * g + q % 2) * PS, PS)]

            def stats(g, p):
                for q in range(4):
                    nc.vector.bn_stats(bst[:, p, q, :], pixels(g, q)).then_inc(vec_step, steps.one())

            def moments(g, p):
                for q in range(4):
                    last = nc.vector.bn_aggr(mv[:, p, q, :], bst[:, p, q, :])
                last.then_inc(stats_ready, 1)

            def apply(g, p):
                vector.wait_ge(sd_ready, g + 1)
                nc.vector.reciprocal(ri[:, p, :], sd[:, p, :]).then_inc(vec_step, steps.one())
                own()
                for q in range(4):
                    last = nc.vector.tensor_scalar(xn[:, p, q, :].rearrange("p (r w) -> p r w", w=PS), pixels(g, q),
                                                   mv[:, p, q, 0:1], ri[:, p, q:q + 1], ALU.subtract, ALU.mult)
                last.then_inc(xn_ready, 1)

            vector.wait_ge(pixels_in, 16 * B)
            stats(0, 0)
            own()
            moments(0, 0)
            stats(1, 1)
            apply(0, 0)
            moments(1, 1)

            def cycle(g, p):
                stats(g + 1, 1 - p)
                apply(g, p)
                moments(g + 1, 1 - p)

            def two(i):
                cycle(2 * i + 1, 1)
                cycle(2 * i + 2, 0)
            repeat(vector, 0, 2, {steps: 10}, two)
            cycle(5, 1)
            apply(6, 0)

            vector.wait_ge(vo_full, 1)
            for h in range(2):
                part_ = slice(h * D, (h + 1) * D)
                at = h * (D + 1)
                nc.vector.tensor_copy(VB[part_, :, at:at + D], P[part_, 7, 0:HEADS * D].rearrange("p (e d) -> p e d", d=D))
                last = nc.vector.tensor_copy(VB[part_, :, at + D], wa[part_, COLS_A["e63"][0]:COLS_A["e63"][1]].broadcast_to([D, HEADS]))
            last.then_inc(vb_ready, 1)
            nc.vector.tensor_scalar(ycol[:, :], col("gn_w"), 0.0, col("gn_b"), ALU.mult, ALU.add).then_inc(vec_step, steps.one())
            own()
            nc.vector.tensor_scalar(woy[:, :], A("wo"), ycol[:, :], None, ALU.mult).then_inc(woy_ready, 1)
            nc.vector.tensor_copy(sel0r[:, :, :], A("sel0", 96).rearrange("p (e n) -> p e n", e=E0)).then_inc(sel0_ready, 1)

            def norm(S):
                for b in range(B):
                    vector.wait_ge(rstd_ready, 4 * S + b + 1)
                    ins = nc.vector.tensor_tensor(xhat[:, b, :], bank(b), rstd_buf(S)[:, b, :], ALU.mult)
                    if S == TOK2:
                        ins.then_inc(vec_step, steps.one())
                        own()
                        ins = nc.vector.tensor_scalar(xhat[:, b, :], xhat[:, b, :], col("ln2_g"), col("ln2_b"), ALU.mult, ALU.add)
                    ins.then_inc(normed, 1)

            norm(TOK2)
            norm(POOL3)
            norm(GATE)
            for b in range(B):
                vector.wait_ge(main_full, 3 * B + b + 1)
                nc.vector.scalar_tensor_tensor(H[:, b, :], bank(4 + b), col("abias"), H[:, b, :], ALU.add, ALU.add)\
                  .then_inc(h_ready, 1)
            norm(MOE0)

            def tt(o, a, b_, op):
                nc.vector.tensor_tensor(o, a, b_, op).then_inc(vec_step, steps.one())
                own()

            def reduce(o, a, op):
                nc.vector.tensor_reduce(o, a, AX.X, op).then_inc(vec_step, steps.one())
                own()

            def gating(gate, E, bias, idx, pair_softmax, asked):
                N = B * NGT * 2
                wide = [GT, N, E]

                def over(r):
                    return r.unsqueeze(2).broadcast_to(wide)
                vector.wait_ge(logits_full, asked["logits"])
                lg = P[0:GT, 4, 0:N * E].rearrange("p (n e) -> p n e", e=E)
                if bias is not None:
                    tt(gate.a[:, :, :], lg, bias.unsqueeze(1).broadcast_to(wide), ALU.add)
                    lg = gate.a[:, :, :]
                reduce(gate.m[:, :], lg, ALU.max)
                nc.vector.tensor_tensor(gate.dif, lg, over(gate.m[:, :]), ALU.subtract).then_inc(expo_in, 1)
                vector.wait_ge(expo_out, asked["exp"])
                reduce(gate.m[:, :], gate.ex, ALU.add)
                nc.vector.reciprocal(gate.m[:, :], gate.m[:, :]).then_inc(vec_step, steps.one())
                own()
                tt(gate.p[:, :, :], gate.ex, over(gate.m[:, :]), ALU.mult)
                best = [gate.v1[:, :], gate.v2[:, :]]
                chosen = [gate.s1[:, :, :], gate.s2[:, :, :]]
                probs = gate.p[:, :, :]
                for r, s in zip(best, chosen):
                    reduce(r, probs, ALU.max)
                    tt(s, probs, over(r), ALU.is_equal)
                    tt(s, s, idx.unsqueeze(1).broadcast_to(wide), ALU.mult)
                    reduce(gate.m[:, :], s, ALU.max)
                    tt(s, s, over(gate.m[:, :]), ALU.is_equal)
                    if r is best[0]:
                        nc.vector.scalar_tensor_tensor(gate.a[:, :, :], s, -2.0, probs, ALU.mult, ALU.add)\
                          .then_inc(vec_step, steps.one())
                        own()
                        probs = gate.a[:, :, :]
                if pair_softmax:
                    nc.vector.tensor_tensor(gate.d21, gate.v2[:, :], gate.v1[:, :], ALU.subtract).then_inc(expo_in, 1)
                    vector.wait_ge(expo_out, asked["exp"] + 1)
                    nc.vector.tensor_scalar(gate.m[:, :], gate.e21, 1.0, None, ALU.add).then_inc(vec_step, steps.one())
                    own()
                    nc.vector.reciprocal(gate.v1[:, :], gate.m[:, :]).then_inc(vec_step, steps.one())
                    own()
                    tt(gate.v2[:, :], gate.e21, gate.v1[:, :], ALU.mult)
                else:
                    tt(gate.m[:, :], gate.v1[:, :], gate.v2[:, :], ALU.add)
                    nc.vector.tensor_scalar(gate.m[:, :], gate.m[:, :], 1e-12, None, ALU.max).then_inc(vec_step, steps.one())
                    own()
                    nc.vector.reciprocal(gate.m[:, :], gate.m[:, :]).then_inc(vec_step, steps.one())
                    own()
                    tt(gate.v1[:, :], gate.v1[:, :], gate.m[:, :], ALU.mult)
                    tt(gate.v2[:, :], gate.v2[:, :], gate.m[:, :], ALU.mult)
                tt(gate.s1[:, :, :], gate.s1[:, :, :], over(gate.v1[:, :]), ALU.mult)
                tt(gate.s2[:, :, :], gate.s2[:, :, :], over(gate.v2[:, :]), ALU.mult)
                tt(gate.p[:, :, :], gate.s1[:, :, :], gate.s2[:, :, :], ALU.add)
                w = gate.p.rearrange("p (n h) e -> p n (h e)", h=2)
                hi, lo = gate.wsp[:, :, 0:2 * E], gate.wsp[:, :, 32:32 + 2 * E]
                nc.vector.tensor_copy(hi, w).then_inc(vec_step, steps.one())
                own()
                nc.vector.tensor_tensor(lo, w, hi.bitcast(F32), ALU.subtract).then_inc(gates_ready, 1)

            nc.vector.memset(gate0.wsp[:, :, :].bitcast(F32), 0.0).then_inc(vec_step, steps.one())
            own()
            gating(gate0, E0, A("gb", GT)[:, 0:E0], A("idx0", GT), True, {"logits": 1, "exp": 1})

            def times_gate(n, buf):
                vector.wait_ge(wbc_full, n + 1)
                nc.vector.tensor_tensor(buf, bank(5 + n % 2), buf, ALU.mult).then_inc(wbc_done, 1)

            for b in range(B):
                for e in range(E0):
                    times_gate(E0 * b + e, h2[:, e, :])
                vector.wait_ge(moe_full, b + 1)
                nc.vector.scalar_tensor_tensor(H[:, b, :], bank(7), col("sb3"), H[:, b, :], ALU.add, ALU.add)\
                  .then_inc(h_ready, 1)

            norm(ATT)
            for n in range(8 * B):
                b, k = n // 8, n % 8
                cols = (slice(None), k // 4, 2 * b + k // 2 % 2, slice(k % 2 * HALF, (k % 2 + 1) * HALF))
                vector.wait_ge(qk_hi, n + 1)
                nc.vector.tensor_tensor(QKL[cols], bank(k % 4), QKH[cols].bitcast(F32), ALU.subtract).then_inc(qk_lo, 1)

            vector.wait_ge(xv_done, B)
            nc.vector.memset(Ks[96:98, :, :].bitcast(F32), 1.0)
            nc.vector.memset(CT[D:128, 3 * T:4 * T], 0.0).then_inc(vec_step, steps.one())
            own()
            nc.vector.memset(CT[0:D, 3 * T:4 * T], 0.0).then_inc(slots_set, 1)

            def row_max(i, s, t):
                vector.wait_ge(max_full, 8 * (4 * i + s) + t + 1)
                nc.vector.tensor_reduce(mx[:, t:t + 1], P[0:T, 0:2, 0:HALF], AX.XY, ALU.max).then_inc(max_done, 1)

            def minus_max(i, s):
                vector.wait_ge(max_done, 8 * (4 * i + s) + 7)
                nc.vector.tensor_scalar(mhl[:, 0:NT], mx[:, :], -1.0, None, ALU.mult).then_inc(vec_step, steps.one())
                own()
                nc.vector.scalar_tensor_tensor(mhl[:, NT:2 * NT], mx[:, :], -1.0, mhl[:, 0:NT].bitcast(F32),
                                               ALU.mult, ALU.subtract).then_inc(mhl_ready, 1)

            def max_rows(i, s):
                vector.wait_ge(max_full, 8 * (4 * i + s) + 8)
                nc.vector.tensor_copy(mT[:, :], P[0:2 * NT, 0, 0:T]).then_inc(max_done, 1)

            def divide(i, s):
                vector.wait_ge(proj_full, 4 * i + s + 1)
                got = P[0:T, 7, 0:NT * (D + 1)].rearrange("p (t d) -> p t d", d=D + 1)
                nc.vector.reciprocal(zi[:, :], got[:, :, D]).then_inc(vec_step, steps.one())
                own()
                over = zi[:, :].unsqueeze(2).broadcast_to([T, NT, D])
                dst = OUT[:, i, :] if s == 0 else part[:, :]
                nc.vector.tensor_tensor(dst.rearrange("p (t d) -> p t d", d=D), got[:, :, 0:D], over, ALU.mult)\
                  .then_inc(proj_done, 1)
                vector.wait_ge(proj_done, 4 * i + s + 1)
                if s:
                    nc.vector.tensor_tensor(OUT[:, i, :], OUT[:, i, :], part[:, :], ALU.add).then_inc(sums, 1)
                    vector.wait_ge(sums, 3 * i + s)

            def four_heads(i, first=False, final=False):
                for s in range(4):
                    for u in range(NT):
                        ahead = 7 * s + u + LEAD
                        if u == 3 and not (first and s == 0):
                            divide(i if s else i - 1, (s - 1) % 4)
                        if u == 2 and not (final and s == 3):
                            max_rows(i + (s == 3), (s + 1) % 4)
                        if not (final and ahead >= 28):
                            row_max(i + ahead // 28, ahead // 7 % 4, ahead % 7)
                            if u == 1:
                                minus_max(i + ahead // 28, ahead // 7 % 4)

            for j in range(LEAD):
                if j == 7:
                    minus_max(0, 0)
                    max_rows(0, 0)
                row_max(0, j // 7, j % 7)
            four_heads(0, first=True)
            repeat(vector, 1, 7, {steps: 4 * 2}, four_heads)
            four_heads(7, final=True)
            divide(7, 3)

            for b in range(B):
                vector.wait_ge(join_full, b + 1)
                nc.vector.tensor_tensor(H[:, b, :], bank(b), H[:, b, :], ALU.add).then_inc(h_ready, 1)

            nc.vector.tensor_copy(sel1r[:, :, :], Bt("sel1", 96).rearrange("p (e n) -> p e n", e=E1)).then_inc(sel1_ready, 1)
            nc.vector.memset(gate1.wsp[:, :, :].bitcast(F32), 0.0).then_inc(vec_step, steps.one())
            own()
            norm(MOE1)
            gating(gate1, E1, None, Bt("idx1", GT), False, {"logits": 2, "exp": 3})
            for b in range(B):
                for e in range(E1):
                    times_gate(B * E0 + E1 * b + e, g1[:, b % 2, e, :])
                vector.wait_ge(moe_full, B + b + 1)
                tt(xhat[:, b, :], bank(7), xhat[:, b, :], ALU.add)
                nc.vector.tensor_tensor(H[:, b, :], xhat[:, b, :], H[:, b, :], ALU.add).then_inc(h_ready, 1)


class Gate:

    def __init__(self, tile, E):
        N = B * NGT * 2
        wide = {n: tile(f"gate{E}_{n}", [GT, N, E]) for n in ("a", "dif", "ex", "p", "s1", "s2")}
        flat = {n: tile(f"gate{E}_{n}", [GT, N]) for n in ("m", "v1", "v2", "d21", "e21")}
        self.a, self.p, self.s1, self.s2 = wide["a"], wide["p"], wide["s1"], wide["s2"]
        self.dif, self.ex = wide["dif"][:, :, :], wide["ex"][:, :, :]
        self.m, self.v1, self.v2 = flat["m"], flat["v1"], flat["v2"]
        self.d21, self.e21 = flat["d21"][:, :], flat["e21"][:, :]
        self.wsp = tile(f"gate{E}_wsp", [GT, B * NGT, 96], F32R)


def kernel(**inputs):
    import concourse.bacc as bacc
    from concourse.bass_utils import run_bass_kernel_spmd as run

    a = {k: np.asarray(v) for k, v in inputs.items()}
    tok = {k[7:]: v for k, v in a.items() if k.startswith("L0_tok_")}
    gate = {k[8:]: v for k, v in a.items() if k.startswith("L0_attn_")}
    moe0 = {k[7:]: v for k, v in a.items() if k.startswith("L0_ffn_")}
    moe1 = {k[7:]: v for k, v in a.items() if k.startswith("L1_ffn_")}

    def table(cols, width, blocks):
        t = np.zeros((128, width), np.float32)
        for name, value in blocks.items():
            lo, hi = cols[name]
            t[0:value.shape[0], lo:hi] = value.reshape(value.shape[0], hi - lo)
        return t

    def diag(w):
        m = np.zeros((128, 2 * w.shape[1]), np.float32)
        m[0:D, 0:w.shape[1]] = w
        m[D:128, w.shape[1]:] = w
        return m

    def side(w):
        m = np.zeros((128, 2, w.shape[1]), np.float32)
        m[0:D, 0] = w
        m[D:128, 1] = w
        return m

    def twice(v):
        return np.concatenate([v, v]).reshape(128, 1)

    def features(v):
        v = v.reshape(PS * PS, C, -1).transpose(1, 0, 2).reshape(2, KF, -1)
        return v.transpose(1, 0, 2)

    def selectors(E):
        m = np.zeros((96, E, 128), np.float32)
        for e in range(E):
            for h in range(2):
                m[h * E + e, e, h * D:(h + 1) * D] = 1
                m[32 + h * E + e, e, h * D:(h + 1) * D] = 1
        return m

    def gate_biases(v):
        E = v.shape[0]
        m = np.zeros((96, 128), np.float32)
        for h in range(2):
            for r in (0, 32):
                m[r + h * E:r + (h + 1) * E, h * D:(h + 1) * D] = v
        return m

    fold = np.eye(D, dtype=np.float32)
    fold[D - 1, :] = -1
    fold[:, D - 1] = 0
    e63 = np.zeros((128, 1), np.float32)
    e63[[D - 1, 127]] = 1
    eye = np.eye(128, dtype=np.float32)
    ones = np.full((D, D), 1.0 / D, np.float32)
    qk = np.stack([np.stack([side(w[4 * g:4 * g + 4].reshape(4 * R, D).T) for g in range(2)], 1)
                   for w in (a["L1_attn_Q"], a["L1_attn_K"])], 1)
    common = {"ident": eye, "center": diag(np.eye(D, dtype=np.float32) - ones), "mean": diag(ones)}
    table_a = table(COLS_A, WIDTH_A, common | {
        "w1": features(tok["W1"]), "wp1": diag(tok["Wp1"]), "wp2": diag(tok["Wp2"]),
        "wg": diag(gate["wg"]), "wo": diag(gate["wo"]), "sw1": diag(moe0["sW1"]),
        "ew1": np.stack([side(moe0["eW1"][e]) for e in range(E0)], 1),
        "ew2": moe0["eW2"].transpose(1, 0, 2), "ew3": np.stack([diag(moe0["eW3"][e]) for e in range(E0)], 1),
        "sw2": side(moe0["sW2"]), "sw3": moe0["sW3"], "gw": diag(moe0["gW"]), "eb3": gate_biases(moe0["eb3"]),
        "sel0": selectors(E0), "gb": np.tile(moe0["gb"], (128, 2)),
        "idx0": np.tile(np.arange(E0, 0, -1, dtype=np.float32), (128, 1)),
        "qk": qk, "vo": a["L1_attn_VO"].transpose(1, 0, 2), "fold": fold, "e63": e63,
        "ln1_g": features(tok["ln1_g"]), "ln1_b": features(tok["ln1_b"]), "b1": twice(tok["b1"]),
        "ln2_g": twice(tok["ln2_g"]), "ln2_b": twice(tok["ln2_b"]), "bp1": twice(tok["bp1"]),
        "lnp_g": twice(tok["lnp_g"]), "lnp_b": twice(tok["lnp_b"]), "bp2": twice(tok["bp2"]),
        "gn_w": twice(gate["gn_weight"]), "gn_b": twice(gate["gn_bias"]), "abias": twice(gate["bias"]),
        "sb1": twice(moe0["sb1"]), "eb1": moe0["eb1"].T, "sb2": moe0["sb2"].reshape(128, 1),
        "eb2": np.concatenate([moe0["eb2"].T, moe0["eb2"].T]), "sb3": twice(moe0["sb3"])})
    table_b = table(COLS_B, WIDTH_B, common | {
        "router": diag(moe1["router_w"].T), "mw1": np.stack([diag(moe1["w1"][e]) for e in range(E1)], 1),
        "mw2": np.stack([diag(moe1["w2"][e]) for e in range(E1)], 1), "mb2": gate_biases(moe1["b2"]),
        "sel1": selectors(E1), "idx1": np.tile(np.arange(E1, 0, -1, dtype=np.float32), (128, 1)),
        "mb1": np.concatenate([moe1["b1"].T, moe1["b1"].T])})

    nc = bacc.Bacc("TRN2", target_bir_lowering=False, num_devices=1)
    arrays = {"x": np.ascontiguousarray(a["x"]), "table_a": table_a, "table_b": table_b}
    aps = [nc.dram_tensor(n, v.shape, F32, kind="ExternalInput").ap() for n, v in arrays.items()]
    result = nc.dram_tensor("out", (B, REP * TOK, D), F32, kind="ExternalOutput").ap()
    build(nc, *aps, result)
    r = run(nc, [arrays], core_ids=[0])
    return r.results[0]["out"]
```

```python
from contextlib import ExitStack

import numpy as np

import concourse.bass as bass
from concourse import mybir
from concourse.alu_op_type import AluOpType as ALU

F32 = mybir.dt.float32
F32R = mybir.dt.float32r
ACT = mybir.ActivationFunctionType
AX = mybir.AxisListType

B, C, IMG, PS = 4, 3, 224, 8
NP = IMG // PS
TOK = NP * NP
HALF = TOK // 2
HCOL = NP // 2
D = 64
FEAT = C * PS * PS
KF = FEAT // 2
REP = 3
EPS = 1e-5
T = 112
NT = TOK // T
HEADS, R = 8, 32
HG = 4
NH = B * HEADS
TURN = 1
LEAD = 15
E0, E1 = 4, 8
PAIRS = E1 // 2
GT = 98
NGT = HALF // GT
HROWS = 98
OJ, OC = 2, HCOL // 2
GROUPS = 7


class Tally:

    def __init__(self, start=0):
        self.n, self.reg = start, 0

    def one(self):
        self.n += 1
        return 1

    def now(self):
        return self.reg + self.n

    def next(self):
        return self.reg + self.n + 1


def repeat(engine, start, stop, per, body):
    before = {t: t.n for t in per}
    with engine.Fori(start, stop) as i:
        for t, k in per.items():
            t.reg = (i - start) * k if start else i * k
        body(i)
        for t, k in per.items():
            assert t.n - before[t] == k, (t.n - before[t], k)
    for t, k in per.items():
        t.n, t.reg = before[t] + k * (stop - start), 0


TABLE_A = [("ident", 128), ("w1", 2 * D), ("ln1_g", 2), ("ln1_b", 2), ("b1", 1),
           ("wp1", 128), ("wp2", 128),
           ("wg", 128), ("wo", 128), ("sw1", 128), ("ew1", E0 * 128), ("ew2", E0 * D),
           ("ew3", E0 * 128), ("sw2", 2 * 128), ("sw3", D), ("gw", 2 * E0), ("eb3", 128),
           ("sel0", E0 * 128), ("gb", 2 * E0), ("idx0", E0),
           ("qk", 2 * 2 * 2 * 128), ("vo", HEADS * D), ("fold", D), ("e63", 1),
           ("ln2_g", 1), ("ln2_b", 1), ("bp1", 1),
           ("lnp_g", 1), ("lnp_b", 1), ("bp2", 1), ("gn_w", 1), ("gn_b", 1), ("abias", 1),
           ("sb1", 1), ("eb1", E0), ("sb2", 1), ("eb2", E0), ("sb3", 1)]
TABLE_B = [("ident", 128), ("center", 128), ("mean", 128), ("router", 2 * E1), ("mw1", PAIRS * 128),
           ("mw2", PAIRS * D), ("mb2", 128), ("sel1", E1 * 128), ("idx1", E1), ("mb1", PAIRS)]


def columns(table):
    at, out = 0, {}
    for name, n in table:
        out[name] = (at, at + n)
        at += n
    return out, at


COLS_A, WIDTH_A = columns(TABLE_A)
EARLY_A = COLS_A["wp1"][0]
COLS_B, WIDTH_B = columns(TABLE_B)


def build(nc, x, table_a, table_b, out):
    ctx = ExitStack()
    with ctx:
        def sem(name):
            return ctx.enter_context(nc.semaphore(name))

        def sb(stack, name, shape, dt=F32):
            return stack.enter_context(nc.sbuf_tensor(name, shape, dt))

        wb = sb(ctx, "wb", [128, WIDTH_B])
        H = sb(ctx, "H", [128, B, HALF])
        xhat = sb(ctx, "xhat", [128, B, HALF])
        eps = sb(ctx, "eps", [128, 1])
        VB = sb(ctx, "VB", [128, HEADS, 2 * D + 2])
        XV = sb(ctx, "XV", [T, B, NT, D])

        reg1 = ExitStack()
        state = sb(reg1, "state", [128, B, HALF])
        act = sb(reg1, "act", [128, B, HALF])
        sel0r = sb(reg1, "sel0r", [96, E0, 128], F32R)
        woy = sb(reg1, "woy", [128, 128])
        ycol = sb(reg1, "ycol", [128, 1])
        patches = ExitStack()
        X = sb(patches, "X", [T, C, PS, IMG])
        xn = sb(patches, "xn", [T, 2, 4, FEAT])
        xT = sb(patches, "xT", [KF, 2, 2, 4 * T])
        bst = sb(patches, "bst", [T, 2, 4, 6])
        mv = sb(patches, "mv", [T, 2, 4, 2])
        sd = sb(patches, "sd", [T, 2, 4])
        ri = sb(patches, "ri", [T, 2, 4])
        patches.close()
        xhl0 = sb(reg1, "xhl0", [128, B, 2, HALF], F32R)
        xs0 = sb(reg1, "xs0", [128, B, TOK], F32R)
        ew1r = sb(reg1, "ew1r", [128, 2, E0, 128], F32R)
        h1 = sb(reg1, "h1", [128, E0, 2, HALF])
        h2 = sb(reg1, "h2", [128, E0, HALF])
        s1 = sb(reg1, "s1", [128, HALF])
        s2 = sb(reg1, "s2", [128, 2, HALF])
        gate0 = Gate(lambda n, shape, dt=F32: sb(reg1, n, shape, dt), E0)
        wT0 = sb(reg1, "wT0", [96, HALF], F32R)
        reg1.close()
        reg1 = ExitStack()
        QKH = sb(reg1, "QKH", [128, 2, B * 2, TOK], F32R)
        QKL = sb(reg1, "QKL", [128, 2, B * 2, TOK], F32R)

        reg2 = ExitStack()
        wa = sb(reg2, "wa", [128, WIDTH_A])
        XF = sb(reg2, "XF", [D, B, TOK])
        sq = sb(reg2, "sq", [128, B, HALF])
        rs = sb(reg2, "rs", [128, B, HALF])
        reg2.close()
        reg2 = ExitStack()
        XVs = sb(reg2, "XVs", [T, 4, NT * D])
        VBs = sb(reg2, "VBs", [128, 4, 2 * D + 2])
        PT = sb(reg2, "PT", [T, 2, TOK])
        CT = sb(reg2, "CT", [128, 4 * T])
        mx = sb(reg2, "mx", [T, 2, NT])
        mxf = sb(reg2, "mxf", [T, NT])
        mhl = sb(reg2, "mhl", [T, 2 * NT], F32R)
        mT = sb(reg2, "mT", [2 * NT, T], F32R)
        zi = sb(reg2, "zi", [T, NT])
        part = sb(reg2, "part", [T, 3, NT * D])
        acc = sb(reg2, "acc", [T, 2, NT * D])
        OUT = sb(reg2, "OUT", [T, 2 * B, NT * D])
        Qs = sb(reg2, "Qs", [HROWS, 4, TOK], F32R)
        Ks = sb(reg2, "Ks", [HROWS, 4, TOK], F32R)
        reg2.close()
        reg1.close()

        reg1 = ExitStack()
        sqm = sb(reg1, "sqm", [128, B, HALF])
        rsm = sb(reg1, "rsm", [128, B, HALF])
        wT1 = sb(reg1, "wT1", [96, 2, HALF], F32R)
        sel1r = sb(reg1, "sel1r", [96, PAIRS, 2, 128], F32R)
        mw1r = sb(reg1, "mw1r", [128, 2, PAIRS, 128], F32R)
        gate1 = Gate(lambda n, shape, dt=F32: sb(reg1, n, shape, dt), E1)
        xhl1 = sb(reg1, "xhl1", [128, B, 2, HALF], F32R)
        xs1 = sb(reg1, "xs1", [128, B, TOK], F32R)
        g1 = sb(reg1, "g1", [128, B, PAIRS, 2, HALF])
        Y = sb(reg1, "Y", [128, B, HALF])
        OT = sb(reg1, "OT", [OJ * NP, B, 2, OC * D])
        reg1.close()

        row_store = [nc.dram_tensor(f"row_store{n}", (2, TOK), F32, kind="Internal").ap() for n in range(4)]
        P = ctx.enter_context(nc.psum_tensor("P", [128, 8, 512], F32))

        def bank(n, w=HALF):
            return P[:, n, 0:w]

        def A(name, rows=128):
            lo, hi = COLS_A[name]
            return wa[0:rows, lo:hi]

        def Bt(name, rows=128):
            lo, hi = COLS_B[name]
            return wb[0:rows, lo:hi]

        def col(name, n=0, rows=128):
            lo = COLS_A[name][0] + n
            return wa[0:rows, lo:lo + 1]

        def square_buf(S):
            return sqm if S == 5 else sq

        def rstd_buf(S):
            return rsm if S == 5 else rs

        TOK2, POOL3, GATE, MOE0, ATT, MOE1 = range(6)

        pixels_in, wa_in, wb_in = sem("pixels_in"), sem("wa_in"), sem("wb_in")
        xf_in = [sem(f"xf_in{b}") for b in range(B)]
        vec_step, act_step = sem("vec_step"), sem("act_step")
        split0, split1, w0_split, w1_split = sem("split0"), sem("split1"), sem("w0_split"), sem("w1_split")
        xs0_in, xs1_in = [[sem(f"xs{m}_in{b}") for b in range(B)] for m in range(2)]
        eps_set, woy_ready, sel0_ready, sel1_ready = sem("eps_set"), sem("woy_ready"), sem("sel0_ready"), sem("sel1_ready")
        stats_ready, sd_ready, xn_ready = sem("stats_ready"), sem("sd_ready"), sem("xn_ready")
        turned, xT_ready, patch_full, t0_done = sem("turned"), sem("xT_ready"), sem("patch_full"), sem("t0_done")
        vo_full, vb_ready = sem("vo_full"), sem("vb_ready")
        centred, squared, var_full, rstd_ready, normed = (sem("centred"), sem("squared"), sem("var_full"),
                                                          sem("rstd_ready"), sem("normed"))
        main_full, t1_ready, silu_ready, h0_ready = sem("main_full"), sem("t1_ready"), sem("silu_ready"), sem("h0_ready")
        h_ready = sem("h_ready")
        logits_full, expo_in, expo_out, gates_ready = (sem("logits_full"), sem("expo_in"), sem("expo_out"),
                                                       sem("gates_ready"))
        hid_full, hid_done = sem("hid_full"), sem("hid_done")
        wbc_full, wbc_done, moe_full = sem("wbc_full"), sem("wbc_done"), sem("moe_full")
        qk_full, qk_hi, qk_lo = sem("qk_full"), sem("qk_hi"), sem("qk_lo")
        xv_full, xv_done, slots_set = sem("xv_full"), sem("xv_done"), sem("slots_set")
        slot_in = [sem(f"slot_in{s}") for s in range(4)]
        value_in = [sem(f"value_in{s}") for s in range(4)]
        mrow_in = [sem(f"mrow_in{s}") for s in range(4)]
        rows_out = sem("rows_out")
        max_full, max_done, mhl_ready = sem("max_full"), sem("max_done"), sem("mhl_ready")
        turn_full, turn_done = sem("turn_full"), sem("turn_done")
        st_full, exp_done, av_done, ctx_done = sem("st_full"), sem("exp_done"), sem("av_done"), sem("ctx_done")
        proj_full, proj_done = sem("proj_full"), sem("proj_done")
        sums, grouped, summed, join_full = sem("sums"), sem("grouped"), sem("summed"), sem("join_full")
        out_full, out_copied, stored = sem("out_full"), sem("out_copied"), [sem(f"stored{b}") for b in range(B)]

        block = ctx.enter_context(nc.Block())
        OUT_PARTS = ((0, 4), (4, OC))

        H_AFTER = {GATE: 0, MOE0: B, ATT: 2 * B, MOE1: 3 * B}

        def hid_index():
            index, n = {}, 0
            for b in range(B + 1):
                if b >= 1:
                    for e in range(E0):
                        index["l2", b - 1, e] = n
                        n += 1
                    for h in range(2):
                        index["s2", b - 1, h] = n
                        n += 1
                    index["wT", b - 1] = n
                    n += 1
                if b < B:
                    for e in range(E0):
                        for h in range(2):
                            index["l1", b, e, h] = n
                            n += 1
                    index["s1", b] = n
                    n += 1
            base = n
            for b in range(B + 1):
                if b >= 1:
                    index["wT1", b - 1] = n
                    n += 1
                if b == 0:
                    for c in range(B):
                        for p in range(PAIRS):
                            for h in range(2):
                                index["g1", c, p, h] = n
                                n += 1
            return index, base

        HID, HID1 = hid_index()

        @block.sync
        def _(sync):
            for b in range(B):
                sync.dma_start(X[NP * b:NP * (b + 1), :, :, :].rearrange("i c p w -> i c (p w)"),
                               x[b].rearrange("c (i p) w -> i c (p w)", p=PS)).then_inc(pixels_in, 16)
            sync.wait_ge(pixels_in, 16 * B)
            sync.dma_start(wa[:, EARLY_A:WIDTH_A], table_a[:, EARLY_A:WIDTH_A]).then_inc(wb_in, 16)
            sync.dma_start(wb[:, :], table_b).then_inc(wb_in, 16)

            def stack_parts(split, xhl, xs, done):
                for b in range(B):
                    sync.wait_ge(split, b + 1)
                    for h in range(2):
                        for part in range(2):
                            sync.dma_start(xs[part * D:(part + 1) * D, b, h * HALF:(h + 1) * HALF].bitcast(F32),
                                           xhl[h * D:(h + 1) * D, b, part, :].bitcast(F32)).then_inc(done[b], 16)

            stack_parts(split0, xhl0, xs0, xs0_in)
            for b in range(B):
                sync.wait_ge(normed, 4 * ATT + b + 1)
                for h in range(2):
                    sync.dma_start(XF[:, b, h * HALF:(h + 1) * HALF],
                                   xhat[h * D:(h + 1) * D, b, :]).then_inc(xf_in[b], 16)

            def fill_stacks(i, s):
                rows = slice(s * R, (s + 1) * R)
                for dst, src in ((Qs[0:R, s, :], QKH[rows, 0, i, :]), (Qs[R:2 * R, s, :], QKH[rows, 0, i, :]),
                                 (Qs[2 * R:3 * R, s, :], QKL[rows, 0, i, :]),
                                 (Ks[0:R, s, :], QKH[rows, 1, i, :]), (Ks[R:2 * R, s, :], QKL[rows, 1, i, :]),
                                 (Ks[2 * R:3 * R, s, :], QKH[rows, 1, i, :])):
                    sync.dma_start(dst.bitcast(F32), src.bitcast(F32)).then_inc(slot_in[s], 16)

            def fill_values(b, group, s):
                sync.dma_start(XVs[:, s, :], XV[:, b, :, :].rearrange("p t d -> p (t d)")).then_inc(value_in[s], 16)
                sync.dma_start(VBs[:, s, :], VB[:, group * 4 + s, :]).then_inc(value_in[s], 16)

            def rows_to_store(i, s):
                sync.wait_ge(turn_done, 4 * i + s + 1)
                sync.dma_start(row_store[s].rearrange("r (t c) -> (r t) c", c=T), mT[:, :].bitcast(F32)).then_inc(rows_out, 16)

            def rows_to_stack(i, s):
                sync.wait_ge(rows_out, 16 * (4 * i + s) + 16)
                sync.dma_start(Qs[96:98, s, :].bitcast(F32), row_store[s]).then_inc(mrow_in[s], 16)

            sync.wait_ge(qk_lo, 8)
            for s in range(4):
                fill_stacks(0, s)
            sync.wait_ge(slots_set, 1)
            for s in range(4):
                fill_values(0, 0, s)
            for s in range(2):
                rows_to_store(0, s)
                rows_to_stack(0, s)

            def heads(i, b, group):
                for s in range(4):
                    on = (i + (s >= 2), (s + 2) % 4)
                    rows_to_store(*on)
                    sync.wait_ge(st_full, 7 * (4 * i + s) + 7)
                    fill_stacks(i + 1, s)
                    rows_to_stack(*on)
                    sync.wait_ge(proj_full, 4 * i + s + 1)
                    fill_values(b, group, s)

            def image(b):
                heads(2 * b, b, 1)
                heads(2 * b + 1, b + 1, 0)
            repeat(sync, 0, B - 1, {}, image)
            heads(2 * B - 2, B - 1, 1)
            for s in range(2, 4):
                rows_to_store(2 * B - 1, s)
                rows_to_stack(2 * B - 1, s)
            stack_parts(split1, xhl1, xs1, xs1_in)
            rows = out.rearrange("b (k i h j cd) d -> b i k h j (cd d)", k=REP, i=NP, h=2, j=OJ)
            for b in range(B):
                sync.wait_ge(out_copied, 2 * (b + 1))
                for j in range(OJ):
                    for k in range(REP):
                        sync.dma_start(rows[b, :, k, :, j, :], OT[j * NP:(j + 1) * NP, b, :, :]).then_inc(stored[b], 16)
            for b in range(B):
                sync.wait_ge(stored[b], 16 * REP * OJ)

        @block.scalar
        def _(scalar):
            scalar.dma_start(wa[:, 0:EARLY_A], table_a[:, 0:EARLY_A]).then_inc(wa_in, 16)
            steps = Tally()

            def deviations(g, p):
                scalar.wait_ge(stats_ready, g + 1)
                nc.scalar.activation(sd[:, p, :], mv[:, p, :, 1], ACT.Sqrt, bias=eps[0:T, :]).then_inc(sd_ready, 1)

            def turned_patches(g, p):
                scalar.wait_ge(turned, g + 1)
                for k in range(2):
                    nc.scalar.activation(xT[:, p, k, :], P[0:KF, 2 * p + k, 0:4 * T], ACT.Identity,
                                         bias=col("ln1_b", k, KF), scale=col("ln1_g", k, KF)).then_inc(xT_ready, 1)

            def tokens_out(g, p):
                scalar.wait_ge(patch_full, g + 1)
                nc.scalar.activation(
                    state.rearrange("p b (j i) -> p b j i", i=NP)[:, :, bass.ds(2 * g, 2), :].rearrange("p b j i -> p j b i"),
                    P[:, 4 + p, 0:2 * T].rearrange("p (j b i) -> p j b i", j=2, b=B), ACT.Identity,
                    bias=col("b1")).then_inc(t0_done, 1)

            scalar.wait_ge(eps_set, 1)
            scalar.wait_ge(wa_in, 16)
            deviations(0, 0)
            deviations(1, 1)
            turned_patches(0, 0)

            def cycle(g, p):
                deviations(g + 1, 1 - p)
                turned_patches(g, p)
                tokens_out(g - 1, 1 - p)

            def two(i):
                cycle(2 * i + 1, 1)
                cycle(2 * i + 2, 0)
            repeat(scalar, 0, 2, {}, two)
            cycle(5, 1)
            turned_patches(6, 0)
            tokens_out(5, 1)
            tokens_out(6, 0)

            def norm(S):
                for b in range(B):
                    scalar.wait_ge(centred, 4 * S + b + 1)
                    nc.scalar.activation(square_buf(S)[:, b, :], bank(b), ACT.Square).then_inc(squared, 1)
                for b in range(B):
                    scalar.wait_ge(var_full, 4 * S + b + 1)
                    nc.scalar.activation(rstd_buf(S)[:, b, :], bank(4 + b), ACT.Ln, bias=eps[:, :]).then_inc(act_step, steps.one())
                for b in range(B):
                    scalar.wait_ge(act_step, steps.now() - (B - 1 - b))
                    nc.scalar.activation(rstd_buf(S)[:, b, :], rstd_buf(S)[:, b, :], ACT.Exp, scale=-0.5).then_inc(rstd_ready, 1)

            norm(TOK2)
            for b in range(B):
                scalar.wait_ge(main_full, b + 1)
                nc.scalar.activation(state[:, b, :], bank(b), ACT.Identity, bias=col("bp1")).then_inc(t1_ready, 1)
            norm(POOL3)
            for b in range(B):
                scalar.wait_ge(normed, 4 * POOL3 + b + 1)
                nc.scalar.activation(act[:, b, :], xhat[:, b, :], ACT.Silu, bias=col("lnp_b"), scale=col("lnp_g"))\
                  .then_inc(silu_ready, 1)
            for b in range(B):
                scalar.wait_ge(main_full, B + b + 1)
                nc.scalar.activation(H[:, b, :], bank(b), ACT.Identity, bias=col("bp2")).then_inc(h0_ready, 1)
            norm(GATE)
            for b in range(B):
                scalar.wait_ge(main_full, 2 * B + b + 1)
                nc.scalar.activation(act[:, b, :], bank(b), ACT.Silu).then_inc(silu_ready, 1)
            norm(MOE0)

            def exponents(gate, n):
                src, dst = (gate.dif, gate.ex) if n == 0 else (gate.d21, gate.e21)
                nc.scalar.activation(dst, src, ACT.Exp).then_inc(expo_out, 1)

            def hidden(key, dst, func, bias=None, rows=128, width=HALF):
                k = HID[key]
                scalar.wait_ge(hid_full, k + 1)
                nc.scalar.activation(dst, P[0:rows, k % 4, 0:width], func, **({} if bias is None else dict(bias=bias)))\
                  .then_inc(hid_done, 1)

            for b in range(B + 1):
                if b >= 1:
                    c = b - 1
                    if c >= 1:
                        scalar.wait_ge(moe_full, c)
                    for e in range(E0):
                        hidden(("l2", c, e), h2[:, e, :], ACT.Relu, col("eb2", e))
                    for h in range(2):
                        hidden(("s2", c, h), s2[:, h, :], ACT.Relu, col("sb2"))
                    if c == 0:
                        scalar.wait_ge(expo_in, 2)
                        exponents(gate0, 1)
                    hidden(("wT", c), wT0[:, :], ACT.Copy, rows=96)
                if b < B:
                    for e in range(E0):
                        for h in range(2):
                            hidden(("l1", b, e, h), h1[:, e, h, :], ACT.Relu, col("eb1", e))
                            if b == 0 and e == 0 and h == 0:
                                scalar.wait_ge(expo_in, 1)
                                exponents(gate0, 0)
                    hidden(("s1", b), s1[:, :], ACT.Relu, col("sb1"))

            norm(ATT)
            for b in range(B):
                for k in range(8):
                    qk, group, h = k // 4, k // 2 % 2, k % 2
                    scalar.wait_ge(qk_full, 8 * b + k + 1)
                    nc.scalar.activation(QKH[:, qk, 2 * b + group, h * HALF:(h + 1) * HALF], bank(k % 4), ACT.Copy)\
                      .then_inc(qk_hi, 1)
                scalar.wait_ge(xv_full, b + 1)
                nc.scalar.activation(XV[:, b, :, 0:D - 1], P[0:T, 4 + b, 0:NT * D].rearrange("p (t d) -> p t d", d=D)[:, :, 0:D - 1],
                                     ACT.Copy).then_inc(xv_done, 1)

            scalar.wait_ge(slots_set, 1)

            def exp_tile(k, p, first):
                scalar.wait_ge(st_full, k + 1)
                if not first:
                    scalar.wait_ge(av_done, k - 1)
                nc.scalar.activation(PT[:, p, :].rearrange("p (c n) -> p c n", c=2), P[0:T, 2 + 2 * p:4 + 2 * p, 0:HALF],
                                     ACT.Exp, scale=float(D) ** -0.5).then_inc(exp_done, 1)

            def context_out(n, first):
                scalar.wait_ge(av_done, 7 * n + 7)
                if not first:
                    scalar.wait_ge(proj_full, n)
                nc.scalar.activation(CT[:, :], P[:, 6, 0:4 * T], ACT.Copy).then_inc(ctx_done, 1)

            def four_heads(i, first=False):
                for s in range(4):
                    for u in range(NT):
                        n, step = 4 * i + s, 7 * s + u
                        exp_tile(7 * n + u, step % 2, first and step < 2)
                        if u == 0 and not (first and s == 0):
                            context_out(n - 1, first and s == 1)
            four_heads(0, True)
            repeat(scalar, 1, 8, {}, four_heads)
            context_out(NH - 1, False)

            norm(MOE1)
            scalar.wait_ge(expo_in, 3)
            exponents(gate1, 0)

            def rows_out_of(b, part):
                c0, c1 = OUT_PARTS[part]
                scalar.wait_ge(out_full, 2 * b + part + 1)
                nc.scalar.activation(OT[:, b, :, :].rearrange("p h (c d) -> p h c d", d=D)[:, :, c0:c1, :],
                                     P[0:OJ * NP, 4, 0:(c1 - c0) * 128].rearrange("p (c h d) -> p h c d", h=2, d=D),
                                     ACT.Copy).then_inc(out_copied, 1)

            for b in range(B):
                for p in range(PAIRS):
                    for h in range(2):
                        hidden(("g1", b, p, h), g1[:, b, p, h, :], ACT.Gelu, Bt("mb1")[:, p:p + 1])
            for b in range(B):
                if b >= 2:
                    scalar.wait_ge(moe_full, B + b - 1)
                hidden(("wT1", b), wT1[:, b % 2, :], ACT.Copy, rows=96)
                if b >= 1:
                    for part in range(2):
                        rows_out_of(b - 1, part)
            for part in range(2):
                rows_out_of(B - 1, part)

        @block.gpsimd
        def _(pool):
            def heads(i):
                for s in (1, 2):
                    pool.wait_ge(proj_done, 4 * i + s + 1)
                    if s == 2:
                        pool.wait_ge(sums, 2 * i + 1)
                    nc.gpsimd.tensor_tensor(acc[:, s - 1, :], acc[:, 0, :] if s == 2 else part[:, 0, :],
                                                  part[:, s, :], ALU.add).then_inc(sums, 1)
            heads(0)
            repeat(pool, 1, 2 * B, {}, heads)

        @block.tensor
        def _(pe):
            def mm(dst, lhsT, rhs, start=True, stop=True, **more):
                return nc.tensor.matmul(dst, lhsT, rhs, start=start, stop=stop, **more)

            pe.wait_ge(wa_in, 16)
            def turn(g, p):
                pe.wait_ge(xn_ready, g + 1)
                for q in range(4):
                    for k in range(2):
                        last = nc.tensor.transpose(P[0:KF, 2 * p + k, q * T:(q + 1) * T], xn[:, p, q, k * KF:(k + 1) * KF],
                                                   A("ident", T)[:, 0:T])
                last.then_inc(turned, 1)

            def project(g, p):
                pe.wait_ge(xT_ready, 2 * g + 2)
                w1 = A("w1", KF).rearrange("p (k d) -> p k d", k=2)
                for k in range(2):
                    for h in range(2):
                        last = mm(P[h * D:(h + 1) * D, 4 + p, 0:2 * T], w1[:, k, :], xT[:, p, k, 2 * T * h:2 * T * (h + 1)],
                                  k == 0, k == 1)
                last.then_inc(patch_full, 1)

            turn(0, 0)

            def two(i):
                turn(2 * i + 1, 1)
                project(2 * i, 0)
                turn(2 * i + 2, 0)
                project(2 * i + 1, 1)
            repeat(pe, 0, 3, {}, two)
            project(6, 0)

            def norm(S, src, source, count):
                for b in range(B):
                    pe.wait_ge(source, count(b))
                    mm(bank(b), Bt("center"), src[:, b, :]).then_inc(centred, 1)
                for b in range(B):
                    pe.wait_ge(squared, 4 * S + b + 1)
                    mm(bank(4 + b), Bt("mean"), square_buf(S)[:, b, :]).then_inc(var_full, 1)

            pe.wait_ge(wb_in, 32)
            for h in range(2):
                last = mm(P[h * D:(h + 1) * D, 7, 0:HEADS * D], A("fold", D), A("vo", D))
            last.then_inc(vo_full, 1)
            pe.wait_ge(vb_ready, 1)
            norm(TOK2, state, t0_done, lambda b: GROUPS)
            for b in range(B):
                pe.wait_ge(normed, 4 * TOK2 + b + 1)
                mm(bank(b), A("wp1"), xhat[:, b, :]).then_inc(main_full, 1)
            norm(POOL3, state, t1_ready, lambda b: b + 1)
            for b in range(B):
                pe.wait_ge(silu_ready, b + 1)
                mm(bank(b), A("wp2"), act[:, b, :]).then_inc(main_full, 1)
            norm(GATE, H, h0_ready, lambda b: b + 1)
            for b in range(B):
                pe.wait_ge(normed, 4 * GATE + b + 1)
                mm(bank(b), A("wg"), xhat[:, b, :]).then_inc(main_full, 1)
            pe.wait_ge(woy_ready, 1)
            for b in range(B):
                pe.wait_ge(silu_ready, B + b + 1)
                mm(bank(4 + b), woy[:, :], act[:, b, :]).then_inc(main_full, 1)
            norm(MOE0, H, h_ready, lambda b: b + 1)

            def logits(weights, E, S):
                pe.wait_ge(normed, 4 * S + B)
                for b in range(B):
                    for ct in range(NGT):
                        at = (b * NGT + ct) * 2 * E
                        last = mm(P[0:GT, 4, at:at + 2 * E], xhat[:, b, ct * GT:(ct + 1) * GT], weights)
                last.then_inc(logits_full, 1)

            def bank_of(key, first):
                k = HID[key]
                if k - 4 >= first:
                    pe.wait_ge(hid_done, k - 3)
                return k % 4

            def gate_rows(key, wsp, b, first):
                n = bank_of(key, first)
                for ct in range(NGT):
                    last = nc.tensor.transpose(P[0:96, n, ct * GT:(ct + 1) * GT], wsp[:, b * NGT + ct, :].bitcast(F32),
                                               Bt("ident", GT)[:, 0:GT])
                last.then_inc(hid_full, 1)

            ew2 = A("ew2").rearrange("p (e n) -> p e n", e=E0)
            ew3 = A("ew3").rearrange("p (e n) -> p e n", e=E0)
            sw2 = A("sw2").rearrange("p (h n) -> p h n", h=2)

            def first_layer(b):
                pe.wait_ge(xs0_in[b], 64)
                if b == 0:
                    pe.wait_ge(w0_split, 1)
                for e in range(E0):
                    for h in range(2):
                        n = bank_of(("l1", b, e, h), 0)
                        for part in range(2):
                            last = mm(bank(n), ew1r[:, part, e, :], xs0[:, b, h * HALF:(h + 1) * HALF], part == 0, part == 1)
                        last.then_inc(hid_full, 1)
                mm(bank(bank_of(("s1", b), 0)), A("sw1"), xhat[:, b, :]).then_inc(hid_full, 1)

            def broadcast_gate(sel, rows, n):
                if n >= 2:
                    pe.wait_ge(wbc_done, n - 1)
                mm(bank(5 + n % 2), sel, rows).then_inc(wbc_full, 1)

            logits(A("gw"), E0, MOE0)
            first_layer(0)
            for b in range(B):
                for e in range(E0):
                    pe.wait_ge(hid_done, HID["l1", b, e, 1] + 1)
                    n = bank_of(("l2", b, e), 0)
                    for h in range(2):
                        last = mm(P[h * D:(h + 1) * D, n, 0:HALF], ew2[:, e, :], h1[:, e, h, :])
                    last.then_inc(hid_full, 1)
                pe.wait_ge(hid_done, HID["s1", b] + 1)
                for h in range(2):
                    mm(bank(bank_of(("s2", b, h), 0)), sw2[:, h, :], s1[:, :]).then_inc(hid_full, 1)
                if b == 0:
                    pe.wait_ge(gates_ready, 1)
                gate_rows(("wT", b), gate0.wsp, b, 0)
                if b + 1 < B:
                    first_layer(b + 1)
                pe.wait_ge(hid_done, HID["wT", b] + 1)
                if b == 0:
                    pe.wait_ge(sel0_ready, 1)
                for e in range(2):
                    broadcast_gate(sel0r[:, e, :], wT0[:, :], E0 * b + e)
                if b >= 1:
                    pe.wait_ge(h_ready, B + b)
                mm(bank(7), A("eb3", 96), wT0[:, :].bitcast(F32), True, False, skip_group_check=True)
                for h in range(2):
                    mm(P[h * D:(h + 1) * D, 7, 0:HALF], A("sw3"), s2[:, h, :], False, False, skip_group_check=True)
                for e in range(E0):
                    if e + 2 < E0:
                        broadcast_gate(sel0r[:, e + 2, :], wT0[:, :], E0 * b + e + 2)
                    pe.wait_ge(wbc_done, E0 * b + e + 1)
                    last = mm(bank(7), ew3[:, e, :], h2[:, e, :], False, e == E0 - 1, skip_group_check=True)
                last.then_inc(moe_full, 1)

            norm(ATT, H, h_ready, lambda b: B + b + 1)
            qk = A("qk").rearrange("p (q g h n) -> p q g h n", q=2, g=2, h=2)
            for b in range(B):
                pe.wait_ge(normed, 4 * ATT + b + 1)
                for k in range(8):
                    if 8 * b + k >= 4:
                        pe.wait_ge(qk_lo, 8 * b + k - 3)
                    elif b == 0:
                        pe.wait_ge(normed, 4 * ATT + B)
                    mm(bank(k % 4), qk[:, k // 4, k // 2 % 2, k % 2, :], xhat[:, b, :]).then_inc(qk_full, 1)
                pe.wait_ge(xf_in[b], 32)
                for t in range(NT):
                    last = nc.tensor.transpose(P[0:T, 4 + b, t * D:(t + 1) * D], XF[:, b, t * T:(t + 1) * T],
                                               A("ident", D)[:, 0:D])
                last.then_inc(xv_full, 1)

            pe.wait_ge(xv_done, B)
            pe.wait_ge(qk_lo, 8 * B)

            def max_tile(i, s, t, c, first=False):
                if t == 0 and c == 0:
                    pe.wait_ge(slot_in[s], 96 * (i + 1))
                if not first:
                    pe.wait_ge(max_done, 14 * (4 * i + s) + 2 * t + c - 1)
                mm(P[0:T, c, 0:HALF], Qs[0:96, s, t * T:(t + 1) * T], Ks[0:96, s, c * HALF:(c + 1) * HALF]).then_inc(max_full, 1)

            def max_turn(i, s):
                pe.wait_ge(mhl_ready, 4 * i + s + 1)
                nc.tensor.transpose(P[0:2 * NT, 7, 0:T], mhl[:, :].bitcast(F32), Bt("ident", T)[:, 0:T]).then_inc(turn_full, 1)

            def score_tile(i, s, u, p, first):
                k = 7 * (4 * i + s) + u
                if u == 0:
                    pe.wait_ge(mrow_in[s], 16 * (i + 1))
                if not first:
                    pe.wait_ge(exp_done, k - 1)
                for c in range(2):
                    last = mm(P[0:T, 2 + 2 * p + c, 0:HALF], Ks[:, s, u * T:(u + 1) * T], Qs[:, s, c * HALF:(c + 1) * HALF])
                last.then_inc(st_full, 1)

            def context_tile(i, s, u, p, first):
                n = 4 * i + s
                if u == 0:
                    pe.wait_ge(value_in[s], 32 * (i + 1))
                    if not first:
                        pe.wait_ge(ctx_done, n)
                pe.wait_ge(exp_done, 7 * n + u + 1)
                tiles = PT[:, p, :].rearrange("p (t c) -> p t c", c=T)
                xv = XVs[:, s, u * D:(u + 1) * D]
                mm(P[0:D, 6, 0:4 * T], xv, tiles[:, 0:7:2, :], u == 0, u == NT - 1)
                mm(P[D:128, 6, 0:3 * T], xv, tiles[:, 1:6:2, :], u == 0, u == NT - 1).then_inc(av_done, 1)

            def head_out(i, s, first):
                n = 4 * i + s
                pe.wait_ge(ctx_done, n + 1)
                if not first:
                    pe.wait_ge(proj_done, n)
                if not (isinstance(n, int) and n > NH - 3):
                    pe.wait_ge(turn_done, n + 3)
                for k in range(4):
                    w = 2 * D + 2 if k < 3 else D + 1
                    last = mm(P[0:T, 7, k * 130:k * 130 + w], CT[:, k * T:(k + 1) * T], VBs[:, s, 0:w])
                last.then_inc(proj_full, 1)

            def four_heads(i, first=False, final=False):
                for s in range(4):
                    for u in range(NT):
                        step = 7 * s + u
                        ahead = step + LEAD
                        more = not (final and ahead >= 28)
                        tile = (i + ahead // 28, ahead // 7 % 4, ahead % 7)
                        score_tile(i, s, u, step % 2, first and step < 2)
                        if more:
                            max_tile(*tile, 0)
                        if u == TURN and not (final and s == 3):
                            if not (first and s < 2):
                                pe.wait_ge(proj_done, 4 * i + s - 1)
                            max_turn(i + (s == 3), (s + 1) % 4)
                        if not (first and step == 0):
                            before = step - 1
                            context_tile(i if before >= 0 else i - 1, before // 7 % 4, before % 7, before % 2,
                                         first and before < 7)
                        if u == 2 and not (first and s == 0):
                            head_out(i if s else i - 1, (s - 1) % 4, first and s == 1)
                        if more:
                            max_tile(*tile, 1)

            for j in range(LEAD):
                if j == 8:
                    max_turn(0, 0)
                for c in range(2):
                    max_tile(0, j // 7, j % 7, c, j == 0)
            four_heads(0, first=True)
            repeat(pe, 1, 7, {}, four_heads)
            four_heads(7, final=True)
            context_tile(7, 3, 6, 1, False)
            head_out(7, 3, False)

            ident = Bt("ident", T)
            for b in range(B):
                pe.wait_ge(summed, b + 1)
                for t in range(NT):
                    lo, hi = t * T, (t + 1) * T
                    rows = OUT[:, 2 * b, t * D:(t + 1) * D]
                    for h in range(2):
                        c0, c1 = max(lo, h * HALF), min(hi, (h + 1) * HALF)
                        if c1 > c0:
                            last = mm(P[h * D:(h + 1) * D, b, c0 - h * HALF:c1 - h * HALF], rows, ident[:, c0 - lo:c1 - lo])
                last.then_inc(join_full, 1)

            norm(MOE1, H, h_ready, lambda b: 2 * B + b + 1)
            logits(Bt("router"), E1, MOE1)

            def turn_out(b, part):
                pe.wait_ge(h_ready, 3 * B + b + 1)
                if b or part:
                    pe.wait_ge(out_copied, 2 * b + part)
                c0, c1 = OUT_PARTS[part]
                for c in range(c0, c1):
                    w = OJ * NP
                    last = nc.tensor.transpose(P[0:w, 4, (c - c0) * 128:(c - c0 + 1) * 128], Y[:, b, c * w:(c + 1) * w], Bt("ident"))
                last.then_inc(out_full, 1)

            mw2 = Bt("mw2").rearrange("p (e n) -> p e n", e=PAIRS)
            pe.wait_ge(w1_split, 1)
            for b in range(B):
                pe.wait_ge(xs1_in[b], 64)
                for p in range(PAIRS):
                    for h in range(2):
                        n = bank_of(("g1", b, p, h), HID1)
                        for part in range(2):
                            last = mm(bank(n), mw1r[:, part, p, :], xs1[:, b, h * HALF:(h + 1) * HALF], part == 0, part == 1)
                        last.then_inc(hid_full, 1)
            for b in range(B):
                if b == 0:
                    pe.wait_ge(gates_ready, 2)
                    pe.wait_ge(sel1_ready, 1)
                gate_rows(("wT1", b), gate1.wsp, b, HID1)
                if b >= 1:
                    turn_out(b - 1, 0)
                pe.wait_ge(hid_done, HID["wT1", b] + 1)
                rows = wT1[:, b % 2, :]
                at = B * E0 + E1 * b
                for e in range(2):
                    broadcast_gate(sel1r[:, 0, e, :], rows, at + e)
                if b >= 1:
                    pe.wait_ge(h_ready, 3 * B + b)
                mm(bank(7), Bt("mb2", 96), rows.bitcast(F32), True, False, skip_group_check=True)
                for e in range(2 * PAIRS):
                    if e + 2 < 2 * PAIRS:
                        broadcast_gate(sel1r[:, e // 2 + 1, e % 2, :], rows, at + e + 2)
                    if e == 2 and b >= 1:
                        turn_out(b - 1, 1)
                    pe.wait_ge(wbc_done, at + e + 1)
                    h = e % 2
                    last = mm(P[h * D:(h + 1) * D, 7, 0:HALF], mw2[:, e // 2, :], g1[:, b, e // 2, h, :], False,
                              e // 2 == PAIRS - 1, skip_group_check=True)
                last.then_inc(moe_full, 1)
            for part in range(2):
                turn_out(B - 1, part)

        @block.vector
        def _(vector):
            steps = Tally()

            def own():
                vector.wait_ge(vec_step, steps.now())

            nc.vector.memset(eps[:, :], EPS).then_inc(eps_set, 1)
            nc.vector.memset(VB[:, :, :], 0.0).then_inc(vec_step, steps.one())
            nc.vector.memset(XV[:, :, :, :], 1.0)

            def pixels(g, q):
                return X.rearrange("p c r w -> p (c r) w")[:, :, bass.ds((q // 2 * HCOL + 2 * g + q % 2) * PS, PS)]

            def stats(g, p):
                for q in range(4):
                    nc.vector.bn_stats(bst[:, p, q, :], pixels(g, q)).then_inc(vec_step, steps.one())

            def moments(g, p):
                for q in range(4):
                    last = nc.vector.bn_aggr(mv[:, p, q, :], bst[:, p, q, :])
                last.then_inc(stats_ready, 1)

            def apply(g, p):
                vector.wait_ge(sd_ready, g + 1)
                nc.vector.reciprocal(ri[:, p, :], sd[:, p, :]).then_inc(vec_step, steps.one())
                own()
                for q in range(4):
                    last = nc.vector.tensor_scalar(xn[:, p, q, :].rearrange("p (r w) -> p r w", w=PS), pixels(g, q),
                                                   mv[:, p, q, 0:1], ri[:, p, q:q + 1], ALU.subtract, ALU.mult)
                last.then_inc(xn_ready, 1)

            vector.wait_ge(pixels_in, 16 * B)
            stats(0, 0)
            own()
            moments(0, 0)
            stats(1, 1)
            apply(0, 0)
            moments(1, 1)

            def cycle(g, p):
                stats(g + 1, 1 - p)
                apply(g, p)
                moments(g + 1, 1 - p)

            def two(i):
                cycle(2 * i + 1, 1)
                cycle(2 * i + 2, 0)
            repeat(vector, 0, 2, {steps: 10}, two)
            cycle(5, 1)
            apply(6, 0)

            vector.wait_ge(wb_in, 32)
            vector.wait_ge(vo_full, 1)
            for h in range(2):
                part_ = slice(h * D, (h + 1) * D)
                at = h * (D + 1)
                nc.vector.tensor_copy(VB[part_, :, at:at + D], P[part_, 7, 0:HEADS * D].rearrange("p (e d) -> p e d", d=D))
                last = nc.vector.tensor_copy(VB[part_, :, at + D], wa[part_, COLS_A["e63"][0]:COLS_A["e63"][1]].broadcast_to([D, HEADS]))
            last.then_inc(vb_ready, 1)
            nc.vector.tensor_scalar(ycol[:, :], col("gn_w"), 0.0, col("gn_b"), ALU.mult, ALU.add).then_inc(vec_step, steps.one())
            own()
            nc.vector.tensor_scalar(woy[:, :], A("wo"), ycol[:, :], None, ALU.mult).then_inc(woy_ready, 1)
            nc.vector.tensor_copy(sel0r[:, :, :], A("sel0", 96).rearrange("p (e n) -> p e n", e=E0)).then_inc(sel0_ready, 1)

            def norm(S):
                for b in range(B):
                    vector.wait_ge(rstd_ready, 4 * S + b + 1)
                    ins = nc.vector.tensor_tensor(xhat[:, b, :], bank(b), rstd_buf(S)[:, b, :], ALU.mult)
                    if S == TOK2:
                        ins.then_inc(vec_step, steps.one())
                        own()
                        ins = nc.vector.tensor_scalar(xhat[:, b, :], xhat[:, b, :], col("ln2_g"), col("ln2_b"), ALU.mult, ALU.add)
                    ins.then_inc(normed, 1)

            norm(TOK2)
            norm(POOL3)
            norm(GATE)
            for b in range(B):
                vector.wait_ge(main_full, 3 * B + b + 1)
                nc.vector.scalar_tensor_tensor(H[:, b, :], bank(4 + b), col("abias"), H[:, b, :], ALU.add, ALU.add)\
                  .then_inc(h_ready, 1)
            norm(MOE0)

            def split_xhat(xhl, done):
                for b in range(B):
                    vector.wait_ge(normed, 4 * (MOE0 if done is split0 else MOE1) + b + 1)
                    nc.vector.tensor_copy(xhl[:, b, 0, :], xhat[:, b, :]).then_inc(vec_step, steps.one())
                    own()
                    nc.vector.tensor_tensor(xhl[:, b, 1, :], xhat[:, b, :], xhl[:, b, 0, :].bitcast(F32), ALU.subtract)\
                      .then_inc(done, 1)

            def split_weights(hi, lo, w):
                nc.vector.tensor_copy(hi, w).then_inc(vec_step, steps.one())
                own()
                return nc.vector.tensor_tensor(lo, w, hi.bitcast(F32), ALU.subtract)

            split_xhat(xhl0, split0)
            split_weights(ew1r[:, 0, :, :], ew1r[:, 1, :, :], A("ew1").rearrange("p (e n) -> p e n", e=E0)).then_inc(w0_split, 1)

            def tt(o, a, b_, op):
                nc.vector.tensor_tensor(o, a, b_, op).then_inc(vec_step, steps.one())
                own()

            def reduce(o, a, op):
                nc.vector.tensor_reduce(o, a, AX.X, op).then_inc(vec_step, steps.one())
                own()

            def gating(gate, E, bias, idx, pair_softmax, asked):
                N = B * NGT * 2
                wide = [GT, N, E]

                def over(r):
                    return r.unsqueeze(2).broadcast_to(wide)
                vector.wait_ge(logits_full, asked["logits"])
                lg = P[0:GT, 4, 0:N * E].rearrange("p (n e) -> p n e", e=E)
                if bias is not None:
                    tt(gate.a[:, :, :], lg, bias.unsqueeze(1).broadcast_to(wide), ALU.add)
                    lg = gate.a[:, :, :]
                reduce(gate.m[:, :], lg, ALU.max)
                nc.vector.tensor_tensor(gate.dif, lg, over(gate.m[:, :]), ALU.subtract).then_inc(expo_in, 1)
                vector.wait_ge(expo_out, asked["exp"])
                reduce(gate.m[:, :], gate.ex, ALU.add)
                nc.vector.reciprocal(gate.m[:, :], gate.m[:, :]).then_inc(vec_step, steps.one())
                own()
                tt(gate.p[:, :, :], gate.ex, over(gate.m[:, :]), ALU.mult)
                best = [gate.v1[:, :], gate.v2[:, :]]
                chosen = [gate.s1[:, :, :], gate.s2[:, :, :]]
                probs = gate.p[:, :, :]
                for r, s in zip(best, chosen):
                    reduce(r, probs, ALU.max)
                    tt(s, probs, over(r), ALU.is_equal)
                    tt(s, s, idx.unsqueeze(1).broadcast_to(wide), ALU.mult)
                    reduce(gate.m[:, :], s, ALU.max)
                    tt(s, s, over(gate.m[:, :]), ALU.is_equal)
                    if r is best[0]:
                        nc.vector.scalar_tensor_tensor(gate.a[:, :, :], s, -2.0, probs, ALU.mult, ALU.add)\
                          .then_inc(vec_step, steps.one())
                        own()
                        probs = gate.a[:, :, :]
                if pair_softmax:
                    nc.vector.tensor_tensor(gate.d21, gate.v2[:, :], gate.v1[:, :], ALU.subtract).then_inc(expo_in, 1)
                    vector.wait_ge(expo_out, asked["exp"] + 1)
                    nc.vector.tensor_scalar(gate.m[:, :], gate.e21, 1.0, None, ALU.add).then_inc(vec_step, steps.one())
                    own()
                    nc.vector.reciprocal(gate.v1[:, :], gate.m[:, :]).then_inc(vec_step, steps.one())
                    own()
                    tt(gate.v2[:, :], gate.e21, gate.v1[:, :], ALU.mult)
                else:
                    tt(gate.m[:, :], gate.v1[:, :], gate.v2[:, :], ALU.add)
                    nc.vector.tensor_scalar(gate.m[:, :], gate.m[:, :], 1e-12, None, ALU.max).then_inc(vec_step, steps.one())
                    own()
                    nc.vector.reciprocal(gate.m[:, :], gate.m[:, :]).then_inc(vec_step, steps.one())
                    own()
                    tt(gate.v1[:, :], gate.v1[:, :], gate.m[:, :], ALU.mult)
                    tt(gate.v2[:, :], gate.v2[:, :], gate.m[:, :], ALU.mult)
                tt(gate.s1[:, :, :], gate.s1[:, :, :], over(gate.v1[:, :]), ALU.mult)
                tt(gate.s2[:, :, :], gate.s2[:, :, :], over(gate.v2[:, :]), ALU.mult)
                tt(gate.p[:, :, :], gate.s1[:, :, :], gate.s2[:, :, :], ALU.add)
                w = gate.p.rearrange("p (n h) e -> p n (h e)", h=2)
                hi, lo = gate.wsp[:, :, 0:2 * E], gate.wsp[:, :, 32:32 + 2 * E]
                nc.vector.tensor_copy(hi, w).then_inc(vec_step, steps.one())
                own()
                nc.vector.tensor_tensor(lo, w, hi.bitcast(F32), ALU.subtract).then_inc(gates_ready, 1)

            nc.vector.memset(gate0.wsp[:, :, :].bitcast(F32), 0.0).then_inc(vec_step, steps.one())
            own()
            gating(gate0, E0, A("gb", GT)[:, 0:E0], A("idx0", GT), True, {"logits": 1, "exp": 1})

            def times_gate(n, buf):
                vector.wait_ge(wbc_full, n + 1)
                nc.vector.tensor_tensor(buf, bank(5 + n % 2), buf, ALU.mult).then_inc(wbc_done, 1)

            for b in range(B):
                for e in range(E0):
                    times_gate(E0 * b + e, h2[:, e, :])
                vector.wait_ge(moe_full, b + 1)
                nc.vector.scalar_tensor_tensor(H[:, b, :], bank(7), col("sb3"), H[:, b, :], ALU.add, ALU.add)\
                  .then_inc(h_ready, 1)

            norm(ATT)
            for n in range(8 * B):
                b, k = n // 8, n % 8
                cols = (slice(None), k // 4, 2 * b + k // 2 % 2, slice(k % 2 * HALF, (k % 2 + 1) * HALF))
                vector.wait_ge(qk_hi, n + 1)
                nc.vector.tensor_tensor(QKL[cols], bank(k % 4), QKH[cols].bitcast(F32), ALU.subtract).then_inc(qk_lo, 1)

            vector.wait_ge(xv_done, B)
            nc.vector.memset(P[D:128, 6, 3 * T:4 * T], 0.0)
            nc.vector.memset(Ks[96:98, :, :].bitcast(F32), 1.0).then_inc(slots_set, 1)

            def row_max(i, s, t, c):
                vector.wait_ge(max_full, 14 * (4 * i + s) + 2 * t + c + 1)
                nc.vector.tensor_reduce(mx[:, c, t:t + 1], bank(c)[0:T, :], AX.X, ALU.max).then_inc(max_done, 1)

            def minus_max(i, s):
                vector.wait_ge(max_done, 14 * (4 * i + s) + 14)
                nc.vector.tensor_tensor(mxf[:, :], mx[:, 0, :], mx[:, 1, :], ALU.max).then_inc(vec_step, steps.one())
                own()
                nc.vector.tensor_scalar(mhl[:, 0:NT], mxf[:, :], -1.0, None, ALU.mult).then_inc(vec_step, steps.one())
                own()
                nc.vector.scalar_tensor_tensor(mhl[:, NT:2 * NT], mxf[:, :], -1.0, mhl[:, 0:NT].bitcast(F32),
                                               ALU.mult, ALU.subtract).then_inc(mhl_ready, 1)

            def max_rows(i, s):
                vector.wait_ge(turn_full, 4 * i + s + 1)
                nc.vector.tensor_copy(mT[:, :], P[0:2 * NT, 7, 0:T]).then_inc(turn_done, 1)

            def divide(i, s):
                n = 4 * i + s
                vector.wait_ge(proj_full, n + 1)
                got = P[0:T, 7, 0:NT * (D + 1)].rearrange("p (t d) -> p t d", d=D + 1)
                nc.vector.reciprocal(zi[:, :], got[:, :, D]).then_inc(vec_step, steps.one())
                own()
                over = zi[:, :].unsqueeze(2).broadcast_to([T, NT, D])
                if s == 3:
                    vector.wait_ge(sums, 2 * i + 1)
                nc.vector.tensor_tensor(part[:, s % 3, :].rearrange("p (t d) -> p t d", d=D), got[:, :, 0:D], over,
                                        ALU.mult).then_inc(proj_done, 1)

            def group_sum(i):
                vector.wait_ge(sums, 2 * i + 2)
                vector.wait_ge(proj_done, 4 * i + 4)
                nc.vector.tensor_tensor(OUT[:, i, :], acc[:, 1, :], part[:, 0, :], ALU.add).then_inc(grouped, 1)

            def image_sum(b):
                vector.wait_ge(grouped, 2 * b + 2)
                nc.vector.tensor_tensor(OUT[:, 2 * b, :], OUT[:, 2 * b, :], OUT[:, 2 * b + 1, :], ALU.add).then_inc(summed, 1)

            def four_heads(i, first=False, final=False):
                for s in range(4):
                    for u in range(NT):
                        ahead = 7 * s + u + LEAD
                        more = not (final and ahead >= 28)
                        tile = (i + ahead // 28, ahead // 7 % 4, ahead % 7)
                        if more:
                            row_max(*tile, 0)
                        if u == TURN and not (final and s == 3):
                            max_rows(i + (s == 3), (s + 1) % 4)
                        if u == 3 and not (first and s == 0):
                            divide(i if s else i - 1, (s - 1) % 4)
                        if u == 4 and s == 0 and not first:
                            group_sum(i - 1)
                        if u == 5 and s < B - 1 and final:
                            image_sum(s)
                        if more:
                            row_max(*tile, 1)
                            if ahead % 7 == 6:
                                minus_max(i + ahead // 28, ahead // 7 % 4)

            for j in range(LEAD):
                if j in (7, 14):
                    minus_max(0, j // 7 - 1)
                if j == 8:
                    max_rows(0, 0)
                for c in range(2):
                    row_max(0, j // 7, j % 7, c)
            four_heads(0, first=True)
            repeat(vector, 1, 7, {steps: 4 * 3}, four_heads)
            four_heads(7, final=True)
            divide(7, 3)
            group_sum(7)
            image_sum(B - 1)

            for b in range(B):
                vector.wait_ge(join_full, b + 1)
                nc.vector.tensor_tensor(H[:, b, :], bank(b), H[:, b, :], ALU.add).then_inc(h_ready, 1)

            nc.vector.tensor_copy(sel1r[:, :, :, :], Bt("sel1", 96).rearrange("p (e h n) -> p e h n", e=PAIRS, h=2))\
              .then_inc(sel1_ready, 1)
            split_weights(mw1r[:, 0, :, :], mw1r[:, 1, :, :], Bt("mw1").rearrange("p (e n) -> p e n", e=PAIRS)).then_inc(w1_split, 1)
            nc.vector.memset(gate1.wsp[:, :, :].bitcast(F32), 0.0).then_inc(vec_step, steps.one())
            own()
            norm(MOE1)
            split_xhat(xhl1, split1)
            gating(gate1, E1, None, Bt("idx1", GT), False, {"logits": 2, "exp": 3})
            for b in range(B):
                for e in range(E1):
                    times_gate(B * E0 + E1 * b + e, g1[:, b, e // 2, e % 2, :])
                vector.wait_ge(moe_full, B + b + 1)
                tt(xhat[:, b, :], bank(7), xhat[:, b, :], ALU.add)
                def view(tile, order):
                    return tile[:, b, :].rearrange(order, c=OC, j=OJ)
                nc.vector.tensor_tensor(view(Y, "p (c j i) -> p c j i"), view(xhat, "p (j c i) -> p c j i"),
                                        view(H, "p (j c i) -> p c j i"), ALU.add).then_inc(h_ready, 1)


class Gate:

    def __init__(self, tile, E):
        N = B * NGT * 2
        wide = {n: tile(f"gate{E}_{n}", [GT, N, E]) for n in ("a", "dif", "ex", "p", "s1", "s2")}
        flat = {n: tile(f"gate{E}_{n}", [GT, N]) for n in ("m", "v1", "v2", "d21", "e21")}
        self.a, self.p, self.s1, self.s2 = wide["a"], wide["p"], wide["s1"], wide["s2"]
        self.dif, self.ex = wide["dif"][:, :, :], wide["ex"][:, :, :]
        self.m, self.v1, self.v2 = flat["m"], flat["v1"], flat["v2"]
        self.d21, self.e21 = flat["d21"][:, :], flat["e21"][:, :]
        self.wsp = tile(f"gate{E}_wsp", [GT, B * NGT, 96], F32R)


def kernel(**inputs):
    import concourse.bacc as bacc
    from concourse.bass_utils import run_bass_kernel_spmd as run

    a = {k: np.asarray(v) for k, v in inputs.items()}
    tok = {k[7:]: v for k, v in a.items() if k.startswith("L0_tok_")}
    gate = {k[8:]: v for k, v in a.items() if k.startswith("L0_attn_")}
    moe0 = {k[7:]: v for k, v in a.items() if k.startswith("L0_ffn_")}
    moe1 = {k[7:]: v for k, v in a.items() if k.startswith("L1_ffn_")}

    def table(cols, width, blocks):
        t = np.zeros((128, width), np.float32)
        for name, value in blocks.items():
            lo, hi = cols[name]
            t[0:value.shape[0], lo:hi] = value.reshape(value.shape[0], hi - lo)
        return t

    def diag(w):
        m = np.zeros((128, 2 * w.shape[1]), np.float32)
        m[0:D, 0:w.shape[1]] = w
        m[D:128, w.shape[1]:] = w
        return m

    def side(w):
        m = np.zeros((128, 2, w.shape[1]), np.float32)
        m[0:D, 0] = w
        m[D:128, 1] = w
        return m

    def stacked(w):
        return np.concatenate([w, w])

    def pair_selectors():
        m = np.zeros((96, PAIRS, 2, 128), np.float32)
        for p in range(PAIRS):
            for h in range(2):
                for e in range(2):
                    for r in (0, 32):
                        m[r + h * E1 + 2 * p + e, p, h, e * D:(e + 1) * D] = 1
        return m

    def twice(v):
        return np.concatenate([v, v]).reshape(128, 1)

    def features(v):
        v = v.reshape(PS * PS, C, -1).transpose(1, 0, 2).reshape(2, KF, -1)
        return v.transpose(1, 0, 2)

    def selectors(E):
        m = np.zeros((96, E, 128), np.float32)
        for e in range(E):
            for h in range(2):
                m[h * E + e, e, h * D:(h + 1) * D] = 1
                m[32 + h * E + e, e, h * D:(h + 1) * D] = 1
        return m

    def gate_biases(v):
        E = v.shape[0]
        m = np.zeros((96, 128), np.float32)
        for h in range(2):
            for r in (0, 32):
                m[r + h * E:r + (h + 1) * E, h * D:(h + 1) * D] = v
        return m

    fold = np.eye(D, dtype=np.float32)
    fold[D - 1, :] = -1
    fold[:, D - 1] = 0
    e63 = np.zeros((128, 1), np.float32)
    e63[[D - 1, 127]] = 1
    eye = np.eye(128, dtype=np.float32)
    ones = np.full((D, D), 1.0 / D, np.float32)
    qk = np.stack([np.stack([side(w[4 * g:4 * g + 4].reshape(4 * R, D).T) for g in range(2)], 1)
                   for w in (a["L1_attn_Q"], a["L1_attn_K"])], 1)
    common = {"ident": eye, "center": diag(np.eye(D, dtype=np.float32) - ones), "mean": diag(ones)}
    table_a = table(COLS_A, WIDTH_A, {"ident": eye,
        "w1": features(tok["W1"]), "wp1": diag(tok["Wp1"]), "wp2": diag(tok["Wp2"]),
        "wg": diag(gate["wg"]), "wo": diag(gate["wo"]), "sw1": diag(moe0["sW1"]),
        "ew1": stacked(moe0["eW1"].transpose(1, 0, 2)),
        "ew2": moe0["eW2"].transpose(1, 0, 2), "ew3": np.stack([diag(moe0["eW3"][e]) for e in range(E0)], 1),
        "sw2": side(moe0["sW2"]), "sw3": moe0["sW3"], "gw": diag(moe0["gW"]), "eb3": gate_biases(moe0["eb3"]),
        "sel0": selectors(E0), "gb": np.tile(moe0["gb"], (128, 2)),
        "idx0": np.tile(np.arange(E0, 0, -1, dtype=np.float32), (128, 1)),
        "qk": qk, "vo": a["L1_attn_VO"].transpose(1, 0, 2), "fold": fold, "e63": e63,
        "ln1_g": features(tok["ln1_g"]), "ln1_b": features(tok["ln1_b"]), "b1": twice(tok["b1"]),
        "ln2_g": twice(tok["ln2_g"]), "ln2_b": twice(tok["ln2_b"]), "bp1": twice(tok["bp1"]),
        "lnp_g": twice(tok["lnp_g"]), "lnp_b": twice(tok["lnp_b"]), "bp2": twice(tok["bp2"]),
        "gn_w": twice(gate["gn_weight"]), "gn_b": twice(gate["gn_bias"]), "abias": twice(gate["bias"]),
        "sb1": twice(moe0["sb1"]), "eb1": moe0["eb1"].T, "sb2": moe0["sb2"].reshape(128, 1),
        "eb2": np.concatenate([moe0["eb2"].T, moe0["eb2"].T]), "sb3": twice(moe0["sb3"])})
    table_b = table(COLS_B, WIDTH_B, common | {
        "router": diag(moe1["router_w"].T), "mw1": stacked(moe1["w1"].transpose(1, 0, 2)),
        "mw2": moe1["w2"].reshape(PAIRS, 128, D).transpose(1, 0, 2), "mb2": gate_biases(moe1["b2"]),
        "sel1": pair_selectors(), "idx1": np.tile(np.arange(E1, 0, -1, dtype=np.float32), (128, 1)),
        "mb1": moe1["b1"].reshape(PAIRS, 128).T})

    nc = bacc.Bacc("TRN2", target_bir_lowering=False, num_devices=1)
    arrays = {"x": np.ascontiguousarray(a["x"]), "table_a": table_a, "table_b": table_b}
    aps = [nc.dram_tensor(n, v.shape, F32, kind="ExternalInput").ap() for n, v in arrays.items()]
    result = nc.dram_tensor("out", (B, REP * TOK, D), F32, kind="ExternalOutput").ap()
    build(nc, *aps, result)
    r = run(nc, [arrays], core_ids=[0])
    return r.results[0]["out"]
```

```python
from contextlib import ExitStack

import numpy as np

import concourse.bass as bass
from concourse import mybir
from concourse.alu_op_type import AluOpType as ALU

F32 = mybir.dt.float32
F32R = mybir.dt.float32r
ACT = mybir.ActivationFunctionType
AX = mybir.AxisListType

B, C, IMG, PS = 4, 3, 224, 8
NP = IMG // PS
TOK = NP * NP
HALF = TOK // 2
HCOL = NP // 2
D = 64
FEAT = C * PS * PS
KF = FEAT // 2
REP = 3
EPS = 1e-5
T = 112
NT = TOK // T
HEADS, R = 8, 32
HG = 4
NH = B * HEADS
TURN = 1
LEAD = 15
E0, E1 = 4, 8
PAIRS = E1 // 2
GT = 98
NGT = HALF // GT
NQ = 2 * NGT
HROWS = 98
OJ, OC = 2, HCOL // 2
GROUPS = 7


class Tally:

    def __init__(self, start=0):
        self.n, self.reg = start, 0

    def one(self):
        self.n += 1
        return 1

    def now(self):
        return self.reg + self.n

    def next(self):
        return self.reg + self.n + 1


def repeat(engine, start, stop, per, body):
    before = {t: t.n for t in per}
    with engine.Fori(start, stop) as i:
        for t, k in per.items():
            t.reg = (i - start) * k if start else i * k
        body(i)
        for t, k in per.items():
            assert t.n - before[t] == k, (t.n - before[t], k)
    for t, k in per.items():
        t.n, t.reg = before[t] + k * (stop - start), 0


TABLE_A = [("ident", 128), ("w1_t", FEAT), ("c64", D), ("ln1_g", 2), ("ln1_b", 2), ("b1", 1),
           ("wp1_t", 128), ("wp2_t", 128), ("wo_t", 128), ("wp2", 128),
           ("wg", 128), ("wo", 128), ("sw1", 128), ("ew1", E0 * 128), ("ew2", E0 * D),
           ("ew3", E0 // 2 * D), ("sw2", 2 * 128), ("sw3", D), ("gw", R), ("eb3", 128),
           ("sel0", E0 * 128), ("gb", 2 * E0), ("idx0", E0),
           ("qk", 2 * 2 * 2 * 128), ("vo", HEADS * D), ("fold", D), ("e63", 1),
           ("ln2_g", 1), ("ln2_b", 1), ("bp1", 1),
           ("lnp_g", 1), ("lnp_b", 1), ("bp2", 1), ("gn_w", 1), ("gn_b", 1), ("abias", 1),
           ("sb1", 1), ("eb1", E0), ("sb2", 1), ("eb2", E0 // 2), ("sb3", 1)]
TABLE_B = [("ident", 128), ("center", 128), ("mean", 128), ("router", R), ("mw1", PAIRS * 128),
           ("mw2", PAIRS * D), ("mb2", 128), ("sel1", E1 * 128), ("idx1", E1), ("mb1", PAIRS)]


def columns(table):
    at, out = 0, {}
    for name, n in table:
        out[name] = (at, at + n)
        at += n
    return out, at


COLS_A, WIDTH_A = columns(TABLE_A)
EARLY_A = COLS_A["wp1_t"][0]
COLS_B, WIDTH_B = columns(TABLE_B)


def build(nc, x, table_a, table_b, out):
    ctx = ExitStack()
    with ctx:
        def sem(name):
            return ctx.enter_context(nc.semaphore(name))

        def sb(stack, name, shape, dt=F32):
            return stack.enter_context(nc.sbuf_tensor(name, shape, dt))

        wb = sb(ctx, "wb", [128, WIDTH_B])
        H = sb(ctx, "H", [128, B, HALF])
        xhat = sb(ctx, "xhat", [128, B, HALF])
        eps = sb(ctx, "eps", [128, 1])
        VB = sb(ctx, "VB", [128, HEADS, 2 * D + 2])
        XV = sb(ctx, "XV", [T, B, NT, D])

        reg1 = ExitStack()
        state = sb(reg1, "state", [128, B, HALF])
        act = sb(reg1, "act", [128, B, HALF])
        sel0r = sb(reg1, "sel0r", [96, E0 // 2, 2, 128], F32R)
        eb3r = sb(reg1, "eb3r", [96, 2, 128], F32R)
        woy = sb(reg1, "woy", [128, 128])
        w1c = sb(reg1, "w1c", [KF, 2, D])
        wp1c = sb(reg1, "wp1c", [128, 128])
        wp2c = sb(reg1, "wp2c", [128, 128])
        woyc = sb(reg1, "woyc", [128, 128])
        b1c = sb(reg1, "b1c", [128, 1])
        biasc = sb(reg1, "biasc", [128, 3])
        ycol = sb(reg1, "ycol", [128, 1])
        patches = ExitStack()
        X = sb(patches, "X", [T, C, PS, IMG])
        xn = sb(patches, "xn", [T, 2, 4, FEAT])
        xT = sb(patches, "xT", [KF, 2, 2, 4 * T])
        bst = sb(patches, "bst", [T, 2, 4, 6])
        mv = sb(patches, "mv", [T, 2, 4, 2])
        sd = sb(patches, "sd", [T, 2, 4])
        ri = sb(patches, "ri", [T, 2, 4])
        patches.close()
        xs0 = sb(reg1, "xs0", [128, B, TOK], F32R)
        ew1r = sb(reg1, "ew1r", [128, 2, E0, 128], F32R)
        h1 = sb(reg1, "h1", [128, E0, 2, HALF])
        h2 = sb(reg1, "h2", [128, E0 // 2, 2, HALF])
        s1 = sb(reg1, "s1", [128, HALF])
        s2 = sb(reg1, "s2", [128, 2, HALF])
        gate0 = Gate(lambda n, shape, dt=F32: sb(reg1, n, shape, dt), E0)
        wT0 = sb(reg1, "wT0", [96, HALF], F32R)
        reg1.close()
        reg1 = ExitStack()
        QKH = sb(reg1, "QKH", [128, 2, B * 2, TOK], F32R)
        QKL = sb(reg1, "QKL", [128, 2, B * 2, TOK], F32R)

        reg2 = ExitStack()
        wa = sb(reg2, "wa", [128, WIDTH_A])
        XF = sb(reg2, "XF", [D, B, TOK])
        sq = sb(reg2, "sq", [128, B, HALF])
        rs = sb(reg2, "rs", [128, B, HALF])
        reg2.close()
        reg2 = ExitStack()
        XVs = sb(reg2, "XVs", [T, 4, NT * D])
        VBs = sb(reg2, "VBs", [128, 4, 2 * D + 2])
        PT = sb(reg2, "PT", [T, 2, TOK])
        CT = sb(reg2, "CT", [128, HALF])
        mx = sb(reg2, "mx", [T, 2, 2, NT])
        mxf = sb(reg2, "mxf", [T, NT])
        mhl = sb(reg2, "mhl", [T, 2 * NT], F32R)
        mT = sb(reg2, "mT", [2 * NT, T], F32R)
        zi = sb(reg2, "zi", [GT, NQ])
        part = sb(reg2, "part", [GT, 3, NQ * D])
        acc = sb(reg2, "acc", [GT, 2, NQ * D])
        OUT = sb(reg2, "OUT", [GT, 2 * B, NQ * D])
        Qs = sb(reg2, "Qs", [HROWS, 4, TOK], F32R)
        Ks = sb(reg2, "Ks", [HROWS, 4, TOK], F32R)
        reg2.close()
        reg1.close()

        reg1 = ExitStack()
        sqm = sb(reg1, "sqm", [128, B, HALF])
        rsm = sb(reg1, "rsm", [128, B, HALF])
        wT1 = sb(reg1, "wT1", [96, B, HALF], F32R)
        mb2r = sb(reg1, "mb2r", [96, 2, 128], F32R)
        sel1r = sb(reg1, "sel1r", [96, PAIRS, 2, 128], F32R)
        mw1r = sb(reg1, "mw1r", [128, 2, PAIRS, 128], F32R)
        gate1 = Gate(lambda n, shape, dt=F32: sb(reg1, n, shape, dt), E1)
        xs1 = sb(reg1, "xs1", [128, B, TOK], F32R)
        g1 = sb(reg1, "g1", [128, B, PAIRS, 2, HALF])
        Y = sb(reg1, "Y", [128, B, HALF])
        OT = sb(reg1, "OT", [OJ * NP, B, 2, OC * D])
        reg1.close()

        row_store = [nc.dram_tensor(f"row_store{n}", (2, TOK), F32, kind="Internal").ap() for n in range(4)]
        P = ctx.enter_context(nc.psum_tensor("P", [128, 8, 512], F32))

        def bank(n, w=HALF):
            return P[:, n, 0:w]

        def A(name, rows=128):
            lo, hi = COLS_A[name]
            return wa[0:rows, lo:hi]

        def Bt(name, rows=128):
            lo, hi = COLS_B[name]
            return wb[0:rows, lo:hi]

        def col(name, n=0, rows=128):
            lo = COLS_A[name][0] + n
            return wa[0:rows, lo:lo + 1]

        def square_buf(S):
            return sqm if S == 5 else sq

        def rstd_buf(S):
            return rsm if S == 5 else rs

        TOK2, POOL3, GATE, MOE0, ATT, MOE1 = range(6)

        pixels_in, wa_in, wb_in = sem("pixels_in"), sem("wa_in"), sem("wb_in")
        xf_in = [sem(f"xf_in{b}") for b in range(B)]
        vec_step, act_step = sem("vec_step"), sem("act_step")
        split0, split1, high_done, w0_split, w1_split = sem("split0"), sem("split1"), sem("high_done"), sem("w0_split"), sem("w1_split")
        w1_full, w1_ready, wp1_full, wp1_ready = sem("w1_full"), sem("w1_ready"), sem("wp1_full"), sem("wp1_ready")
        eps_set, woy_ready, sel0_ready, sel1_ready = sem("eps_set"), sem("woy_ready"), sem("sel0_ready"), sem("sel1_ready")
        stats_ready, sd_ready, xn_ready = sem("stats_ready"), sem("sd_ready"), sem("xn_ready")
        turned, xT_ready, patch_full, t0_done = sem("turned"), sem("xT_ready"), sem("patch_full"), sem("t0_done")
        vo_full, vb_ready = sem("vo_full"), sem("vb_ready")
        squared_vec = sem("squared_vec")
        centred, squared, var_full, rstd_ready, normed = (sem("centred"), sem("squared"), sem("var_full"),
                                                          sem("rstd_ready"), sem("normed"))
        main_full, silu_ready, h0_ready = sem("main_full"), sem("silu_ready"), sem("h0_ready")
        h_ready = sem("h_ready")
        rows_cleared = sem("rows_cleared")
        logits_out, logits_turned = sem("logits_out"), sem("logits_turned")
        logits_full, expo_in, expo_out, gates_ready = (sem("logits_full"), sem("expo_in"), sem("expo_out"),
                                                       sem("gates_ready"))
        hid_full, hid_done = sem("hid_full"), sem("hid_done")
        wbc_full, wbc_done, moe_full = sem("wbc_full"), sem("wbc_done"), sem("moe_full")
        qk_full, qk_hi, qk_lo = sem("qk_full"), sem("qk_hi"), sem("qk_lo")
        xv_full, xv_done, slots_set = sem("xv_full"), sem("xv_done"), sem("slots_set")
        slot_in = [sem(f"slot_in{s}") for s in range(4)]
        value_in = [sem(f"value_in{s}") for s in range(4)]
        mrow_in = [sem(f"mrow_in{s}") for s in range(4)]
        rows_out = sem("rows_out")
        max_full, max_done, mhl_ready = sem("max_full"), sem("max_done"), sem("mhl_ready")
        turn_full, turn_done = sem("turn_full"), sem("turn_done")
        st_full, exp_done, av_done, ctx_done = sem("st_full"), sem("exp_done"), sem("av_done"), sem("ctx_done")
        proj_full, proj_done, block_done = sem("proj_full"), sem("proj_done"), sem("block_done")
        sums, grouped, summed, join_full = sem("sums"), sem("grouped"), sem("summed"), sem("join_full")
        stored = [sem(f"stored{b}") for b in range(B)]

        block = ctx.enter_context(nc.Block())
        LEAD_BANKS = (0, 1, 6)
        MOE1_BANKS = (7, 3)
        OUT_PARTS = ((0, 4), (4, OC))

        def hid_index():
            index, n = {}, 0
            for b in range(B + 1):
                if b >= 1:
                    for p in range(E0 // 2):
                        for h in range(2):
                            index["l2", b - 1, p, h] = n
                            n += 1
                    for h in range(2):
                        index["s2", b - 1, h] = n
                        n += 1
                    index["wT", b - 1] = n
                    n += 1
                if b < B:
                    index["s1", b] = n
                    n += 1
                    for e in range(E0):
                        for h in range(2):
                            index["l1", b, e, h] = n
                            n += 1
            base = n
            order = [("g1", c, p, h) for c in range(3) for p in range(PAIRS) for h in range(2)]
            order += [("wT1", b) for b in range(B)] + [("g1", 3, p, h) for p in range(PAIRS) for h in range(2)]
            order += [("out", b, part) for b in range(B) for part in range(2)]
            for n, key in enumerate(order):
                index[key] = base + n
            return index, base

        HID, HID1 = hid_index()

        def ring(k):
            return (k % 4, 4) if k < HID1 else ((k - HID1) % 3, 3)

        def wbc_banks(n):
            return (0, (5, 6)) if n < B * E0 else (B * E0, (4, 5, 6))

        def wait_centred(engine, S, b):
            if S == TOK2:
                engine.wait_ge(t0_done, GROUPS)
            elif S == POOL3:
                engine.wait_ge(main_full, b + 1)
            else:
                engine.wait_ge(centred, 4 * (S - GATE) + b + 1)

        def bias_of(S):
            return biasc[:, S - POOL3:S - POOL3 + 1] if S in (POOL3, GATE, MOE0) else None

        def rows_bank(S, b):
            return bank(4 + b if S == MOE0 else b)

        def var_bank(S, b):
            return bank(b if S == MOE0 else 4 + b)

        @block.sync
        def _(sync):
            for b in range(B):
                sync.dma_start(X[NP * b:NP * (b + 1), :, :, :].rearrange("i c p w -> i c (p w)"),
                               x[b].rearrange("c (i p) w -> i c (p w)", p=PS)).then_inc(pixels_in, 16)
            sync.wait_ge(pixels_in, 16 * B)
            sync.dma_start(wa[:, EARLY_A:WIDTH_A], table_a[:, EARLY_A:WIDTH_A]).then_inc(wb_in, 16)
            sync.dma_start(wb[:, :], table_b).then_inc(wb_in, 16)
            for b in range(B):
                sync.wait_ge(normed, 4 * ATT + b + 1)
                for h in range(2):
                    sync.dma_start(XF[:, b, h * HALF:(h + 1) * HALF],
                                   xhat[h * D:(h + 1) * D, b, :]).then_inc(xf_in[b], 16)

            def fill_stacks(i, s):
                rows = slice(s * R, (s + 1) * R)
                for dst, src in ((Qs[0:R, s, :], QKH[rows, 0, i, :]), (Qs[R:2 * R, s, :], QKH[rows, 0, i, :]),
                                 (Qs[2 * R:3 * R, s, :], QKL[rows, 0, i, :]),
                                 (Ks[0:R, s, :], QKH[rows, 1, i, :]), (Ks[R:2 * R, s, :], QKL[rows, 1, i, :]),
                                 (Ks[2 * R:3 * R, s, :], QKH[rows, 1, i, :])):
                    sync.dma_start(dst.bitcast(F32), src.bitcast(F32)).then_inc(slot_in[s], 16)

            def fill_values(b, group, s):
                sync.dma_start(XVs[:, s, :], XV[:, b, :, :].rearrange("p t d -> p (t d)")).then_inc(value_in[s], 16)
                sync.dma_start(VBs[:, s, :], VB[:, group * 4 + s, :]).then_inc(value_in[s], 16)

            def rows_to_store(i, s):
                sync.wait_ge(turn_done, 4 * i + s + 1)
                sync.dma_start(row_store[s].rearrange("r (t c) -> (r t) c", c=T), mT[:, :].bitcast(F32)).then_inc(rows_out, 16)

            def rows_to_stack(i, s):
                sync.wait_ge(rows_out, 16 * (4 * i + s) + 16)
                sync.dma_start(Qs[96:98, s, :].bitcast(F32), row_store[s]).then_inc(mrow_in[s], 16)

            sync.wait_ge(qk_lo, 8)
            for s in range(4):
                fill_stacks(0, s)
            sync.wait_ge(slots_set, 1)
            for s in range(4):
                fill_values(0, 0, s)
            for s in range(2):
                rows_to_store(0, s)
                rows_to_stack(0, s)

            def heads(i, b, group):
                for s in range(4):
                    on = (i + (s >= 2), (s + 2) % 4)
                    rows_to_store(*on)
                    sync.wait_ge(st_full, 7 * (4 * i + s) + 7)
                    fill_stacks(i + 1, s)
                    rows_to_stack(*on)
                    sync.wait_ge(proj_full, 4 * i + s + 1)
                    fill_values(b, group, s)

            def image(b):
                heads(2 * b, b, 1)
                heads(2 * b + 1, b + 1, 0)
            repeat(sync, 0, B - 1, {}, image)
            heads(2 * B - 2, B - 1, 1)
            for s in range(2, 4):
                rows_to_store(2 * B - 1, s)
                rows_to_stack(2 * B - 1, s)
            rows = out.rearrange("b (k i h j cd) d -> b i k h j (cd d)", k=REP, i=NP, h=2, j=OJ)
            for b in range(B):
                sync.wait_ge(hid_done, HID["out", b, 1] + 1)
                for j in range(OJ):
                    for k in range(REP):
                        sync.dma_start(rows[b, :, k, :, j, :], OT[j * NP:(j + 1) * NP, b, :, :]).then_inc(stored[b], 16)
            for b in range(B):
                sync.wait_ge(stored[b], 16 * REP * OJ)

        @block.scalar
        def _(scalar):
            scalar.dma_start(wa[:, 0:EARLY_A], table_a[:, 0:EARLY_A]).then_inc(wa_in, 16)
            steps = Tally()

            def deviations(g, p):
                scalar.wait_ge(stats_ready, g + 1)
                nc.scalar.activation(sd[:, p, :], mv[:, p, :, 1], ACT.Sqrt, bias=eps[0:T, :]).then_inc(sd_ready, 1)

            def turned_patches(g, p):
                scalar.wait_ge(turned, g + 1)
                for k in range(2):
                    nc.scalar.activation(xT[:, p, k, :], P[0:KF, 2 * p + k, 0:4 * T], ACT.Identity,
                                         bias=col("ln1_b", k, KF), scale=col("ln1_g", k, KF)).then_inc(xT_ready, 1)

            def tokens_out(g, p):
                scalar.wait_ge(patch_full, g + 1)
                nc.scalar.activation(
                    state.rearrange("p b (j i) -> p b j i", i=NP)[:, :, bass.ds(2 * g, 2), :].rearrange("p b j i -> p j b i"),
                    P[:, 4 + p, 0:2 * T].rearrange("p (j b i) -> p j b i", j=2, b=B), ACT.Identity,
                    bias=b1c[:, :]).then_inc(t0_done, 1)

            scalar.wait_ge(eps_set, 1)
            scalar.wait_ge(wa_in, 16)
            scalar.wait_ge(w1_ready, 1)
            deviations(0, 0)
            deviations(1, 1)
            turned_patches(0, 0)

            def cycle(g, p):
                deviations(g + 1, 1 - p)
                turned_patches(g, p)
                tokens_out(g - 1, 1 - p)

            def two(i):
                cycle(2 * i + 1, 1)
                cycle(2 * i + 2, 0)
            repeat(scalar, 0, 2, {}, two)
            cycle(5, 1)
            turned_patches(6, 0)
            tokens_out(5, 1)
            tokens_out(6, 0)

            def norm(S):
                for b in range(2):
                    wait_centred(scalar, S, b)
                    nc.scalar.activation(square_buf(S)[:, b, :], state[:, b, :] if S == TOK2 else rows_bank(S, b), ACT.Square,
                                         **({} if bias_of(S) is None else dict(bias=bias_of(S)))).then_inc(squared, 1)
                for b in range(B):
                    scalar.wait_ge(var_full, 4 * S + b + 1)
                    nc.scalar.activation(rstd_buf(S)[:, b, :], var_bank(S, b), ACT.Ln, bias=eps[:, :]).then_inc(act_step, steps.one())
                for b in range(B):
                    scalar.wait_ge(act_step, steps.now() - (B - 1 - b))
                    nc.scalar.activation(rstd_buf(S)[:, b, :], rstd_buf(S)[:, b, :], ACT.Exp, scale=-0.5).then_inc(rstd_ready, 1)

            norm(TOK2)
            norm(POOL3)
            for b in range(B):
                scalar.wait_ge(normed, 4 * POOL3 + b + 1)
                nc.scalar.activation(act[:, b, :], xhat[:, b, :], ACT.Silu, bias=col("lnp_b"), scale=col("lnp_g"))\
                  .then_inc(silu_ready, 1)
            norm(GATE)
            for b in range(B):
                scalar.wait_ge(main_full, 2 * B + b + 1)
                nc.scalar.activation(state[:, b, :], bank(b), ACT.Silu).then_inc(silu_ready, 1)
            norm(MOE0)

            def high_parts(S, xs):
                for b in range(B):
                    scalar.wait_ge(normed, 4 * S + b + 1)
                    for h in range(2):
                        nc.scalar.activation(xs[0:D, b, h * HALF:(h + 1) * HALF], xhat[h * D:(h + 1) * D, b, :], ACT.Copy)\
                          .then_inc(high_done, 1)

            high_parts(MOE0, xs0)

            def exponents(gate, n):
                src, dst = (gate.dif, gate.ex) if n == 0 else (gate.d21, gate.e21)
                nc.scalar.activation(dst, src, ACT.Exp).then_inc(expo_out, 1)

            def hidden(key, dst, func, bias=None, rows=128, width=HALF):
                k = HID[key]
                scalar.wait_ge(hid_full, k + 1)
                nc.scalar.activation(dst, P[0:rows, ring(k)[0], 0:width], func, **({} if bias is None else dict(bias=bias)))\
                  .then_inc(hid_done, 1)

            for b in range(B + 1):
                if b >= 1:
                    c = b - 1
                    if c >= 1:
                        scalar.wait_ge(moe_full, c)
                    if c == 0:
                        scalar.wait_ge(expo_in, 2)
                        exponents(gate0, 1)
                    for p in range(E0 // 2):
                        for h in range(2):
                            hidden(("l2", c, p, h), h2[:, p, h, :], ACT.Relu, col("eb2", p))
                    for h in range(2):
                        hidden(("s2", c, h), s2[:, h, :], ACT.Relu, col("sb2"))
                    hidden(("wT", c), wT0[:, :], ACT.Copy, rows=96)
                if b < B:
                    hidden(("s1", b), s1[:, :], ACT.Relu, col("sb1"))
                    if b == 0:
                        hidden(("l1", 0, 0, 0), h1[:, 0, 0, :], ACT.Relu, col("eb1", 0))
                        scalar.wait_ge(expo_in, 1)
                        exponents(gate0, 0)
                    for e in range(E0):
                        for h in range(2):
                            if b or e or h:
                                hidden(("l1", b, e, h), h1[:, e, h, :], ACT.Relu, col("eb1", e))

            norm(ATT)
            for b in range(B):
                for k in range(8):
                    qk, group, h = k // 4, k // 2 % 2, k % 2
                    scalar.wait_ge(qk_full, 8 * b + k + 1)
                    nc.scalar.activation(QKH[:, qk, 2 * b + group, h * HALF:(h + 1) * HALF], bank(4 + k % 4), ACT.Copy)\
                      .then_inc(qk_hi, 1)
                scalar.wait_ge(xv_full, b + 1)
                nc.scalar.activation(XV[:, b, :, 0:D - 1], P[0:T, b, 0:NT * D].rearrange("p (t d) -> p t d", d=D)[:, :, 0:D - 1],
                                     ACT.Copy).then_inc(xv_done, 1)

            scalar.wait_ge(slots_set, 1)

            def exp_tile(k, p, first):
                scalar.wait_ge(st_full, k + 1)
                if not first:
                    scalar.wait_ge(av_done, k - 1)
                nc.scalar.activation(PT[:, p, :].rearrange("p (c n) -> p c n", c=2), P[0:T, 2 + 2 * p:4 + 2 * p, 0:HALF],
                                     ACT.Exp, scale=float(D) ** -0.5).then_inc(exp_done, 1)

            def context_out(n, first):
                scalar.wait_ge(av_done, 7 * n + 7)
                if not first:
                    scalar.wait_ge(proj_full, n)
                nc.scalar.activation(CT[:, :], bank(6), ACT.Copy).then_inc(ctx_done, 1)

            def four_heads(i, first=False):
                for s in range(4):
                    for u in range(NT):
                        n, step = 4 * i + s, 7 * s + u
                        exp_tile(7 * n + u, step % 2, first and step < 2)
                        if u == 0 and not (first and s == 0):
                            context_out(n - 1, first and s == 1)
                        if u == 6 and s == 0 and not first:
                            group_out(i - 1)

            def group_out(i):
                scalar.wait_ge(sums, 3 * i + 3)
                nc.scalar.activation(OUT[:, i, :], acc[:, 0, :], ACT.Copy).then_inc(grouped, 1)

            four_heads(0, True)
            repeat(scalar, 1, 8, {}, four_heads)
            context_out(NH - 1, False)

            norm(MOE1)
            high_parts(MOE1, xs1)
            scalar.wait_ge(expo_in, 3)
            exponents(gate1, 0)

            def rows_out_of(b, part):
                c0, c1 = OUT_PARTS[part]
                k = HID["out", b, part]
                scalar.wait_ge(hid_full, k + 1)
                nc.scalar.activation(OT[:, b, :, :].rearrange("p h (c d) -> p h c d", d=D)[:, :, c0:c1, :],
                                     P[0:OJ * NP, ring(k)[0], 0:(c1 - c0) * 128].rearrange("p (c h d) -> p h c d", h=2, d=D),
                                     ACT.Copy).then_inc(hid_done, 1)

            def gelus(b):
                for p in range(PAIRS):
                    for h in range(2):
                        hidden(("g1", b, p, h), g1[:, b, p, h, :], ACT.Gelu, Bt("mb1")[:, p:p + 1])

            for b in range(3):
                gelus(b)
            for b in range(B):
                hidden(("wT1", b), wT1[:, b, :], ACT.Copy, rows=96)
            gelus(3)
            for b in range(B):
                for part in range(2):
                    rows_out_of(b, part)

        @block.gpsimd
        def _(pool):
            def heads(i, first=False, final=False):
                for s, (dst, a, b_) in enumerate(((acc[:, 0, :], part[:, 0, :], part[:, 1, :]),
                                                  (acc[:, 1, :], acc[:, 0, :], part[:, 2, :]),
                                                  (acc[:, 0, :], acc[:, 1, :], part[:, 0, :]))[0:2 if final else 3], 1):
                    pool.wait_ge(proj_done, 4 * i + s + 1)
                    if s > 1:
                        pool.wait_ge(sums, 3 * i + s - 1)
                    elif not first:
                        pool.wait_ge(grouped, i)
                    nc.gpsimd.tensor_tensor(dst, a, b_, ALU.add).then_inc(sums, 1)
            heads(0, True)
            repeat(pool, 1, 2 * B - 1, {}, heads)
            heads(2 * B - 1, final=True)
            pool.wait_ge(join_full, 1)
            nc.gpsimd.memset(gate1.wsp[:, :, :].bitcast(F32), 0.0).then_inc(rows_cleared, 1)

        @block.tensor
        def _(pe):
            def mm(dst, lhsT, rhs, start=True, stop=True, **more):
                return nc.tensor.matmul(dst, lhsT, rhs, start=start, stop=stop, **more)

            pe.wait_ge(wa_in, 16)
            w1_t = A("w1_t", D)
            for k in range(2):
                mm(P[0:KF, 7, k * D:(k + 1) * D], w1_t[:, k * KF:(k + 1) * KF], A("c64", D))
            for h in range(2):
                last = mm(P[h * D:(h + 1) * D, 7, FEAT:FEAT + 1], A("c64", D), A("b1", D))
            last.then_inc(w1_full, 1)

            def turn(g, p):
                pe.wait_ge(xn_ready, g + 1)
                for q in range(4):
                    for k in range(2):
                        last = nc.tensor.transpose(P[0:KF, 2 * p + k, q * T:(q + 1) * T], xn[:, p, q, k * KF:(k + 1) * KF],
                                                   A("ident", T)[:, 0:T])
                last.then_inc(turned, 1)

            def project(g, p):
                pe.wait_ge(xT_ready, 2 * g + 2)
                for k in range(2):
                    for h in range(2):
                        last = mm(P[h * D:(h + 1) * D, 4 + p, 0:2 * T], w1c[:, k, :], xT[:, p, k, 2 * T * h:2 * T * (h + 1)],
                                  k == 0, k == 1)
                last.then_inc(patch_full, 1)

            turn(0, 0)
            pe.wait_ge(w1_ready, 1)

            def two(i):
                turn(2 * i + 1, 1)
                project(2 * i, 0)
                turn(2 * i + 2, 0)
                project(2 * i + 1, 1)
            repeat(pe, 0, 3, {}, two)
            project(6, 0)

            def norm(S, source=None, count=None):
                if source is not None:
                    for b in range(B):
                        pe.wait_ge(source, count(b))
                        mm(bank(b), Bt("center"), H[:, b, :]).then_inc(centred, 1)
                for b in range(B):
                    if b < 2:
                        pe.wait_ge(squared, 2 * S + b + 1)
                    else:
                        pe.wait_ge(squared_vec, 2 * S + b - 1)
                    mm(var_bank(S, b), Bt("mean"), square_buf(S)[:, b, :]).then_inc(var_full, 1)

            pe.wait_ge(wb_in, 32)
            for h in range(2):
                last = mm(P[h * D:(h + 1) * D, 0, 0:HEADS * D], A("fold", D), A("vo", D))
            last.then_inc(vo_full, 1)
            mm(P[:, 1, 0:128], A("wp1_t"), Bt("center"))
            mm(P[:, 2, 0:128], A("wp2_t"), Bt("center"))
            mm(P[:, 2, 128:256], A("wo_t"), Bt("center"))
            for n, name in enumerate(("bp1", "bp2", "abias")):
                last = mm(P[:, 1, 128 + n:129 + n], Bt("center"), col(name))
            last.then_inc(wp1_full, 1)
            norm(TOK2)
            pe.wait_ge(vb_ready, 1)
            pe.wait_ge(wp1_ready, 1)
            pe.wait_ge(woy_ready, 1)
            for b in range(B):
                pe.wait_ge(normed, 4 * TOK2 + b + 1)
                mm(bank(b), wp1c[:, :], xhat[:, b, :]).then_inc(main_full, 1)
            norm(POOL3)
            for b in range(B):
                pe.wait_ge(silu_ready, b + 1)
                mm(bank(b), wp2c[:, :], act[:, b, :]).then_inc(centred, 1)
            norm(GATE)
            for b in range(B):
                pe.wait_ge(act_step, 4 * GATE + b + 1)
                mm(bank(4 + b), A("wp2"), act[:, b, :]).then_inc(main_full, 1)
            for b in range(B):
                pe.wait_ge(normed, 4 * GATE + b + 1)
                mm(bank(b), A("wg"), xhat[:, b, :]).then_inc(main_full, 1)
            for b in range(B):
                pe.wait_ge(h0_ready, b + 1)
                mm(bank(4 + b), Bt("center"), H[:, b, :], True, False)
            for b in range(B):
                pe.wait_ge(silu_ready, B + b + 1)
                mm(bank(4 + b), woyc[:, :], state[:, b, :], False, True).then_inc(centred, 1)
            norm(MOE0)
            for b in range(B):
                pe.wait_ge(act_step, 4 * MOE0 + b + 1)
                mm(bank(b), woy[:, :], state[:, b, :]).then_inc(main_full, 1)

            def logits(weights, gate, S):
                for b in range(B):
                    pe.wait_ge(normed, 4 * S + b + 1)
                    last = mm(P[b * R:(b + 1) * R, 4, 0:HALF], weights, xhat[:, b, :])
                last.then_inc(logits_full, 1)
                pe.wait_ge(logits_out, 1 + (S == MOE1))
                for ct in range(NGT):
                    last = nc.tensor.transpose(P[0:GT, 4, ct * 128:(ct + 1) * 128], gate.lt[:, ct * GT:(ct + 1) * GT], Bt("ident"))
                last.then_inc(logits_turned, 1)

            def bank_of(key, first):
                k = HID[key]
                n, size = ring(k)
                if k - size >= first:
                    pe.wait_ge(hid_done, k - size + 1)
                elif k < size:
                    pe.wait_ge(h_ready, k + 1)
                return n

            def gate_rows(key, wsp, b, first):
                n = bank_of(key, first)
                for ct in range(NGT):
                    last = nc.tensor.transpose(P[0:96, n, ct * GT:(ct + 1) * GT], wsp[:, ct * B + b, :].bitcast(F32),
                                               Bt("ident", GT)[:, 0:GT])
                last.then_inc(hid_full, 1)

            ew2 = A("ew2").rearrange("p (e n) -> p e n", e=E0)
            ew3 = A("ew3").rearrange("p (e n) -> p e n", e=E0 // 2)
            sw2 = A("sw2").rearrange("p (h n) -> p h n", h=2)

            def first_layer(b):
                mm(bank(bank_of(("s1", b), 0)), A("sw1"), xhat[:, b, :]).then_inc(hid_full, 1)
                pe.wait_ge(split0, 2 * b + 2)
                if b == 0:
                    pe.wait_ge(w0_split, 1)
                for e in range(E0):
                    for h in range(2):
                        n = bank_of(("l1", b, e, h), 0)
                        for part in range(2):
                            last = mm(bank(n), ew1r[:, part, e, :], xs0[:, b, h * HALF:(h + 1) * HALF], part == 0, part == 1)
                        last.then_inc(hid_full, 1)

            def broadcast_gate(sel, rows, n):
                first, banks = wbc_banks(n)
                if n >= first + len(banks):
                    pe.wait_ge(wbc_done, n - len(banks) + 1)
                mm(bank(banks[(n - first) % len(banks)]), sel, rows).then_inc(wbc_full, 1)

            logits(A("gw"), gate0, MOE0)
            first_layer(0)
            for b in range(B):
                for p in range(E0 // 2):
                    pe.wait_ge(hid_done, HID["l1", b, 2 * p + 1, 1] + 1)
                    for h in range(2):
                        n = bank_of(("l2", b, p, h), 0)
                        for e in range(2):
                            last = mm(P[e * D:(e + 1) * D, n, 0:HALF], ew2[:, 2 * p + e, :], h1[:, 2 * p + e, h, :])
                        last.then_inc(hid_full, 1)
                pe.wait_ge(hid_done, HID["s1", b] + 1)
                for h in range(2):
                    mm(bank(bank_of(("s2", b, h), 0)), sw2[:, h, :], s1[:, :]).then_inc(hid_full, 1)
                if b == 0:
                    pe.wait_ge(gates_ready, 1)
                gate_rows(("wT", b), gate0.wsp, b, 0)
                if b + 1 < B:
                    first_layer(b + 1)
                pe.wait_ge(hid_done, HID["wT", b] + 1)
                if b == 0:
                    pe.wait_ge(sel0_ready, 1)
                for m in range(2):
                    broadcast_gate(sel0r[:, 0, m, :], wT0[:, :], E0 * b + m)
                if b >= 1:
                    pe.wait_ge(h_ready, B + b)
                for part in range(2):
                    mm(bank(7), eb3r[:, part, :], wT0[:, :], part == 0, False, skip_group_check=True)
                for h in range(2):
                    mm(P[h * D:(h + 1) * D, 7, 0:HALF], A("sw3"), s2[:, h, :], False, False, skip_group_check=True)
                for m in range(E0):
                    if m + 2 < E0:
                        broadcast_gate(sel0r[:, 1, m, :], wT0[:, :], E0 * b + m + 2)
                    pe.wait_ge(wbc_done, E0 * b + m + 1)
                    h = m % 2
                    last = mm(P[h * D:(h + 1) * D, 7, 0:HALF], ew3[:, m // 2, :], h2[:, m // 2, h, :], False,
                              m // 2 == E0 // 2 - 1, skip_group_check=True)
                last.then_inc(moe_full, 1)

            norm(ATT, h_ready, lambda b: B + b + 1)
            qk = A("qk").rearrange("p (q g h n) -> p q g h n", q=2, g=2, h=2)
            for b in range(B):
                pe.wait_ge(normed, 4 * ATT + b + 1)
                for k in range(8):
                    if 8 * b + k >= 4:
                        pe.wait_ge(qk_lo, 8 * b + k - 3)
                    mm(bank(4 + k % 4), qk[:, k // 4, k // 2 % 2, k % 2, :], xhat[:, b, :]).then_inc(qk_full, 1)
                pe.wait_ge(xf_in[b], 32)
                for t in range(NT):
                    last = nc.tensor.transpose(P[0:T, b, t * D:(t + 1) * D], XF[:, b, t * T:(t + 1) * T],
                                               A("ident", D)[:, 0:D])
                last.then_inc(xv_full, 1)

            pe.wait_ge(xv_done, B)
            pe.wait_ge(qk_lo, 8 * B)

            def max_tile(i, s, t, c, lead=None):
                if t == 0 and c == 0:
                    pe.wait_ge(slot_in[s], 96 * (i + 1))
                if lead is None:
                    pe.wait_ge(max_done, 14 * (4 * i + s) + 2 * t + c - 1)
                    n = c
                else:
                    n = LEAD_BANKS[lead % 3]
                    if lead >= 3:
                        pe.wait_ge(max_done, lead - 2)
                mm(P[0:T, n, 0:HALF], Qs[0:96, s, t * T:(t + 1) * T], Ks[0:96, s, c * HALF:(c + 1) * HALF]).then_inc(max_full, 1)

            def max_turn(i, s):
                pe.wait_ge(mhl_ready, 4 * i + s + 1)
                nc.tensor.transpose(P[0:2 * NT, 7, 0:T], mhl[:, :].bitcast(F32), Bt("ident", T)[:, 0:T]).then_inc(turn_full, 1)

            def score_tile(i, s, u, p, first):
                k = 7 * (4 * i + s) + u
                if u == 0:
                    pe.wait_ge(mrow_in[s], 16 * (i + 1))
                if not first:
                    pe.wait_ge(exp_done, k - 1)
                for c in range(2):
                    last = mm(P[0:T, 2 + 2 * p + c, 0:HALF], Ks[:, s, u * T:(u + 1) * T], Qs[:, s, c * HALF:(c + 1) * HALF])
                last.then_inc(st_full, 1)

            def context_tile(i, s, u, p, first):
                n = 4 * i + s
                if u == 0:
                    pe.wait_ge(value_in[s], 32 * (i + 1))
                    if not first:
                        pe.wait_ge(ctx_done, n)
                pe.wait_ge(exp_done, 7 * n + u + 1)
                for h in range(2):
                    last = mm(P[h * D:(h + 1) * D, 6, 0:HALF], XVs[:, s, u * D:(u + 1) * D], PT[:, p, h * HALF:(h + 1) * HALF],
                              u == 0, u == NT - 1, skip_group_check=True)
                last.then_inc(av_done, 1)

            def head_out(i, s, first, bank1_used):
                n = 4 * i + s
                pe.wait_ge(ctx_done, n + 1)
                if not first:
                    pe.wait_ge(proj_done, n)
                if not (isinstance(n, int) and n > NH - 3):
                    pe.wait_ge(turn_done, n + 3)
                W = D + 1
                for k in range(NGT):
                    tokens = CT[:, k * GT:(k + 1) * GT]
                    if k < NGT - 1:
                        mm(P[0:GT, 7, 2 * k * W:2 * (k + 1) * W], tokens, VBs[:, s, :])
                mm(P[0:GT, 7, 6 * W:7 * W], tokens, VBs[:, s, 0:W])
                pe.wait_ge(max_done, bank1_used)
                mm(P[0:GT, 1, HALF:HALF + W], tokens, VBs[:, s, W:2 * W]).then_inc(proj_full, 1)

            def four_heads(i, first=False, final=False):
                for s in range(4):
                    for u in range(NT):
                        step = 7 * s + u
                        ahead = step + LEAD
                        more = not (final and ahead >= 28)
                        tile = (i + ahead // 28, ahead // 7 % 4, ahead % 7)
                        score_tile(i, s, u, step % 2, first and step < 2)
                        if more:
                            max_tile(*tile, 0)
                        if u == TURN and not (final and s == 3):
                            if not (first and s < 2):
                                pe.wait_ge(proj_done, 4 * i + s - 1)
                            max_turn(i + (s == 3), (s + 1) % 4)
                        if not (first and step == 0):
                            before = step - 1
                            context_tile(i if before >= 0 else i - 1, before // 7 % 4, before % 7, before % 2,
                                         first and before < 7)
                        if u == 2 and not (first and s == 0):
                            used = 14 * (4 * tile[0] + tile[1]) + 2 * tile[2] if more else 14 * NH
                            head_out(i if s else i - 1, (s - 1) % 4, first and s == 1, used)
                        if more:
                            if u == 3 and not (first and s == 0):
                                pe.wait_ge(block_done, 4 * i + s)
                            max_tile(*tile, 1)

            for j in range(LEAD):
                if j == 8:
                    max_turn(0, 0)
                for c in range(2):
                    max_tile(0, j // 7, j % 7, c, 2 * j + c)
            four_heads(0, first=True)
            repeat(pe, 1, 7, {}, four_heads)
            four_heads(7, final=True)
            context_tile(7, 3, 6, 1, False)
            head_out(7, 3, False, 14 * NH)

            for b in range(B):
                pe.wait_ge(summed, b + 1)
                for k in range(NGT):
                    for h in range(2):
                        last = mm(P[h * D:(h + 1) * D, 2 + b, k * GT:(k + 1) * GT], OUT[:, 2 * b, (2 * k + h) * D:(2 * k + h + 1) * D],
                                  Bt("ident", GT)[:, 0:GT])
                last.then_inc(join_full, 1)

            norm(MOE1, h_ready, lambda b: 2 * B + b + 1)
            logits(Bt("router"), gate1, MOE1)

            def turn_out(b, part):
                if part == 0:
                    pe.wait_ge(h_ready, 3 * B + b + 1)
                n = bank_of(("out", b, part), HID1)
                c0, c1 = OUT_PARTS[part]
                for c in range(c0, c1):
                    w = OJ * NP
                    last = nc.tensor.transpose(P[0:w, n, (c - c0) * 128:(c - c0 + 1) * 128], Y[:, b, c * w:(c + 1) * w], Bt("ident"))
                last.then_inc(hid_full, 1)

            def hidden_layer(b):
                pe.wait_ge(split1, 2 * b + 2)
                for p in range(PAIRS):
                    for h in range(2):
                        n = bank_of(("g1", b, p, h), HID1)
                        for part in range(2):
                            last = mm(bank(n), mw1r[:, part, p, :], xs1[:, b, h * HALF:(h + 1) * HALF], part == 0, part == 1)
                        last.then_inc(hid_full, 1)

            AHEAD = 2

            def gate_of(m):
                if m < B * E1:
                    if m % E1 == 0:
                        pe.wait_ge(hid_done, HID["wT1", m // E1] + 1)
                    broadcast_gate(sel1r[:, m // 2 % PAIRS, m % 2, :], wT1[:, m // E1, :], B * E0 + m)

            mw2 = Bt("mw2").rearrange("p (e n) -> p e n", e=PAIRS)
            pe.wait_ge(w1_split, 1)
            for b in range(3):
                hidden_layer(b)
            pe.wait_ge(gates_ready, 2)
            pe.wait_ge(sel1_ready, 1)
            for b in range(B):
                gate_rows(("wT1", b), gate1.wsp, b, HID1)
            for m in range(AHEAD):
                gate_of(m)
            for b in range(B):
                sums = MOE1_BANKS[b % 2]
                if b >= 2:
                    pe.wait_ge(h_ready, 3 * B + b - 1)
                for part in range(2):
                    mm(bank(sums), mb2r[:, part, :], wT1[:, b, :], part == 0, False, skip_group_check=True)
                for e in range(2 * PAIRS):
                    gate_of(E1 * b + e + AHEAD)
                    if b >= 1 and e in (5, 7):
                        turn_out(b - 1, int(e == 7))
                    pe.wait_ge(wbc_done, B * E0 + E1 * b + e + 1)
                    h = e % 2
                    last = mm(P[h * D:(h + 1) * D, sums, 0:HALF], mw2[:, e // 2, :], g1[:, b, e // 2, h, :], False,
                              e // 2 == PAIRS - 1, skip_group_check=True)
                last.then_inc(moe_full, 1)
                if b == 0:
                    hidden_layer(3)
            for part in range(2):
                turn_out(B - 1, part)

        @block.vector
        def _(vector):
            steps = Tally()

            def own():
                vector.wait_ge(vec_step, steps.now())

            nc.vector.memset(eps[:, :], EPS).then_inc(eps_set, 1)
            nc.vector.memset(VB[:, :, :], 0.0).then_inc(vec_step, steps.one())
            nc.vector.memset(XV[:, :, :, :], 1.0)

            def pixels(g, q):
                return X.rearrange("p c r w -> p (c r) w")[:, :, bass.ds((q // 2 * HCOL + 2 * g + q % 2) * PS, PS)]

            def stats(g, p):
                for q in range(4):
                    nc.vector.bn_stats(bst[:, p, q, :], pixels(g, q)).then_inc(vec_step, steps.one())

            def moments(g, p):
                for q in range(4):
                    last = nc.vector.bn_aggr(mv[:, p, q, :], bst[:, p, q, :])
                last.then_inc(stats_ready, 1)

            def apply(g, p):
                vector.wait_ge(sd_ready, g + 1)
                nc.vector.reciprocal(ri[:, p, :], sd[:, p, :]).then_inc(vec_step, steps.one())
                own()
                for q in range(4):
                    last = nc.vector.tensor_scalar(xn[:, p, q, :].rearrange("p (r w) -> p r w", w=PS), pixels(g, q),
                                                   mv[:, p, q, 0:1], ri[:, p, q:q + 1], ALU.subtract, ALU.mult)
                last.then_inc(xn_ready, 1)

            vector.wait_ge(w1_full, 1)
            nc.vector.tensor_copy(w1c[:, :, :], P[0:KF, 7, 0:2 * D].rearrange("p (k d) -> p k d", k=2))
            nc.vector.tensor_copy(b1c[:, :], P[:, 7, FEAT:FEAT + 1]).then_inc(w1_ready, 1)
            vector.wait_ge(pixels_in, 16 * B)
            stats(0, 0)
            own()
            moments(0, 0)
            stats(1, 1)
            apply(0, 0)
            moments(1, 1)

            def cycle(g, p):
                stats(g + 1, 1 - p)
                apply(g, p)
                moments(g + 1, 1 - p)

            def two(i):
                cycle(2 * i + 1, 1)
                cycle(2 * i + 2, 0)
            repeat(vector, 0, 2, {steps: 10}, two)
            cycle(5, 1)
            apply(6, 0)

            def split_weights(hi, lo, w):
                nc.vector.tensor_copy(hi, w).then_inc(vec_step, steps.one())
                own()
                return nc.vector.tensor_tensor(lo, w, hi.bitcast(F32), ALU.subtract)

            def norm(S, between=None):
                for b in range(2, B):
                    wait_centred(vector, S, b)
                    rows = state[:, b, :] if S == TOK2 else xhat[:, b, :]
                    if S != TOK2:
                        if bias_of(S) is not None:
                            nc.vector.tensor_scalar(rows, rows_bank(S, b), bias_of(S), None, ALU.add).then_inc(vec_step, steps.one())
                        else:
                            nc.vector.tensor_copy(rows, rows_bank(S, b)).then_inc(vec_step, steps.one())
                        own()
                    nc.vector.tensor_tensor(square_buf(S)[:, b, :], rows, rows, ALU.mult).then_inc(squared_vec, 1)
                if between is not None:
                    between()

                for b in range(B):
                    vector.wait_ge(rstd_ready, 4 * S + b + 1)
                    rstd = rstd_buf(S)[:, b, :]
                    if bias_of(S) is not None:
                        ins = nc.vector.scalar_tensor_tensor(xhat[:, b, :], rows_bank(S, b), bias_of(S), rstd, ALU.add, ALU.mult)
                    else:
                        ins = nc.vector.tensor_tensor(xhat[:, b, :], state[:, b, :] if S == TOK2 else rows_bank(S, b), rstd,
                                                      ALU.mult)
                    if S == TOK2:
                        ins.then_inc(vec_step, steps.one())
                        own()
                        ins = nc.vector.tensor_scalar(xhat[:, b, :], xhat[:, b, :], col("ln2_g"), col("ln2_b"), ALU.mult, ALU.add)
                    ins.then_inc(normed, 1)

            def first_operands():
                vector.wait_ge(wb_in, 32)
                vector.wait_ge(vo_full, 1)
                for h in range(2):
                    part_ = slice(h * D, (h + 1) * D)
                    at = h * (D + 1)
                    nc.vector.tensor_copy(VB[part_, :, at:at + D], P[part_, 0, 0:HEADS * D].rearrange("p (e d) -> p e d", d=D))
                    last = nc.vector.tensor_copy(VB[part_, :, at + D], wa[part_, COLS_A["e63"][0]:COLS_A["e63"][1]].broadcast_to([D, HEADS]))
                last.then_inc(vb_ready, 1)
                vector.wait_ge(wp1_full, 1)
                nc.vector.tensor_copy(wp1c[:, :], P[:, 1, 0:128])
                nc.vector.tensor_copy(wp2c[:, :], P[:, 2, 0:128])
                nc.vector.tensor_copy(biasc[:, :], P[:, 1, 128:131]).then_inc(wp1_ready, 1)
                nc.vector.tensor_scalar(ycol[:, :], col("gn_w"), 0.0, col("gn_b"), ALU.mult, ALU.add).then_inc(vec_step, steps.one())
                own()
                nc.vector.tensor_scalar(woy[:, :], A("wo"), ycol[:, :], None, ALU.mult)
                nc.vector.tensor_scalar(woyc[:, :], P[:, 2, 128:256], ycol[:, :], None, ALU.mult).then_inc(woy_ready, 1)
                nc.vector.tensor_copy(sel0r[:, :, :, :], A("sel0", 96).rearrange("p (e h n) -> p e h n", e=E0 // 2, h=2))\
                  .then_inc(sel0_ready, 1)
                nc.vector.memset(gate0.wsp[:, :, :].bitcast(F32), 0.0).then_inc(vec_step, steps.one())

                split_weights(eb3r[:, 0, :], eb3r[:, 1, :], A("eb3", 96))
                split_weights(ew1r[:, 0, :, :], ew1r[:, 1, :, :], A("ew1").rearrange("p (e n) -> p e n", e=E0)).then_inc(w0_split, 1)

            norm(TOK2, first_operands)
            norm(POOL3)

            def tokenizer_out():
                for b in range(B):
                    vector.wait_ge(main_full, B + b + 1)
                    nc.vector.tensor_scalar(H[:, b, :], bank(4 + b), col("bp2"), None, ALU.add).then_inc(h0_ready, 1)

            norm(GATE, tokenizer_out)
            norm(MOE0)

            def tt(o, a, b_, op):
                nc.vector.tensor_tensor(o, a, b_, op).then_inc(vec_step, steps.one())
                own()

            def reduce(o, a, op):
                nc.vector.tensor_reduce(o, a, AX.X, op).then_inc(vec_step, steps.one())
                own()

            def low_part(xs, split, b):
                for h in range(2):
                    vector.wait_ge(high_done, (8 if xs is xs1 else 0) + 2 * b + h + 1)
                    cols = slice(h * HALF, (h + 1) * HALF)
                    nc.vector.tensor_tensor(xs[D:128, b, cols], xhat[h * D:(h + 1) * D, b, :], xs[0:D, b, cols].bitcast(F32),
                                            ALU.subtract).then_inc(split, 1)

            def copy_logits(gate, n):
                vector.wait_ge(logits_full, n)
                nc.vector.tensor_copy(gate.lt[:, :], bank(4)).then_inc(logits_out, 1)

            def gating(gate, E, bias, idx, pair_softmax, asked, meanwhile):
                N = B * NGT * 2
                wide = [GT, N, E]

                def over(r):
                    return r.unsqueeze(2).broadcast_to(wide)
                vector.wait_ge(logits_turned, asked["logits"])
                lg = P[0:GT, 4, 0:N // 2 * R].rearrange("p (n x) -> p n x", x=R)[:, :, 0:2 * E]
                if bias is None:
                    nc.vector.tensor_copy(gate.a.rearrange("p (n h) e -> p n (h e)", h=2), lg).then_inc(vec_step, steps.one())
                    own()
                else:
                    tt(gate.a.rearrange("p (n h) e -> p n (h e)", h=2), lg, bias.unsqueeze(1).broadcast_to([GT, N // 2, 2 * E]), ALU.add)
                reduce(gate.m[:, :], gate.a[:, :, :], ALU.max)
                nc.vector.tensor_tensor(gate.dif, gate.a[:, :, :], over(gate.m[:, :]), ALU.subtract).then_inc(expo_in, 1)
                meanwhile(0)
                vector.wait_ge(expo_out, asked["exp"])
                reduce(gate.m[:, :], gate.ex, ALU.add)
                nc.vector.reciprocal(gate.m[:, :], gate.m[:, :]).then_inc(vec_step, steps.one())
                own()
                tt(gate.p[:, :, :], gate.ex, over(gate.m[:, :]), ALU.mult)
                best = [gate.v1[:, :], gate.v2[:, :]]
                chosen = [gate.s1[:, :, :], gate.s2[:, :, :]]
                probs = gate.p[:, :, :]
                for r, s in zip(best, chosen):
                    reduce(r, probs, ALU.max)
                    tt(s, probs, over(r), ALU.is_equal)
                    tt(s, s, idx.unsqueeze(1).broadcast_to(wide), ALU.mult)
                    reduce(gate.m[:, :], s, ALU.max)
                    tt(s, s, over(gate.m[:, :]), ALU.is_equal)
                    if r is best[0]:
                        nc.vector.scalar_tensor_tensor(gate.a[:, :, :], s, -2.0, probs, ALU.mult, ALU.add)\
                          .then_inc(vec_step, steps.one())
                        own()
                        probs = gate.a[:, :, :]
                if pair_softmax:
                    nc.vector.tensor_tensor(gate.d21, gate.v2[:, :], gate.v1[:, :], ALU.subtract).then_inc(expo_in, 1)
                    meanwhile(1)
                    vector.wait_ge(expo_out, asked["exp"] + 1)
                    nc.vector.tensor_scalar(gate.m[:, :], gate.e21, 1.0, None, ALU.add).then_inc(vec_step, steps.one())
                    own()
                    nc.vector.reciprocal(gate.v1[:, :], gate.m[:, :]).then_inc(vec_step, steps.one())
                    own()
                    tt(gate.v2[:, :], gate.e21, gate.v1[:, :], ALU.mult)
                else:
                    tt(gate.m[:, :], gate.v1[:, :], gate.v2[:, :], ALU.add)
                    nc.vector.tensor_scalar(gate.m[:, :], gate.m[:, :], 1e-12, None, ALU.max).then_inc(vec_step, steps.one())
                    own()
                    nc.vector.reciprocal(gate.m[:, :], gate.m[:, :]).then_inc(vec_step, steps.one())
                    own()
                    tt(gate.v1[:, :], gate.v1[:, :], gate.m[:, :], ALU.mult)
                    tt(gate.v2[:, :], gate.v2[:, :], gate.m[:, :], ALU.mult)
                tt(gate.s1[:, :, :], gate.s1[:, :, :], over(gate.v1[:, :]), ALU.mult)
                tt(gate.s2[:, :, :], gate.s2[:, :, :], over(gate.v2[:, :]), ALU.mult)
                tt(gate.p[:, :, :], gate.s1[:, :, :], gate.s2[:, :, :], ALU.add)
                w = gate.p.rearrange("p (n h) e -> p n (h e)", h=2)
                if gate is gate1:
                    vector.wait_ge(rows_cleared, 1)
                hi, lo = gate.wsp[:, :, 0:2 * E], gate.wsp[:, :, 32:32 + 2 * E]
                nc.vector.tensor_copy(hi, w).then_inc(vec_step, steps.one())
                own()
                nc.vector.tensor_tensor(lo, w, hi.bitcast(F32), ALU.subtract).then_inc(gates_ready, 1)

            low_part(xs0, split0, 0)
            copy_logits(gate0, 1)
            for b in range(B):
                vector.wait_ge(main_full, 3 * B + b + 1)
                nc.vector.scalar_tensor_tensor(H[:, b, :], bank(b), col("abias"), H[:, b, :], ALU.add, ALU.add)\
                  .then_inc(h_ready, 1)
            gating(gate0, E0, A("gb", GT), A("idx0", GT), True, {"logits": 1, "exp": 1},
                   lambda n: low_part(xs0, split0, n + 1))
            low_part(xs0, split0, 3)

            def times_gate(n, buf):
                vector.wait_ge(wbc_full, n + 1)
                first, banks = wbc_banks(n)
                nc.vector.tensor_tensor(buf, bank(banks[(n - first) % len(banks)]), buf, ALU.mult).then_inc(wbc_done, 1)

            for b in range(B):
                for e in range(E0):
                    times_gate(E0 * b + e, h2[:, e // 2, e % 2, :])
                vector.wait_ge(moe_full, b + 1)
                nc.vector.scalar_tensor_tensor(H[:, b, :], bank(7), col("sb3"), H[:, b, :], ALU.add, ALU.add)\
                  .then_inc(h_ready, 1)

            norm(ATT)
            for n in range(8 * B):
                b, k = n // 8, n % 8
                cols = (slice(None), k // 4, 2 * b + k // 2 % 2, slice(k % 2 * HALF, (k % 2 + 1) * HALF))
                vector.wait_ge(qk_hi, n + 1)
                nc.vector.tensor_tensor(QKL[cols], bank(4 + k % 4), QKH[cols].bitcast(F32), ALU.subtract).then_inc(qk_lo, 1)

            vector.wait_ge(xv_done, B)
            nc.vector.memset(Ks[96:98, :, :].bitcast(F32), 1.0).then_inc(slots_set, 1)

            def row_max(i, s, t, c, n=None):
                vector.wait_ge(max_full, 14 * (4 * i + s) + 2 * t + c + 1)
                nc.vector.tensor_reduce(mx[:, s % 2, c, t:t + 1], bank(c if n is None else n)[0:T, :], AX.X, ALU.max)\
                  .then_inc(max_done, 1)

            def minus_max(i, s, part_):
                if part_ == 0:
                    vector.wait_ge(max_done, 14 * (4 * i + s) + 14)
                    nc.vector.tensor_tensor(mxf[:, :], mx[:, s % 2, 0, :], mx[:, s % 2, 1, :], ALU.max).then_inc(vec_step, steps.one())
                elif part_ == 1:
                    own()
                    nc.vector.tensor_scalar(mhl[:, 0:NT], mxf[:, :], -1.0, None, ALU.mult).then_inc(vec_step, steps.one())
                else:
                    own()
                    nc.vector.scalar_tensor_tensor(mhl[:, NT:2 * NT], mxf[:, :], -1.0, mhl[:, 0:NT].bitcast(F32),
                                                   ALU.mult, ALU.subtract).then_inc(mhl_ready, 1)

            def max_rows(i, s):
                vector.wait_ge(turn_full, 4 * i + s + 1)
                nc.vector.tensor_copy(mT[:, :], P[0:2 * NT, 7, 0:T]).then_inc(turn_done, 1)

            def divide_block(i, s, tile, first=False):
                if tile is None:
                    vector.wait_ge(proj_full, 4 * i + s + 1)
                else:
                    vector.wait_ge(max_full, 14 * (4 * tile[0] + tile[1]) + 2 * tile[2] + 2)
                nc.vector.reciprocal(zi[:, NQ - 1:NQ], P[0:GT, 1, HALF + D:HALF + D + 1]).then_inc(vec_step, steps.one())
                own()
                if s == 3:
                    vector.wait_ge(sums, 3 * i + 1)
                elif s == 0 and not first:
                    vector.wait_ge(sums, 3 * i)
                nc.vector.tensor_scalar(part[:, s % 3, (NQ - 1) * D:NQ * D], P[0:GT, 1, HALF:HALF + D], zi[:, NQ - 1:NQ], None,
                                        ALU.mult).then_inc(block_done, 1)

            def divide(i, s):
                got = P[0:GT, 7, 0:(NQ - 1) * (D + 1)].rearrange("p (t d) -> p t d", d=D + 1)
                nc.vector.reciprocal(zi[:, 0:NQ - 1], got[:, :, D]).then_inc(vec_step, steps.one())
                own()
                nc.vector.tensor_tensor(part[:, s % 3, 0:(NQ - 1) * D].rearrange("p (t d) -> p t d", d=D), got[:, :, 0:D],
                                        zi[:, 0:NQ - 1].unsqueeze(2).broadcast_to([GT, NQ - 1, D]), ALU.mult).then_inc(proj_done, 1)

            def image_sum(b):
                vector.wait_ge(grouped, 2 * b + 2)
                nc.vector.tensor_tensor(OUT[:, 2 * b, :], OUT[:, 2 * b, :], OUT[:, 2 * b + 1, :], ALU.add).then_inc(summed, 1)

            def four_heads(i, first=False, final=False):
                for s in range(4):
                    for u in range(NT):
                        ahead = 7 * s + u + LEAD
                        more = not (final and ahead >= 28)
                        tile = (i + ahead // 28, ahead // 7 % 4, ahead % 7)
                        if more:
                            row_max(*tile, 0)
                        before = (i + (ahead - 7) // 28, (ahead - 7) // 7 % 4)
                        if ahead % 7 == 0 and not (final and ahead >= 29):
                            minus_max(*before, 1)
                        if u == TURN and not (final and s == 3):
                            max_rows(i + (s == 3), (s + 1) % 4)
                        if u == 5 and s < B - 1 and final:
                            image_sum(s)
                        done = (i if s else i - 1, (s - 1) % 4)
                        if u == 2 and not (first and s == 0):
                            divide_block(*done, tile if more else None, first)
                        if u == 3 and not (first and s == 0):
                            divide(*done)
                        if more:
                            row_max(*tile, 1)
                        if ahead % 7 == 6 and not (final and ahead >= 28):
                            minus_max(tile[0], tile[1], 0)
                        if ahead % 7 == 0 and not (final and ahead >= 29):
                            minus_max(*before, 2)

            for j in range(LEAD):
                if j in (7, 14):
                    for part_ in range(3):
                        minus_max(0, j // 7 - 1, part_)
                if j == 8:
                    max_rows(0, 0)
                for c in range(2):
                    row_max(0, j // 7, j % 7, c, LEAD_BANKS[(2 * j + c) % 3])
            four_heads(0, first=True)
            repeat(vector, 1, 7, {steps: 4 * 4}, four_heads)
            four_heads(7, final=True)
            vector.wait_ge(grouped, 2 * B - 1)
            vector.wait_ge(sums, 3 * (2 * B - 1) + 2)
            nc.vector.tensor_tensor(OUT[:, 2 * B - 1, :], OUT[:, 2 * B - 2, :], acc[:, 1, :], ALU.add).then_inc(vec_step, steps.one())
            divide_block(7, 3, None)
            divide(7, 3)
            vector.wait_ge(proj_done, NH)
            nc.vector.tensor_tensor(OUT[:, 2 * B - 2, :], OUT[:, 2 * B - 1, :], part[:, 0, :], ALU.add).then_inc(summed, 1)

            for b in range(B):
                vector.wait_ge(join_full, b + 1)
                nc.vector.tensor_tensor(H[:, b, :], bank(2 + b), H[:, b, :], ALU.add).then_inc(h_ready, 1)

            def operands():
                nc.vector.tensor_copy(sel1r[:, :, :, :], Bt("sel1", 96).rearrange("p (e h n) -> p e h n", e=PAIRS, h=2))\
                  .then_inc(sel1_ready, 1)
                split_weights(mb2r[:, 0, :], mb2r[:, 1, :], Bt("mb2", 96))
                split_weights(mw1r[:, 0, :, :], mw1r[:, 1, :, :], Bt("mw1").rearrange("p (e n) -> p e n", e=PAIRS))\
                  .then_inc(w1_split, 1)

            norm(MOE1, operands)
            low_part(xs1, split1, 0)
            copy_logits(gate1, 2)
            low_part(xs1, split1, 1)
            gating(gate1, E1, None, Bt("idx1", GT), False, {"logits": 2, "exp": 3}, lambda n: low_part(xs1, split1, 2))
            low_part(xs1, split1, 3)

            def block_sum(b):
                vector.wait_ge(moe_full, B + b + 1)
                tt(xhat[:, b, :], bank(MOE1_BANKS[b % 2]), xhat[:, b, :], ALU.add)

                def view(tile, order):
                    return tile[:, b, :].rearrange(order, c=OC, j=OJ)
                nc.vector.tensor_tensor(view(Y, "p (c j i) -> p c j i"), view(xhat, "p (j c i) -> p c j i"),
                                        view(H, "p (j c i) -> p c j i"), ALU.add).then_inc(h_ready, 1)

            for b in range(B):
                if b == 3:
                    vector.wait_ge(hid_done, HID["g1", 3, PAIRS - 1, 1] + 1)
                for e in range(E1):
                    times_gate(B * E0 + E1 * b + e, g1[:, b, e // 2, e % 2, :])
                    if b >= 1 and e == 1:
                        block_sum(b - 1)
            block_sum(B - 1)


class Gate:

    def __init__(self, tile, E):
        N = B * NGT * 2
        wide = {n: tile(f"gate{E}_{n}", [GT, N, E]) for n in ("a", "dif", "ex", "p", "s1", "s2")}
        flat = {n: tile(f"gate{E}_{n}", [GT, N]) for n in ("m", "v1", "v2", "d21", "e21")}
        self.a, self.p, self.s1, self.s2 = wide["a"], wide["p"], wide["s1"], wide["s2"]
        self.dif, self.ex = wide["dif"][:, :, :], wide["ex"][:, :, :]
        self.m, self.v1, self.v2 = flat["m"], flat["v1"], flat["v2"]
        self.d21, self.e21 = flat["d21"][:, :], flat["e21"][:, :]
        self.lt = tile(f"gate{E}_lt", [128, HALF])
        self.wsp = tile(f"gate{E}_wsp", [GT, B * NGT, 96], F32R)


def kernel(**inputs):
    import concourse.bacc as bacc
    from concourse.bass_utils import run_bass_kernel_spmd as run

    a = {k: np.asarray(v) for k, v in inputs.items()}
    tok = {k[7:]: v for k, v in a.items() if k.startswith("L0_tok_")}
    gate = {k[8:]: v for k, v in a.items() if k.startswith("L0_attn_")}
    moe0 = {k[7:]: v for k, v in a.items() if k.startswith("L0_ffn_")}
    moe1 = {k[7:]: v for k, v in a.items() if k.startswith("L1_ffn_")}

    def table(cols, width, blocks):
        t = np.zeros((128, width), np.float32)
        for name, value in blocks.items():
            lo, hi = cols[name]
            t[0:value.shape[0], lo:hi] = value.reshape(value.shape[0], hi - lo)
        return t

    def diag(w):
        m = np.zeros((128, 2 * w.shape[1]), np.float32)
        m[0:D, 0:w.shape[1]] = w
        m[D:128, w.shape[1]:] = w
        return m

    def side(w):
        m = np.zeros((128, 2, w.shape[1]), np.float32)
        m[0:D, 0] = w
        m[D:128, 1] = w
        return m

    def padded(w):
        return np.concatenate([w, np.zeros((128, R - w.shape[1]), np.float32)], 1)

    def stacked(w):
        return np.concatenate([w, w])

    def pair_selectors(E):
        m = np.zeros((96, E // 2, 2, 128), np.float32)
        for p in range(E // 2):
            for h in range(2):
                for e in range(2):
                    for r in (0, 32):
                        m[r + h * E + 2 * p + e, p, h, e * D:(e + 1) * D] = 1
        return m

    def twice(v):
        return np.concatenate([v, v]).reshape(128, 1)

    def features(v):
        v = v.reshape(PS * PS, C, -1).transpose(1, 0, 2).reshape(2, KF, -1)
        return v.transpose(1, 0, 2)

    def gate_biases(v):
        E = v.shape[0]
        m = np.zeros((96, 128), np.float32)
        for h in range(2):
            for r in (0, 32):
                m[r + h * E:r + (h + 1) * E, h * D:(h + 1) * D] = v
        return m

    fold = np.eye(D, dtype=np.float32)
    fold[D - 1, :] = -1
    fold[:, D - 1] = 0
    e63 = np.zeros((128, 1), np.float32)
    e63[[D - 1, 127]] = 1
    eye = np.eye(128, dtype=np.float32)
    ones = np.full((D, D), 1.0 / D, np.float32)
    qk = np.stack([np.stack([side(w[4 * g:4 * g + 4].reshape(4 * R, D).T) for g in range(2)], 1)
                   for w in (a["L1_attn_Q"], a["L1_attn_K"])], 1)
    common = {"ident": eye, "center": diag(np.eye(D, dtype=np.float32) - ones), "mean": diag(ones)}
    table_a = table(COLS_A, WIDTH_A, {"ident": eye,
        "w1_t": features(tok["W1"]).transpose(2, 1, 0), "c64": common["center"][0:D, 0:D], "wp1_t": diag(tok["Wp1"].T), "wp2_t": diag(tok["Wp2"].T), "wo_t": diag(gate["wo"].T), "wp2": diag(tok["Wp2"]),
        "wg": diag(gate["wg"]), "wo": diag(gate["wo"]), "sw1": diag(moe0["sW1"]),
        "ew1": stacked(moe0["eW1"].transpose(1, 0, 2)),
        "ew2": moe0["eW2"].transpose(1, 0, 2), "ew3": moe0["eW3"].reshape(E0 // 2, 128, D).transpose(1, 0, 2),
        "sw2": side(moe0["sW2"]), "sw3": moe0["sW3"], "gw": padded(diag(moe0["gW"])), "eb3": gate_biases(moe0["eb3"]),
        "sel0": pair_selectors(E0), "gb": np.tile(moe0["gb"], (128, 2)),
        "idx0": np.tile(np.arange(E0, 0, -1, dtype=np.float32), (128, 1)),
        "qk": qk, "vo": a["L1_attn_VO"].transpose(1, 0, 2), "fold": fold, "e63": e63,
        "ln1_g": features(tok["ln1_g"]), "ln1_b": features(tok["ln1_b"]), "b1": twice(tok["b1"]),
        "ln2_g": twice(tok["ln2_g"]), "ln2_b": twice(tok["ln2_b"]), "bp1": twice(tok["bp1"]),
        "lnp_g": twice(tok["lnp_g"]), "lnp_b": twice(tok["lnp_b"]), "bp2": twice(tok["bp2"]),
        "gn_w": twice(gate["gn_weight"]), "gn_b": twice(gate["gn_bias"]), "abias": twice(gate["bias"]),
        "sb1": twice(moe0["sb1"]), "eb1": moe0["eb1"].T, "sb2": moe0["sb2"].reshape(128, 1),
        "eb2": moe0["eb2"].reshape(E0 // 2, 128).T, "sb3": twice(moe0["sb3"])})
    table_b = table(COLS_B, WIDTH_B, common | {
        "router": padded(diag(moe1["router_w"].T)), "mw1": stacked(moe1["w1"].transpose(1, 0, 2)),
        "mw2": moe1["w2"].reshape(PAIRS, 128, D).transpose(1, 0, 2), "mb2": gate_biases(moe1["b2"]),
        "sel1": pair_selectors(E1), "idx1": np.tile(np.arange(E1, 0, -1, dtype=np.float32), (128, 1)),
        "mb1": moe1["b1"].reshape(PAIRS, 128).T})

    nc = bacc.Bacc("TRN2", target_bir_lowering=False, num_devices=1)
    arrays = {"x": np.ascontiguousarray(a["x"]), "table_a": table_a, "table_b": table_b}
    aps = [nc.dram_tensor(n, v.shape, F32, kind="ExternalInput").ap() for n, v in arrays.items()]
    result = nc.dram_tensor("out", (B, REP * TOK, D), F32, kind="ExternalOutput").ap()
    build(nc, *aps, result)
    r = run(nc, [arrays], core_ids=[0])
    return r.results[0]["out"]
```
